# Optimizing a Trainium2 kernel written in Bass

```python
import numpy as np
import jax
import jax.numpy as jnp

def _softmax(x, axis=-1):
    return jax.nn.softmax(x, axis=axis)

def _gelu(x):
    return jax.nn.gelu(x, approximate=True)

def _silu(x):
    return jax.nn.silu(x)

def _sigmoid(x):
    return jax.nn.sigmoid(x)

def _layernorm(x, axis=-1, eps=1e-05):
    m = jnp.mean(x, axis=axis, keepdims=True)
    v = jnp.var(x, axis=axis, keepdims=True)
    return (x - m) / jnp.sqrt(v + eps)

def _scatter_add(tgt, idx, src, axis=0):
    return tgt.at[idx].add(src)

def _segment_sum(src, seg, n):
    return jax.ops.segment_sum(src, seg, n)
kernel_name = 'mk_seq_postln_d2_jaxref_r8_d67195'

def setup_inputs(seed: int=0):
    np.random.seed(seed)
    _w = jnp.asarray

    def _L0_attn_setup():
        import jax, jax.numpy as jnp
        import numpy as np
        D = 128
        B = 4
        S = 512
        LN_EPS = 1e-05

        def _layer_norm(x, gamma, beta):
            mu = jnp.mean(x, axis=-1, keepdims=True)
            var = jnp.mean(jnp.square(x - mu), axis=-1, keepdims=True)
            return (x - mu) * jax.lax.rsqrt(var + LN_EPS) * gamma + beta
        key = jax.random.key(seed)
        ks = jax.random.split(key, 5)
        scale = 1.0 / np.sqrt(D)
        return {'hidden_states': jax.random.normal(ks[0], (B, S, D), dtype=jnp.float32), 'attention_mask': jnp.ones((B, S), dtype=jnp.int32), 'Wk': jax.random.normal(ks[1], (D, D), dtype=jnp.float32) * scale, 'bk': jnp.zeros((D,), dtype=jnp.float32), 'Wka': jax.random.normal(ks[2], (D, D), dtype=jnp.float32) * scale, 'bka': jnp.zeros((D,), dtype=jnp.float32), 'Wv': jax.random.normal(ks[3], (D, D), dtype=jnp.float32) * scale, 'bv': jnp.zeros((D,), dtype=jnp.float32), 'gamma': jnp.ones((D,), dtype=jnp.float32), 'beta': jnp.zeros((D,), dtype=jnp.float32)}
    _L0_attn_in = _L0_attn_setup()

    def _L0_ffn_setup():
        import jax, jax.numpy as jnp
        import numpy as np
        MAX_VAL = 100.0
        key = jax.random.key(seed)
        k1, k2, k3 = jax.random.split(key, 3)
        B, S, D_IN, D_OUT = (4, 1024, 128, 128)
        x = jax.random.normal(k1, (B, S, D_IN), dtype=jnp.float32)
        weights = jax.random.normal(k2, (D_OUT, D_IN), dtype=jnp.float32)
        scale = jnp.ones((D_OUT,), dtype=jnp.float32)
        bias = jax.random.normal(k3, (D_OUT,), dtype=jnp.float32)
        return {'x': x, 'weights': weights, 'scale': scale, 'bias': bias}
    _L0_ffn_in = _L0_ffn_setup()

    def _L1_attn_setup():
        import jax, jax.numpy as jnp
        import numpy as np
        L, H, D_MODEL, D_FF = (4, 16, 128, 512)
        HD = D_MODEL // H
        LN_EPS = 1e-05
        ATT_EPS = 1e-06
        CHUNK = 128

        def _ln(x, g, b):
            m = jnp.mean(x, axis=-1, keepdims=True)
            v = jnp.var(x, axis=-1, keepdims=True)
            return (x - m) * jax.lax.rsqrt(v + LN_EPS) * g + b

        def _feature_map(x):
            return jax.nn.elu(x) + 1.0

        def _causal_linear_attention(q, k, v):
            B, S, Hn, D = q.shape
            nC = S // CHUNK
            q = q.reshape(B, nC, CHUNK, Hn, D)
            k = k.reshape(B, nC, CHUNK, Hn, D)
            v = v.reshape(B, nC, CHUNK, Hn, D)
            KV = jnp.einsum('bnchd,bnche->bnhde', k, v)
            Ks = jnp.sum(k, axis=2)
            KVcum = jnp.cumsum(KV, axis=1) - KV
            Kcum = jnp.cumsum(Ks, axis=1) - Ks
            inter = jnp.einsum('bnchd,bnhde->bnche', q, KVcum)
            den_inter = jnp.einsum('bnchd,bnhd->bnch', q, Kcum)
            scores = jnp.einsum('bnchd,bnkhd->bnhck', q, k)
            mask = jnp.tril(jnp.ones((CHUNK, CHUNK), dtype=bool))
            scores = jnp.where(mask, scores, 0.0)
            intra = jnp.einsum('bnhck,bnkhe->bnche', scores, v)
            den_intra = jnp.transpose(jnp.sum(scores, axis=-1), (0, 1, 3, 2))
            out = (inter + intra) / (den_inter + den_intra + ATT_EPS)[..., None]
            return out.reshape(B, S, Hn, D)

        def _forward(x, Wq, bq, Wk, bk, Wv, bv, Wo, bo, W1, b1, W2, b2, g1, be1, g2, be2, gf, bef):
            B, S, Dm = x.shape
            for l in range(L):
                q = (x @ Wq[l] + bq[l]).reshape(B, S, H, HD)
                k = (x @ Wk[l] + bk[l]).reshape(B, S, H, HD)
                v = (x @ Wv[l] + bv[l]).reshape(B, S, H, HD)
                att = _causal_linear_attention(_feature_map(q), _feature_map(k), v)
                x = x + att.reshape(B, S, Dm) @ Wo[l] + bo[l]
                y = x = _ln(x, g1[l], be1[l])
                y = jax.nn.gelu(y @ W1[l] + b1[l], approximate=False)
                y = y @ W2[l] + b2[l]
                x = _ln(x + y, g2[l], be2[l])
            return _ln(x, gf, bef)
        key = jax.random.key(seed)
        ks = jax.random.split(key, 8)
        B, S = (2, 512)
        sc = 0.02

        def w(k, shape):
            return jax.random.normal(k, shape, jnp.float32) * sc
        return {'x': jax.random.normal(ks[0], (B, S, D_MODEL), jnp.float32), 'Wq': w(ks[1], (L, D_MODEL, D_MODEL)), 'bq': jnp.zeros((L, D_MODEL), jnp.float32), 'Wk': w(ks[2], (L, D_MODEL, D_MODEL)), 'bk': jnp.zeros((L, D_MODEL), jnp.float32), 'Wv': w(ks[3], (L, D_MODEL, D_MODEL)), 'bv': jnp.zeros((L, D_MODEL), jnp.float32), 'Wo': w(ks[4], (L, D_MODEL, D_MODEL)), 'bo': jnp.zeros((L, D_MODEL), jnp.float32), 'W1': w(ks[5], (L, D_MODEL, D_FF)), 'b1': jnp.zeros((L, D_FF), jnp.float32), 'W2': w(ks[6], (L, D_FF, D_MODEL)), 'b2': jnp.zeros((L, D_MODEL), jnp.float32), 'g1': jnp.ones((L, D_MODEL), jnp.float32), 'be1': jnp.zeros((L, D_MODEL), jnp.float32), 'g2': jnp.ones((L, D_MODEL), jnp.float32), 'be2': jnp.zeros((L, D_MODEL), jnp.float32), 'gf': jnp.ones((D_MODEL,), jnp.float32), 'bef': jnp.zeros((D_MODEL,), jnp.float32)}
    _L1_attn_in = _L1_attn_setup()

    def _L1_ffn_setup():
        import jax, jax.numpy as jnp
        import numpy as np
        NUM_EXPERTS = 8
        EXPERT_CAPACITY = 2.0
        key = jax.random.key(seed)
        k1, k2, k3, k4 = jax.random.split(key, 4)
        B, T, C, H, E = (4, 512, 128, 512, NUM_EXPERTS)
        x = jax.random.normal(k1, (B, T, C), jnp.float32)
        gate_w = jax.random.normal(k2, (C, E), jnp.float32) * 0.02
        w1 = jax.random.normal(k3, (E, C, H), jnp.float32) * 0.02
        w2 = jax.random.normal(k4, (E, H, C), jnp.float32) * 0.02
        return {'x': x, 'gate_w': gate_w, 'w1': w1, 'w2': w2}
    _L1_ffn_in = _L1_ffn_setup()
    _d = {'L0_attn_hidden_states': _L0_attn_in['hidden_states'], 'L0_attn_attention_mask': _L0_attn_in['attention_mask'], 'L0_attn_Wk': _L0_attn_in['Wk'], 'L0_attn_bk': _L0_attn_in['bk'], 'L0_attn_Wka': _L0_attn_in['Wka'], 'L0_attn_bka': _L0_attn_in['bka'], 'L0_attn_Wv': _L0_attn_in['Wv'], 'L0_attn_bv': _L0_attn_in['bv'], 'L0_attn_gamma': _L0_attn_in['gamma'], 'L0_attn_beta': _L0_attn_in['beta'], 'L0_ffn_weights': _L0_ffn_in['weights'], 'L0_ffn_scale': _L0_ffn_in['scale'], 'L0_ffn_bias': _L0_ffn_in['bias'], 'L1_attn_Wq': _L1_attn_in['Wq'], 'L1_attn_bq': _L1_attn_in['bq'], 'L1_attn_Wk': _L1_attn_in['Wk'], 'L1_attn_bk': _L1_attn_in['bk'], 'L1_attn_Wv': _L1_attn_in['Wv'], 'L1_attn_bv': _L1_attn_in['bv'], 'L1_attn_Wo': _L1_attn_in['Wo'], 'L1_attn_bo': _L1_attn_in['bo'], 'L1_attn_W1': _L1_attn_in['W1'], 'L1_attn_b1': _L1_attn_in['b1'], 'L1_attn_W2': _L1_attn_in['W2'], 'L1_attn_b2': _L1_attn_in['b2'], 'L1_attn_g1': _L1_attn_in['g1'], 'L1_attn_be1': _L1_attn_in['be1'], 'L1_attn_g2': _L1_attn_in['g2'], 'L1_attn_be2': _L1_attn_in['be2'], 'L1_attn_gf': _L1_attn_in['gf'], 'L1_attn_bef': _L1_attn_in['bef'], 'L1_ffn_gate_w': _L1_ffn_in['gate_w'], 'L1_ffn_w1': _L1_ffn_in['w1'], 'L1_ffn_w2': _L1_ffn_in['w2']}
    _x0 = _d['L0_attn_hidden_states']
    _d['L0_attn_hidden_states'] = jax.random.normal(jax.random.fold_in(jax.random.key(seed), 1), (4, 512, 128), dtype=_x0.dtype)
    del _x0
    return _d

def reference(L0_attn_hidden_states, L0_attn_attention_mask, L0_attn_Wk, L0_attn_bk, L0_attn_Wka, L0_attn_bka, L0_attn_Wv, L0_attn_bv, L0_attn_gamma, L0_attn_beta, L0_ffn_weights, L0_ffn_scale, L0_ffn_bias, L1_attn_Wq, L1_attn_bq, L1_attn_Wk, L1_attn_bk, L1_attn_Wv, L1_attn_bv, L1_attn_Wo, L1_attn_bo, L1_attn_W1, L1_attn_b1, L1_attn_W2, L1_attn_b2, L1_attn_g1, L1_attn_be1, L1_attn_g2, L1_attn_be2, L1_attn_gf, L1_attn_bef, L1_ffn_gate_w, L1_ffn_w1, L1_ffn_w2):

    def _L0_attn_ref(hidden_states, attention_mask, Wk, bk, Wka, bka, Wv, bv, gamma, beta):
        import jax, jax.numpy as jnp
        import numpy as np
        D = 128
        B = 4
        S = 512
        LN_EPS = 1e-05

        def _layer_norm(x, gamma, beta):
            mu = jnp.mean(x, axis=-1, keepdims=True)
            var = jnp.mean(jnp.square(x - mu), axis=-1, keepdims=True)
            return (x - mu) * jax.lax.rsqrt(var + LN_EPS) * gamma + beta
        h = _layer_norm(hidden_states, gamma, beta)
        d_model = h.shape[-1]
        keys = jnp.einsum('bsd,ed->bse', h, Wk) + bk
        values = jnp.einsum('bsd,ed->bse', h, Wv) + bv
        key_att = jnp.einsum('bsd,ed->bse', keys, Wka) + bka
        keys_weight = jnp.exp(key_att / jnp.sqrt(jnp.asarray(d_model, h.dtype)))
        keys_weight = keys_weight / jnp.cumsum(keys_weight, axis=1)
        pooled_keys = jnp.cumsum(keys_weight * keys, axis=1)
        return pooled_keys * values

    def _L0_ffn_ref(x, weights, scale, bias):
        import jax, jax.numpy as jnp
        import numpy as np
        MAX_VAL = 100.0
        w = (weights >= 0.0).astype(x.dtype) * 2.0 - 1.0
        y = jnp.einsum('bsi,oi->bso', x, w)
        y = y * scale + bias
        y = jnp.clip(y, -MAX_VAL, MAX_VAL)
        return y

    def _L1_attn_ref(x, Wq, bq, Wk, bk, Wv, bv, Wo, bo, W1, b1, W2, b2, g1, be1, g2, be2, gf, bef):
        import jax, jax.numpy as jnp
        import numpy as np
        L, H, D_MODEL, D_FF = (4, 16, 128, 512)
        HD = D_MODEL // H
        LN_EPS = 1e-05
        ATT_EPS = 1e-06
        CHUNK = 128

        def _ln(x, g, b):
            m = jnp.mean(x, axis=-1, keepdims=True)
            v = jnp.var(x, axis=-1, keepdims=True)
            return (x - m) * jax.lax.rsqrt(v + LN_EPS) * g + b

        def _feature_map(x):
            return jax.nn.elu(x) + 1.0

        def _causal_linear_attention(q, k, v):
            B, S, Hn, D = q.shape
            nC = S // CHUNK
            q = q.reshape(B, nC, CHUNK, Hn, D)
            k = k.reshape(B, nC, CHUNK, Hn, D)
            v = v.reshape(B, nC, CHUNK, Hn, D)
            KV = jnp.einsum('bnchd,bnche->bnhde', k, v)
            Ks = jnp.sum(k, axis=2)
            KVcum = jnp.cumsum(KV, axis=1) - KV
            Kcum = jnp.cumsum(Ks, axis=1) - Ks
            inter = jnp.einsum('bnchd,bnhde->bnche', q, KVcum)
            den_inter = jnp.einsum('bnchd,bnhd->bnch', q, Kcum)
            scores = jnp.einsum('bnchd,bnkhd->bnhck', q, k)
            mask = jnp.tril(jnp.ones((CHUNK, CHUNK), dtype=bool))
            scores = jnp.where(mask, scores, 0.0)
            intra = jnp.einsum('bnhck,bnkhe->bnche', scores, v)
            den_intra = jnp.transpose(jnp.sum(scores, axis=-1), (0, 1, 3, 2))
            out = (inter + intra) / (den_inter + den_intra + ATT_EPS)[..., None]
            return out.reshape(B, S, Hn, D)

        def _forward(x, Wq, bq, Wk, bk, Wv, bv, Wo, bo, W1, b1, W2, b2, g1, be1, g2, be2, gf, bef):
            B, S, Dm = x.shape
            for l in range(L):
                q = (x @ Wq[l] + bq[l]).reshape(B, S, H, HD)
                k = (x @ Wk[l] + bk[l]).reshape(B, S, H, HD)
                v = (x @ Wv[l] + bv[l]).reshape(B, S, H, HD)
                att = _causal_linear_attention(_feature_map(q), _feature_map(k), v)
                x = x + att.reshape(B, S, Dm) @ Wo[l] + bo[l]
                y = x = _ln(x, g1[l], be1[l])
                y = jax.nn.gelu(y @ W1[l] + b1[l], approximate=False)
                y = y @ W2[l] + b2[l]
                x = _ln(x + y, g2[l], be2[l])
            return _ln(x, gf, bef)
        return _forward(x, Wq, bq, Wk, bk, Wv, bv, Wo, bo, W1, b1, W2, b2, g1, be1, g2, be2, gf, bef)

    def _L1_ffn_ref(x, gate_w, w1, w2):
        import jax, jax.numpy as jnp
        import numpy as np
        NUM_EXPERTS = 8
        EXPERT_CAPACITY = 2.0
        B, T, C = x.shape
        E = gate_w.shape[1]
        cap = int(EXPERT_CAPACITY * T / E)
        scores = jnp.einsum('BTC,CE->BTE', x, gate_w)
        probs = jax.nn.softmax(scores, axis=-1)
        probs_et = jnp.transpose(probs, (0, 2, 1))
        top_p, top_idx = jax.lax.top_k(probs_et, cap)
        xin = jnp.take_along_axis(x[:, None, :, :], top_idx[..., None], axis=2)
        h = jax.nn.gelu(jnp.einsum('BElC,ECH->BElH', xin, w1), approximate=False)
        y = jnp.einsum('BElH,EHC->BElC', h, w2)
        y = y * top_p[..., None]
        b_idx = jnp.arange(B)[:, None, None]
        out = jnp.zeros((B, T, C), x.dtype).at[b_idx, top_idx].add(y)
        return out
    x = L0_attn_hidden_states
    x = _layernorm(x + _L0_attn_ref(x, L0_attn_attention_mask, L0_attn_Wk, L0_attn_bk, L0_attn_Wka, L0_attn_bka, L0_attn_Wv, L0_attn_bv, L0_attn_gamma, L0_attn_beta), axis=-1)
    x = _layernorm(x + _L0_ffn_ref(x, L0_ffn_weights, L0_ffn_scale, L0_ffn_bias), axis=-1)
    x = _layernorm(x + _L1_attn_ref(x, L1_attn_Wq, L1_attn_bq, L1_attn_Wk, L1_attn_bk, L1_attn_Wv, L1_attn_bv, L1_attn_Wo, L1_attn_bo, L1_attn_W1, L1_attn_b1, L1_attn_W2, L1_attn_b2, L1_attn_g1, L1_attn_be1, L1_attn_g2, L1_attn_be2, L1_attn_gf, L1_attn_bef), axis=-1)
    x = _layernorm(x + _L1_ffn_ref(x, L1_ffn_gate_w, L1_ffn_w1, L1_ffn_w2), axis=-1)
    return x

_drawn_inputs = setup_inputs


def setup_inputs(seed=0):
    import zlib

    import numpy as np

    out = dict(_drawn_inputs(seed))
    spreads = {'L0_attn_bk': (0.0, 0.1),
     'L0_attn_bka': (0.0, 2.0),
     'L0_attn_bv': (0.0, 0.1),
     'L0_attn_gamma': (1.0, 0.2),
     'L0_attn_beta': (0.0, 0.1),
     'L0_ffn_scale': (1.0, 0.2),
     'L1_attn_bq': (0.0, 2.0),
     'L1_attn_bk': (0.0, 2.0),
     'L1_attn_bv': (0.0, 0.339),
     'L1_attn_bo': (0.0, 0.1),
     'L1_attn_b1': (0.0, 0.311),
     'L1_attn_b2': (0.0, 0.1),
     'L1_attn_g1': (1.0, 0.2),
     'L1_attn_be1': (0.0, 0.1),
     'L1_attn_g2': (1.0, 0.2),
     'L1_attn_be2': (0.0, 0.1),
     'L1_attn_gf': (1.0, 0.2),
     'L1_attn_bef': (0.0, 0.1)}
    factors = {'L1_attn_Wq': 8.0,
     'L1_attn_Wk': 8.0,
     'L1_attn_Wv': 3.771,
     'L1_ffn_gate_w': 5.42,
     'L1_ffn_w1': 4.738,
     'L1_ffn_w2': 4.645}
    for name, (base, spread) in spreads.items():
        noise = np.random.default_rng([zlib.crc32(name.encode()), seed]).standard_normal(out[name].shape)
        drawn = base * np.exp(spread * noise) if base else spread * noise
        out[name] = jnp.asarray(drawn.astype(out[name].dtype))
    for name, factor in factors.items():
        out[name] = (out[name] * factor).astype(out[name].dtype)
    return out
```

```python
import concourse.bass as bass
from concourse import mybir
from contextlib import ExitStack

D = 128
B = 4
S = 512
NT = S // 128
L = 4
FF = 512
NF = FF // 128
HEADS = 16
HD = D // HEADS
Q4 = 4
C = 32
NC = S // C
E = 8
CAP = 2 * S // E
LN_EPS = 1e-5
ATT_EPS = 1e-6
MAX_VAL = 100.0
UNITS = L * B
LN_EXP = "natural_log_exp_and_others"


def build(nc, a, out):
    f32 = mybir.dt.float32
    i32 = mybir.dt.int32
    ALU = mybir.AluOpType
    ACT = mybir.ActivationFunctionType
    AX = mybir.AxisListType

    ctx = ExitStack()
    with ctx:
        def sb(name, shape, dt=f32):
            return ctx.enter_context(nc.sbuf_tensor(name, shape, dt))

        def pb(name):
            return ctx.enter_context(nc.psum_tensor(name, [128, 512], f32))

        def sem(name):
            return ctx.enter_context(nc.semaphore(name))

        ident = sb("ident", [128, 128])
        ones = sb("ones", [128, 128])
        causal = sb("causal", [128, 4, 128])
        same_g = sb("same_g", [128, 4])
        same_g_wide = sb("same_g_wide", [128, C, NC])
        scan_keep = sb("scan_keep", [128, C, NC])
        same_head = sb("same_head", [128, 128])
        slot_row = sb("slot_row", [128, 128])
        slot_int = sb("slot_int", [128, 128], i32)
        ln_eps = sb("ln_eps", [128, 1])
        att_eps = sb("att_eps", [128, 1])

        w0 = sb("w0", [128, 4, 128])
        w0_sign = sb("w0_sign", [128, 128])
        cols0 = sb("cols0", [128, 5])
        bka_s = sb("bka_s", [128, 1])
        rows0 = sb("rows0", [128, 5, 128])
        w_qkv = sb("w_qkv", [128, 3, 128])
        w_o = sb("w_o", [128, 128])
        w_1 = sb("w_1", [128, FF])
        w_2 = sb("w_2", [128, NF, 128])
        cols_a = sb("cols_a", [128, 2])
        row_v = sb("row_v", [128, 128])
        cols_1 = sb("cols_1", [128, 2 + NF])
        rows_1 = sb("rows_1", [128, 3, 128])
        cols_2 = sb("cols_2", [128, 2])
        rows_2 = sb("rows_2", [128, 3, 128])
        shift_1 = sb("shift_1", [128, 128])
        shift_2 = sb("shift_2", [128, 128])
        gate_w = sb("gate_w", [128, E])
        we_1 = sb("we_1", [128, E, FF])
        we_2 = sb("we_2", [128, E, NF, 128])

        xT = sb("xT", [128, B, S])
        res = sb("res", [128, B, NT, 128])
        x2 = sb("x2", [128, B, NT, 128])

        qT = sb("qT", [128, S])
        kT = sb("kT", [128, S])
        q_exp = sb("q_exp", [128, S])
        k_exp = sb("k_exp", [128, S])
        q_lin = sb("q_lin", [128, S])
        k_lin = sb("k_lin", [128, S])
        keys_g = sb("keys_g", [128, NC, 4, C])
        queries_j = sb("queries_j", [128, NC, 4, C])
        values_g = sb("values_g", [128, NC, 4, 4, HD])
        keys_tm = sb("keys_tm", [128, NT, 128])
        v_blk = sb("v_blk", [128, NT, 4, 128])
        probs = sb("probs", [128, NC, 128])
        kv = sb("kv", [128, C, NC])
        state = sb("state", [128, C, NC])
        state_blk = sb("state_blk", [128, NC, 128])
        k_sum = sb("k_sum", [128, S])
        qk_sum = sb("qk_sum", [128, S])
        log_den = sb("log_den", [128, S])
        inv_den = sb("inv_den", [128, S])
        attT = sb("attT", [128, S])
        y1 = sb("y1", [128, NT, 128])
        z1 = sb("z1", [128, NT, 128])
        x1T = sb("x1T", [128, S])
        res1 = sb("res1", [128, NT, 128])
        hidden = sb("hidden", [128, NF, S])
        y2 = sb("y2", [128, NT, 128])
        z2 = sb("z2", [128, NT, 128])
        bn1 = sb("bn1", [128, NT, 6])
        mv1 = sb("mv1", [128, NT, 2])
        lv1 = sb("lv1", [128, NT])
        rs1 = sb("rs1", [128, NT])
        bn2 = sb("bn2", [128, NT, 6])
        mv2 = sb("mv2", [128, NT, 2])
        lv2 = sb("lv2", [128, NT])
        rs2 = sb("rs2", [128, NT])
        bn0 = sb("bn0", [128, B, NT, 6])
        mv0 = sb("mv0", [128, B, NT, 2])
        lv0 = sb("lv0", [128, B, NT])
        rs0 = sb("rs0", [128, B, NT])
        logits_max = sb("logits_max", [128, B * NT])
        gate_e = sb("gate_e", [128, B, NT, E])
        gate_sum = sb("gate_sum", [128, B * NT])
        gate_inv = sb("gate_inv", [128, B * NT])
        gate_p = sb("gate_p", [128, B, NT, E])
        gate_t = sb("gate_t", [128, NT, B * E])
        pos_tm = sb("pos_tm", [128, NT, B * E])
        top8 = sb("top8", [32, 8])
        rank_a = sb("rank_a", [32, S])
        rank_b = sb("rank_b", [32, S])

        x_in = probs[:, :, :].rearrange("p (b t) d -> p b t d", b=B)
        z0 = state_blk[:, :, :].rearrange("p (b t) d -> p b t d", b=B)
        hT = keys_g[:, :, :, :].rearrange("p (b n) g c -> p b (n g c)", b=B)
        keys0 = hidden
        vals0 = we_1[:, 0:4, :]
        ka0 = we_1[:, 4:8, :]
        cum0 = we_2[:, 0:4, :, :].rearrange("p a f d -> p a (f d)")
        kw0 = we_2[:, 4:8, :, :].rearrange("p a f d -> p a (f d)")
        pick = [t[:, 8 * i:8 * i + 8, :, :].rearrange("p (h n) g c -> p h (n g c)", h=2)
                for t in (keys_g, queries_j) for i in range(2)]
        xg_a = [t[:, :, :] for t in (probs, state_blk)]

        bank_q = pb("bank_q")
        bank_k = pb("bank_k")
        bank_tm = pb("bank_tm")
        bank_tr = pb("bank_tr")
        bank_kv = pb("bank_kv")
        bank_s = [pb("bank_s0"), pb("bank_s1")]
        bank_o = pb("bank_o")
        banks = [bank_q, bank_k, bank_tm, bank_tr, bank_kv, bank_s[0], bank_s[1], bank_o]

        def tiles(bank):
            return bank[:, :].rearrange("p (t d) -> p t d", d=128)

        def over_tiles(row):
            return row.unsqueeze(1).broadcast_to([128, NT, 128])

        ld_x = [sem(f"ld_x{b}") for b in range(B)]
        ld_w0 = sem("ld_w0")
        ld_c0 = sem("ld_c0")
        ld_r0 = sem("ld_r0")
        ld_a = sem("ld_a")
        ld_o = sem("ld_o")
        ld_1 = sem("ld_1")
        ld_2 = sem("ld_2")
        ld_2v = sem("ld_2v")
        ld_e = sem("ld_e")
        st_out = sem("st_out")
        c_set = sem("c_set")
        c_sel = sem("c_sel")
        c_done = sem("c_done")
        c_wide = sem("c_wide")
        d_bn = sem("d_bn")
        d_mv = sem("d_mv")
        d_lv = sem("d_lv")
        d_rs = sem("d_rs")
        d_z = sem("d_z")
        p_a = sem("p_a")
        a_hT = sem("a_hT")
        a_key = sem("a_key")
        v_val = sem("v_val")
        v_bka = sem("v_bka")
        v_sgn = sem("v_sgn")
        a_ka = sem("a_ka")
        a_ew = sem("a_ew")
        v_cum = sem("v_cum")
        a_lc = sem("a_lc")
        v_t = sem("v_t")
        a_kw = sem("a_kw")
        g_pk = sem("g_pk")
        v_pool = sem("v_pool")
        g_prod = sem("g_prod")
        v_y = sem("v_y")
        a_x1T = sem("a_x1T")
        v_sc = sem("v_sc")
        g_bi = sem("g_bi")
        v_cl = sem("v_cl")
        pe_q = sem("pe_q")
        pe_k = sem("pe_k")
        pe_v = sem("pe_v")
        pe_z1T = sem("pe_z1T")
        pe_h = sem("pe_h")
        pe_kT = sem("pe_kT")
        pe_kv = sem("pe_kv")
        pe_s = sem("pe_s")
        pe_den = sem("pe_den")
        pe_y2 = sem("pe_y2")
        pe_o = sem("pe_o")
        pe_z2T = sem("pe_z2T")
        pe_wo = sem("pe_wo")
        s_qe = sem("s_qe")
        s_ke = sem("s_ke")
        s_lv1 = sem("s_lv1")
        s_rs1 = sem("s_rs1")
        s_lv2 = sem("s_lv2")
        s_rs2 = sem("s_rs2")
        s_x1T = sem("s_x1T")
        s_h = sem("s_h")
        s_qj = sem("s_qj")
        s_ktm = sem("s_ktm")
        s_sblk = sem("s_sblk")
        s_ld = sem("s_ld")
        s_inv = sem("s_inv")
        s_xT = sem("s_xT")
        s_y1 = sem("s_y1")
        s_bn1 = sem("s_bn1")
        s_mv1 = sem("s_mv1")
        s_z1 = sem("s_z1")
        s_ql = sem("s_ql")
        s_kl = sem("s_kl")
        s_q = sem("s_q")
        s_k = sem("s_k")
        s_v = sem("s_v")
        s_kg = sem("s_kg")
        s_ks = sem("s_ks")
        s_kv = sem("s_kv")
        s_st = sem("s_st")
        s_p = sem("s_p")
        s_y2 = sem("s_y2")
        s_bn2 = sem("s_bn2")
        s_mv2 = sem("s_mv2")
        s_z2 = sem("s_z2")
        s_att = sem("s_att")
        s_sh1 = sem("s_sh1")
        s_sh2 = sem("s_sh2")
        s_r1m = sem("s_r1m")
        s_r1 = sem("s_r1")
        s_r2m = sem("s_r2m")
        s_res = sem("s_res")
        s_vg = sem("s_vg")
        s_vd = sem("s_vd")
        s_qk = sem("s_qk")
        f_bn = sem("f_bn")
        f_mv = sem("f_mv")
        f_lv = sem("f_lv")
        f_rs = sem("f_rs")
        f_z = sem("f_z")
        f_g = sem("f_g")
        f_b = sem("f_b")
        f_y = sem("f_y")
        pe_x3 = sem("pe_x3")
        a_x3 = sem("a_x3")
        pe_lg = sem("pe_lg")
        m_gate = sem("m_gate")
        a_gate = sem("a_gate")
        pe_gt = sem("pe_gt")
        m_rank = sem("m_rank")
        pe_pt = sem("pe_pt")
        m_pos = sem("m_pos")
        m_pick = sem("m_pick")
        pe_g = sem("pe_g")
        m_xg = sem("m_xg")
        pe_u = sem("pe_u")
        a_u = sem("a_u")
        pe_d = sem("pe_d")
        m_d = sem("m_d")
        m_pp = sem("m_pp")
        pe_pp = sem("pe_pp")
        a_pp = sem("a_pp")
        pe_sc = sem("pe_sc")
        m_sc = sem("m_sc")

        block = ctx.enter_context(nc.Block())

        def unit(l, b):
            return l * B + b

        def of_unit(u):
            return u // B, u % B

        def rows_of(ap):
            return ap.unsqueeze(0).broadcast_to([128] + list(ap.shape))

        one_row = ones[:, 0:1].broadcast_to([128, S])

        def xg(e):
            return xg_a[e // 4][:, 4 * (e % 4):4 * (e % 4) + 4, :]

        def ye(e):
            return xg(e)

        def spread_values(eng, r, g):
            src = v_blk[32 * r:32 * r + 32, :, r, :].rearrange("p t (j g d) -> p t j g d", j=4, g=4)
            dst = values_g[32 * g:32 * g + 32, :, :, :, :].rearrange("p (t r) j g d -> p t r j g d", r=4)
            return eng.tensor_copy(dst[:, :, r, :, g, :], src[:, :, :, g, :])

        def h_e(e):
            return hidden if e % 2 == 0 else he_b

        he_b = v_blk[:, :, :, :].rearrange("p t c d -> p t (c d)")

        def pick_t(k):
            return values_g[:, 8 * (k % 2):8 * (k % 2) + 8, :, :, :].rearrange("p e j g d -> p e (j g d)")

        def expert_down(pe, e):
            pe.wait_ge(a_u, NF * (e + 1))
            if e >= 2:
                pe.wait_ge(m_d, e - 1)
            for b in range(B):
                for f in range(NF):
                    mm = pe.matmul(banks[6 + e % 2][:, b * 128:(b + 1) * 128],
                                   h_e(e)[:, f, b * 128:(b + 1) * 128], we_2[:, e, f, :],
                                   start=(f == 0), stop=(f == NF - 1))
            mm.then_inc(pe_d, 1)

        def gathered(dve, b):
            dve.wait_ge(pe_g, NT * (b + 1))
            for h in range(2):
                dve.tensor_copy(xg_a[h].rearrange("p (e s) d -> p e s d", s=4)[:, :, b, :],
                                tiles(banks[2 * (b % 2) + h])).then_inc(m_xg, 1)

        def weighted(dve, n):
            b, t = n // NT, n % NT
            if n < 4:
                dve.wait_ge(pe_g, B * NT)
            else:
                dve.wait_ge(pe_pp, 2 * (n - 3))
            for e in range(E):
                k = b * E + e
                ins = dve.tensor_scalar(pick[n % 4][:, e // 4, (e % 4) * 128:(e % 4 + 1) * 128],
                                        slot_row[:, :], pos_tm[:, t, k:k + 1], gate_t[:, t, k:k + 1],
                                        ALU.is_equal, ALU.mult)
            ins.then_inc(m_pp, 1)

        @block.sync
        def _(sp):
            x_v = a["x"].rearrange("b (t p) d -> b p t d", p=128)
            for b in range(B):
                sp.dma_start(x_in[:, b, :, :], x_v[b]).then_inc(ld_x[b], 16)
                if b == 0:
                    sp.dma_start(cols0[:, :], a["cols0"]).then_inc(ld_c0, 16)
                    sp.dma_start(w0[:, :, :], a["w0"].rearrange("n i o -> i n o")).then_inc(ld_w0, 16)
            sp.dma_start(rows0[:, :, :], rows_of(a["rows0"])).then_inc(ld_r0, 16)
            sp.dma_start(gate_w[:, :], a["gate_w"]).then_inc(ld_r0, 16)
            for l in range(L):
                if l:
                    sp.wait_ge(s_v, 4 * unit(l, 0))
                    sp.wait_ge(s_ke, unit(l, 0))
                sp.dma_start(w_qkv[:, :, :], a["w_qkv"][l].rearrange("n i o -> i n o")).then_inc(ld_a, 16)
                sp.dma_start(cols_a[:, :], a["cols_a"][l]).then_inc(ld_a, 16)
                sp.dma_start(row_v[:, :], rows_of(a["row_v"][l])).then_inc(ld_a, 16)
                if l:
                    sp.wait_ge(pe_wo, unit(l, 0))
                sp.dma_start(w_o[:, :], a["w_o"][l]).then_inc(ld_o, 16)
                if l:
                    sp.wait_ge(s_h, NF * unit(l, 0))
                    sp.wait_ge(s_sh1, l)
                    sp.wait_ge(s_r1, unit(l, 0))
                sp.dma_start(w_1[:, :], a["w_1"][l]).then_inc(ld_1, 16)
                sp.dma_start(cols_1[:, :], a["cols_1"][l]).then_inc(ld_1, 16)
                sp.dma_start(rows_1[:, :, :], rows_of(a["rows_1"][l])).then_inc(ld_1, 16)
                if l:
                    sp.wait_ge(pe_y2, unit(l, 0))
                sp.dma_start(w_2[:, :, :], a["w_2"][l].rearrange("(f p) d -> p f d", p=128)).then_inc(ld_2, 16)
                if l:
                    sp.wait_ge(s_xT, unit(l + 1, 0))
                    sp.wait_ge(s_res, unit(l + 1, 0))
                sp.dma_start(cols_2[:, :], a["cols_2"][l]).then_inc(ld_2v, 16)
                sp.dma_start(rows_2[:, :, :], rows_of(a["rows_2"][l])).then_inc(ld_2v, 16)
                if l == 0:
                    sp.wait_ge(p_a, 5 * B)
                    sp.dma_start(we_1[:, :, :], a["we_1"].rearrange("e i f -> i e f")).then_inc(ld_e, 16)
                    sp.dma_start(we_2[:, :, :, :],
                                 a["we_2"].rearrange("e (f p) d -> p e f d", p=128)).then_inc(ld_e, 16)
            o_v = out.rearrange("b (t p) d -> b p t d", p=128)
            for n in range(B * NT):
                sp.wait_ge(f_z, NT * 2 * B + n + 1)
                sp.dma_start(o_v[n // NT, :, n % NT, :], res[:, n // NT, n % NT, :]).then_inc(st_out, 16)
            sp.wait_ge(st_out, 16 * B * NT)

        @block.tensor
        def _(pe):
            def transpose4(bank, src):
                for t in range(NT):
                    mm = pe.transpose(bank[:, t * 128:(t + 1) * 128], src[:, t, :], ident[:, :])
                return mm

            pe.wait_ge(c_done, 1)
            for b in range(B):
                pe.wait_ge(d_z, NT * (b + 1))
                transpose4(banks[b], z0[:, b]).then_inc(p_a, 1)
            pe.wait_ge(ld_w0, 16)
            for b in range(B):
                pe.wait_ge(a_hT, b + 1)
                pe.matmul(banks[4 + b][:, :], w0[:, 0, :], hT[:, b], start=True, stop=True).then_inc(p_a, 1)
                pe.matmul(banks[b][:, :], w0[:, 1, :], hT[:, b], start=True, stop=True).then_inc(p_a, 1)
            for b in range(B):
                pe.wait_ge(a_key, b + 1)
                pe.matmul(banks[4 + b][:, :], w0[:, 2, :], keys0[:, b, :], start=True, stop=True)\
                    .then_inc(p_a, 1)
            for b in range(B):
                pe.wait_ge(g_prod, b + 1)
                pe.wait_ge(v_val, b + 1)
                transpose4(banks[b], ka0[:, b].rearrange("p (t d) -> p t d", d=128)).then_inc(p_a, 1)
            for b in range(B):
                pe.wait_ge(d_z, NT * (B + b + 1))
                pe.wait_ge(a_ka, b + 1)
                transpose4(banks[4 + b], res[:, b]).then_inc(p_a, 1)
            pe.wait_ge(v_sgn, 2)
            for b in range(B):
                pe.wait_ge(a_x1T, b + 1)
                for t in range(NT):
                    mm = pe.matmul(banks[b][:, t * 128:(t + 1) * 128], xT[:, b, t * 128:(t + 1) * 128],
                                   w0_sign[:, :], start=True, stop=True)
                mm.then_inc(p_a, 1)
            for b in range(B):
                pe.wait_ge(d_z, NT * (2 * B + b + 1))
                transpose4(banks[4 + b], x2[:, b]).then_inc(p_a, 1)

            def project(l, b):
                u = unit(l, b)
                if b == 0:
                    pe.wait_ge(ld_a, 48 * (l + 1))
                pe.wait_ge(s_xT, u + 1)
                if u:
                    pe.wait_ge(s_ql, u)
                pe.matmul(bank_q[:, :], w_qkv[:, 0, :], xT[:, b, :], start=True, stop=True).then_inc(pe_q, 1)
                if u:
                    pe.wait_ge(s_kl, u)
                pe.matmul(bank_k[:, :], w_qkv[:, 1, :], xT[:, b, :], start=True, stop=True).then_inc(pe_k, 1)
                if u:
                    pe.wait_ge(s_y1, u)
                for t in range(NT):
                    mm = pe.matmul(bank_tm[:, t * 128:(t + 1) * 128], xT[:, b, t * 128:(t + 1) * 128],
                                   w_qkv[:, 2, :], start=True, stop=True)
                mm.then_inc(pe_v, 1)

            def keys_to_tokens(l, b):
                u = unit(l, b)
                pe.wait_ge(s_k, u + 1)
                if u:
                    pe.wait_ge(s_x1T, u)
                transpose4(bank_tr, kT[:, :].rearrange("p (t d) -> p t d", d=128)).then_inc(pe_kT, 1)

            def mlp_up(l, b, other):
                m = unit(l, b)
                pe.wait_ge(s_z1, NT * (m + 1))
                if 2 <= m <= UNITS - B + 1:
                    pe.wait_ge(s_xT, B + m - 1)
                elif m > UNITS - B + 1:
                    pe.wait_ge(s_ktm, m + 1)
                transpose4(bank_tr, z1).then_inc(pe_z1T, 1)
                if b == 0:
                    pe.wait_ge(ld_1, 48 * (l + 1))
                pe.wait_ge(s_x1T, m + 1)
                for f in range(NF):
                    if f < 2:
                        pe.wait_ge(s_p, 4 * (m + 1))
                    else:
                        pe.wait_ge(s_h, NF * m + f - 1)
                    pe.matmul(bank_s[f % 2][:, :], w_1[:, f * 128:(f + 1) * 128], x1T[:, :],
                              start=True, stop=True).then_inc(pe_h, 1)
                    if f == 1 and other:
                        keys_to_tokens(*other)

            def states(l, b):
                u = unit(l, b)
                if u == 1:
                    pe.wait_ge(s_ld, u)
                if u >= 2:
                    pe.wait_ge(s_y2, u - 1)
                pe.wait_ge(s_ktm, u + 1)
                pe.wait_ge(s_v, 4 * (u + 1))
                kv_out = bank_kv[:, :].rearrange("p (c t r) -> p t r c", t=NT, r=4)
                for t in range(NT):
                    for j in range(4):
                        q = slice(32 * j, 32 * j + 32)
                        mm = pe.matmul(kv_out[q, t, :, :], keys_tm[:, t, q], v_blk[:, t, :, q],
                                       start=True, stop=True, skip_group_check=True)
                mm.then_inc(pe_kv, 1)

            def scores(l, b):
                u = unit(l, b)
                pe.wait_ge(s_kg, 4 * (u + 1))
                pe.wait_ge(s_qj, 4 * (u + 1))
                for c4 in range(4):
                    if c4 < 2:
                        if u:
                            pe.wait_ge(s_h, NF * (u - 1) + 3 + c4)
                    else:
                        pe.wait_ge(s_p, 4 * u + c4 - 1)
                    for i in range(4):
                        n = 4 * c4 + i
                        mm = pe.matmul(bank_s[c4 % 2][:, i * 128:(i + 1) * 128], keys_g[:, n, :, :],
                                       queries_j[:, n, :, :], start=True, stop=True)
                    mm.then_inc(pe_s, 1)

            def denominators(l, b):
                u = unit(l, b)
                pe.wait_ge(s_qk, u + 1)
                pe.wait_ge(s_kv, u + 1)
                pe.matmul(bank_kv[:, :], same_head[:, :], qk_sum[:, :], start=True, stop=True)\
                    .then_inc(pe_den, 1)

            def mlp_down(l, b, first, last):
                m = unit(l, b)
                if first == 0:
                    if b == 0:
                        pe.wait_ge(ld_2, 16 * (l + 1))
                    pe.wait_ge(s_h, NF * (m + 1))
                    if m + 1 < UNITS:
                        pe.wait_ge(s_ld, m + 2)
                    else:
                        pe.wait_ge(s_y2, m)
                for t in range(first, last):
                    for f in range(NF):
                        mm = pe.matmul(bank_kv[:, t * 128:(t + 1) * 128], hidden[:, f, t * 128:(t + 1) * 128],
                                       w_2[:, f, :], start=(f == 0), stop=(f == NF - 1))
                if last == NT:
                    mm.then_inc(pe_y2, 1)

            def attend(l, b):
                u = unit(l, b)
                if u:
                    pe.wait_ge(s_att, u)
                pe.wait_ge(s_sblk, 4 * (u + 1))
                for n in range(1, NC):
                    pe.matmul(bank_o[:, n * C:(n + 1) * C], state_blk[:, n - 1, :], qT[:, n * C:(n + 1) * C],
                              start=(n == 1), stop=False, skip_group_check=True)
                pe.wait_ge(s_vg, 8 * (u + 1))
                pe.wait_ge(s_vd, 8 * (u + 1))
                for n in range(NC):
                    if n % 4 == 0:
                        pe.wait_ge(s_p, 4 * u + n // 4 + 1)
                    for j in range(4):
                        mm = pe.matmul(bank_o[32 * j:32 * j + 32, n * C:(n + 1) * C], values_g[:, n, j, :, :],
                                       probs[:, n, j * C:(j + 1) * C], start=False, stop=True,
                                       skip_group_check=True)
                mm.then_inc(pe_o, 1)

            def back_to_features(l, b):
                m = unit(l, b)
                pe.wait_ge(s_z2, NT * (m + 1))
                pe.wait_ge(s_ktm, m + 3)
                transpose4(bank_tr, z2).then_inc(pe_z2T, 1)

            def output(l, b):
                u = unit(l, b)
                if b == 0:
                    pe.wait_ge(ld_o, 16 * (l + 1))
                pe.wait_ge(s_att, u + 1)
                pe.wait_ge(s_v, 4 * (u + 1))
                for t in range(NT):
                    mm = pe.matmul(bank_tm[:, t * 128:(t + 1) * 128], attT[:, t * 128:(t + 1) * 128],
                                   w_o[:, :], start=True, stop=True)
                mm.then_inc(pe_wo, 1)

            pe.wait_ge(g_bi, B)
            pe.wait_ge(s_xT, B)
            pe.wait_ge(c_wide, 4)
            for u in range(UNITS + 1):
                now, before, old = of_unit(u), of_unit(u - 1), of_unit(u - 2)
                if u < UNITS:
                    project(*now)
                if u:
                    mlp_up(*before, now if u < UNITS else None)
                else:
                    keys_to_tokens(*now)
                if u < UNITS:
                    states(*now)
                    scores(*now)
                    denominators(*now)
                    attend(*now)
                if 2 <= u < UNITS - B + 2:
                    back_to_features(*old)
                if u:
                    mlp_down(*before, 0, 1)
                if u < UNITS:
                    output(*now)
                if u:
                    mlp_down(*before, 1, NT)

            pe.wait_ge(s_y1, UNITS)
            pe.wait_ge(s_x1T, UNITS)
            for b in range(B):
                pe.wait_ge(f_z, NT * (B + b + 1))
                transpose4(banks[b], x2[:, b]).then_inc(pe_x3, 1)
            pe.wait_ge(ld_r0, 32)
            for b in range(B):
                pe.wait_ge(a_x3, b + 1)
                for t in range(NT):
                    n = b * NT + t
                    mm = pe.matmul(banks[4][:, n * E:(n + 1) * E], xT[:, b, t * 128:(t + 1) * 128],
                                   gate_w[:, :], start=True, stop=True)
            mm.then_inc(pe_lg, 1)
            pe.wait_ge(m_gate, 5)
            for t in range(NT):
                mm = pe.transpose(banks[5][0:32, t * 128:(t + 1) * 128], gate_t[:, t, :], ident[:, :])
            mm.then_inc(pe_gt, 1)
            pe.wait_ge(m_rank, 36)
            for t in range(NT):
                mm = pe.transpose(banks[6][:, t * 32:(t + 1) * 32], rank_b[:, t * 128:(t + 1) * 128],
                                  ident[0:32, 0:32])
            mm.then_inc(pe_pt, 1)
            for b in range(B):
                for t in range(NT):
                    n = b * NT + t
                    pe.wait_ge(m_pick, n + 1)
                    if t == 0 and b >= 2:
                        pe.wait_ge(m_xg, 2 * (b - 1))
                    for h in range(2):
                        mm = pe.matmul(banks[2 * (b % 2) + h][:, :], x2[:, b, t, :],
                                       pick[n % 4][:, h, :],
                                       start=(t == 0), stop=(t == NT - 1), skip_group_check=True)
                    mm.then_inc(pe_g, 1)
            pe.wait_ge(ld_e, 32)
            for e in range(E):
                for f in range(NF):
                    n = e * NF + f
                    if e == 0 and f == 0:
                        pe.wait_ge(m_xg, 2 * B)
                    if n >= 2:
                        pe.wait_ge(a_u, n - 1)
                    pe.matmul(banks[4 + n % 2][:, :], we_1[:, e, f * 128:(f + 1) * 128], xg(e),
                              start=True, stop=True).then_inc(pe_u, 1)
                if e:
                    expert_down(pe, e - 1)
            expert_down(pe, E - 1)
            for n in range(B * NT + 1):
                if n < B * NT:
                    pe.wait_ge(m_pp, n + 1)
                    for h in range(2):
                        if n == 0:
                            pe.wait_ge(m_xg, 2 * B)
                        else:
                            pe.wait_ge(a_pp, 2 * (n - 1) + h + 1)
                        for i in range(4):
                            mm = pe.transpose(banks[h][:, i * 128:(i + 1) * 128],
                                              pick[n % 4][:, h, i * 128:(i + 1) * 128], ident[:, :])
                        mm.then_inc(pe_pp, 1)
                if n:
                    k = n - 1
                    pe.wait_ge(a_pp, 2 * (k + 1))
                    if k == 0:
                        pe.wait_ge(m_d, E)
                    if k >= 2:
                        pe.wait_ge(m_sc, k - 1)
                    for e in range(E):
                        mm = pe.matmul(banks[2 + k % 2][:, 0:128], pick_t(k)[:, e, :], ye(e)[:, k // NT, :],
                                       start=(e == 0), stop=(e == E - 1))
                    mm.then_inc(pe_sc, 1)

        @block.scalar
        def _(act):
            def rstd(mv, lv, rs, ready, count, s_lv, s_rs, n):
                act.wait_ge(ready, count)
                act.activation(lv, mv, ACT.Ln, bias=ln_eps[:, 0:1]).then_inc(s_lv, 1)
                act.wait_ge(s_lv, n)
                act.activation(rs, lv, ACT.Exp, scale=-0.5).then_inc(s_rs, 1)

            act.preload_act_table_set(LN_EXP)
            act.wait_ge(c_set, 2)
            for b in range(B):
                rstd(mv0[:, b, :, 1], lv0[:, b, :], rs0[:, b, :], d_mv, NT * (b + 1), d_lv, d_rs, b + 1)
            act.wait_ge(ld_c0, 16)
            for b in range(B):
                act.wait_ge(p_a, b + 1)
                act.activation(hT[:, b], banks[b][:, :], ACT.Identity, bias=cols0[:, 1:2],
                               scale=cols0[:, 0:1]).then_inc(a_hT, 1)
            for b in range(B):
                act.wait_ge(p_a, B + 2 * b + 1)
                act.activation(keys0[:, b, :], banks[4 + b][:, :], ACT.Identity, bias=cols0[:, 2:3])\
                    .then_inc(a_key, 1)
            act.wait_ge(v_bka, 1)
            for b in range(B):
                act.wait_ge(p_a, 3 * B + b + 1)
                act.activation(ka0[:, b], banks[4 + b][:, :], ACT.Identity, bias=bka_s[:, 0:1],
                               scale=float(D) ** -0.5).then_inc(a_ka, 1)
                act.wait_ge(a_ka, b + 1)
                act.activation(kw0[:, b], ka0[:, b], ACT.Exp).then_inc(a_ew, 1)
            for b in range(B):
                act.wait_ge(v_cum, b + 1)
                act.activation(cum0[:, b], cum0[:, b], ACT.Ln).then_inc(a_lc, 1)
            for b in range(B):
                act.wait_ge(v_t, b + 1)
                act.activation(kw0[:, b], ka0[:, b], ACT.Exp).then_inc(a_kw, 1)
            for b in range(B):
                rstd(mv0[:, b, :, 1], lv0[:, b, :], rs0[:, b, :], d_mv, NT * (B + b + 1), d_lv, d_rs, B + b + 1)
            for b in range(B):
                act.wait_ge(p_a, 5 * B + b + 1)
                act.activation(xT[:, b, :], banks[4 + b][:, :], ACT.Copy).then_inc(a_x1T, 1)
            for b in range(B):
                rstd(mv0[:, b, :, 1], lv0[:, b, :], rs0[:, b, :], d_mv, NT * (2 * B + b + 1), d_lv, d_rs,
                     2 * B + b + 1)
            for b in range(B):
                act.wait_ge(p_a, 7 * B + b + 1)
                act.activation(xT[:, b, :], banks[4 + b][:, :], ACT.Copy).then_inc(s_xT, 1)

            def norm1(l, b):
                m = unit(l, b)
                rstd(mv1[:, :, 1], lv1[:, :], rs1[:, :], s_mv1, NT * (m + 1), s_lv1, s_rs1, m + 1)

            def feature_map_exp(l, b):
                u = unit(l, b)
                if b == 0:
                    act.wait_ge(ld_a, 48 * (l + 1))
                act.wait_ge(pe_q, u + 1)
                act.activation(q_exp[:, :], bank_q[:, :], ACT.Exp, bias=cols_a[:, 0:1]).then_inc(s_qe, 1)
                act.wait_ge(pe_k, u + 1)
                act.activation(k_exp[:, :], bank_k[:, :], ACT.Exp, bias=cols_a[:, 1:2]).then_inc(s_ke, 1)

            def norm1_to_features(l, b):
                m = unit(l, b)
                if b == 0:
                    act.wait_ge(ld_1, 48 * (l + 1))
                act.wait_ge(pe_z1T, m + 1)
                act.activation(x1T[:, :], bank_tr[:, :], ACT.Identity, bias=cols_1[:, 1:2],
                               scale=cols_1[:, 0:1]).then_inc(s_x1T, 1)

            def gelu(l, b, f):
                m = unit(l, b)
                act.wait_ge(pe_h, NF * m + f + 1)
                act.activation(hidden[:, f, :], bank_s[f % 2][:, :], ACT.Gelu, bias=cols_1[:, 2 + f:3 + f])\
                    .then_inc(s_h, 1)

            def spread_queries(l, b, j):
                act.wait_ge(s_q, unit(l, b) + 1)
                q = slice(32 * j, 32 * j + 32)
                act.activation(queries_j[q, :, j, :], qT[q, :].rearrange("p (n c) -> p n c", c=C),
                               ACT.Copy).then_inc(s_qj, 1)

            def spread_state(l, b):
                act.wait_ge(s_st, unit(l, b) + 1)
                for j in range(4):
                    q = slice(32 * j, 32 * j + 32)
                    act.activation(state_blk[q, :, q], state[q, :, :].rearrange("p c n -> p n c"),
                                   ACT.Copy).then_inc(s_sblk, 1)

            def inverse_denominators(l, b):
                u = unit(l, b)
                act.wait_ge(pe_den, u + 1)
                act.activation(log_den[:, :], bank_kv[:, :], ACT.Ln, bias=att_eps[:, 0:1]).then_inc(s_ld, 1)
                act.wait_ge(s_ld, u + 1)
                act.activation(inv_den[:, :], log_den[:, :], ACT.Exp, scale=-1.0).then_inc(s_inv, 1)

            def norm2(l, b):
                m = unit(l, b)
                rstd(mv2[:, :, 1], lv2[:, :], rs2[:, :], s_mv2, NT * (m + 1), s_lv2, s_rs2, m + 1)

            def norm2_to_features(l, b):
                m = unit(l, b)
                if b == 0:
                    act.wait_ge(ld_2v, 32 * (l + 1))
                act.wait_ge(pe_z2T, m + 1)
                act.activation(xT[:, b, :], bank_tr[:, :], ACT.Identity, bias=cols_2[:, 1:2],
                               scale=cols_2[:, 0:1]).then_inc(s_xT, 1)

            act.wait_ge(c_wide, 4)
            for u in range(UNITS + 2):
                now, before, old = of_unit(u), of_unit(u - 1), of_unit(u - 2)
                if 1 <= u <= UNITS:
                    norm1(*before)
                if u < UNITS:
                    feature_map_exp(*now)
                if 1 <= u <= UNITS:
                    norm1_to_features(*before)
                for f in range(NF):
                    if 1 <= u <= UNITS:
                        gelu(*before, f)
                    if u < UNITS:
                        spread_queries(*now, f)
                if 1 <= u <= UNITS:
                    act.preload_act_table_set(LN_EXP)
                if u < UNITS:
                    spread_state(*now)
                    inverse_denominators(*now)
                if u >= 2:
                    norm2(*old)
                if 2 <= u < UNITS - B + 2:
                    norm2_to_features(*old)

            for n in range(2 * B):
                b = n % B
                rstd(mv0[:, b, :, 1], lv0[:, b, :], rs0[:, b, :], f_mv, NT * (n + 1), f_lv, f_rs, n + 1)
            for b in range(B):
                act.wait_ge(pe_x3, b + 1)
                act.activation(xT[:, b, :], banks[b][:, :], ACT.Copy).then_inc(a_x3, 1)
            act.wait_ge(m_gate, 2)
            act.activation(gate_e[:, :, :, :], gate_e[:, :, :, :], ACT.Exp).then_inc(a_gate, 1)
            for e in range(E):
                for f in range(NF):
                    n = e * NF + f
                    act.wait_ge(pe_u, n + 1)
                    if e >= 2 and f == 0:
                        act.wait_ge(pe_d, e - 1)
                    act.activation(h_e(e)[:, f, :], banks[4 + n % 2][:, :], ACT.Gelu).then_inc(a_u, 1)
            act.preload_act_table_set(LN_EXP)
            for n in range(B * NT + 1):
                for h in range(2 if n < B * NT else 0):
                    act.wait_ge(pe_pp, 2 * n + h + 1)
                    if n >= 2 and h == 0:
                        act.wait_ge(pe_sc, n - 1)
                    act.activation(pick_t(n)[:, 4 * h:4 * h + 4, :], tiles(banks[h])[:, :, :], ACT.Copy)\
                        .then_inc(a_pp, 1)
                if n and n % NT == 0:
                    b = n // NT - 1
                    rstd(mv0[:, b, :, 1], lv0[:, b, :], rs0[:, b, :], f_mv, NT * (2 * B + b + 1), f_lv, f_rs,
                         2 * B + b + 1)

        @block.vector
        def _(dve):
            def stats(src, bn, mv, s_bn, s_mv, n):
                for t in range(NT):
                    dve.bn_stats(bn[:, t, :], src[:, t, :]).then_inc(s_bn, 1)
                for t in range(NT):
                    dve.wait_ge(s_bn, NT * (n - 1) + t + 1)
                    dve.bn_aggr(mv[:, t, :], bn[:, t, :]).then_inc(s_mv, 1)

            def normalise(dst, src, mv, rs, s_rs, s_z, n):
                dve.wait_ge(s_rs, n)
                for t in range(NT):
                    dve.tensor_scalar(dst[:, t, :], src[:, t, :], mv[:, t, 0:1], rs[:, t:t + 1],
                                      ALU.subtract, ALU.mult).then_inc(s_z, 1)

            for b in range(B):
                dve.wait_ge(ld_x[b], 16)
                stats(x_in[:, b], bn0[:, b], mv0[:, b], d_bn, d_mv, b + 1)
            for b in range(B):
                normalise(z0[:, b], x_in[:, b], mv0[:, b], rs0[:, b], d_rs, d_z, b + 1)
            dve.wait_ge(ld_c0, 16)
            dve.tensor_scalar(bka_s[:, :], cols0[:, 4:5], float(D) ** -0.5, None, ALU.mult).then_inc(v_bka, 1)
            dve.wait_ge(ld_w0, 16)
            dve.tensor_scalar(w0_sign[:, :], w0[:, 3, :], 0.0, 2.0, ALU.is_ge, ALU.mult).then_inc(v_sgn, 1)
            dve.wait_ge(v_sgn, 1)
            dve.tensor_scalar(w0_sign[:, :], w0_sign[:, :], -1.0, None, ALU.add).then_inc(v_sgn, 1)
            for b in range(B):
                dve.wait_ge(p_a, B + 2 * b + 2)
                dve.tensor_scalar(vals0[:, b, :], banks[b][:, :], cols0[:, 3:4], None, ALU.add)\
                    .then_inc(v_val, 1)
            dve.wait_ge(c_set, 3)
            for b in range(B):
                dve.wait_ge(a_ew, b + 1)
                dve.tensor_tensor_scan(cum0[:, b], one_row, kw0[:, b], 0.0, ALU.mult, ALU.add)\
                    .then_inc(v_cum, 1)
            for b in range(B):
                dve.wait_ge(a_lc, b + 1)
                dve.tensor_tensor(ka0[:, b], ka0[:, b], cum0[:, b], ALU.subtract).then_inc(v_t, 1)
            for b in range(B):
                dve.wait_ge(g_pk, b + 1)
                dve.tensor_tensor_scan(cum0[:, b], one_row, kw0[:, b], 0.0, ALU.mult, ALU.add)\
                    .then_inc(v_pool, 1)
            for b in range(B):
                dve.wait_ge(p_a, 4 * B + b + 1)
                dve.tensor_tensor(x_in[:, b, :, :], tiles(banks[b]), x_in[:, b, :, :], ALU.add).then_inc(v_y, 1)
                dve.wait_ge(v_y, b + 1)
                stats(x_in[:, b], bn0[:, b], mv0[:, b], d_bn, d_mv, B + b + 1)
            for b in range(B):
                normalise(res[:, b], x_in[:, b], mv0[:, b], rs0[:, b], d_rs, d_z, B + b + 1)
            dve.wait_ge(ld_r0, 32)
            for b in range(B):
                dve.wait_ge(p_a, 6 * B + b + 1)
                dve.tensor_tensor(x_in[:, b, :, :], tiles(banks[b]), over_tiles(rows0[:, 0, :]), ALU.mult)\
                    .then_inc(v_sc, 1)
            for b in range(B):
                dve.wait_ge(g_bi, b + 1)
                dve.tensor_scalar(x_in[:, b, :, :], x_in[:, b, :, :], -MAX_VAL, MAX_VAL, ALU.max, ALU.min)\
                    .then_inc(v_cl, 1)
                dve.wait_ge(v_cl, b + 1)
                dve.tensor_tensor(x_in[:, b, :, :], x_in[:, b, :, :], res[:, b, :, :], ALU.add)\
                    .then_inc(v_y, 1)
                dve.wait_ge(v_y, B + b + 1)
                stats(x_in[:, b], bn0[:, b], mv0[:, b], d_bn, d_mv, 2 * B + b + 1)
            for b in range(B):
                normalise(x2[:, b], x_in[:, b], mv0[:, b], rs0[:, b], d_rs, d_z, 2 * B + b + 1)

            def norm1(l, b):
                m = unit(l, b)
                dve.wait_ge(pe_wo, m + 1)
                dve.wait_ge(s_res, m + 1)
                dve.tensor_tensor(y1[:, :, :], tiles(bank_tm), res[:, b, :, :], ALU.add).then_inc(s_y1, 1)
                dve.wait_ge(s_y1, m + 1)
                stats(y1, bn1, mv1, s_bn1, s_mv1, m + 1)
                if m:
                    dve.wait_ge(s_r1m, m)
                normalise(z1, y1, mv1, rs1, s_rs1, s_z1, m + 1)

            def feature_map(l, b):
                u = unit(l, b)
                if b == 0:
                    dve.wait_ge(ld_a, 48 * (l + 1))
                dve.wait_ge(s_qe, u + 1)
                dve.tensor_scalar(q_lin[:, :], bank_q[:, :], cols_a[:, 0:1], 0.0, ALU.add, ALU.max)\
                    .then_inc(s_ql, 1)
                dve.wait_ge(s_ke, u + 1)
                dve.tensor_scalar(k_lin[:, :], bank_k[:, :], cols_a[:, 1:2], 0.0, ALU.add, ALU.max)\
                    .then_inc(s_kl, 1)
                dve.wait_ge(s_ql, u + 1)
                dve.scalar_tensor_tensor(out=qT[:, :], in0=q_exp[:, :], scalar=1.0, in1=q_lin[:, :],
                                         op0=ALU.min, op1=ALU.add).then_inc(s_q, 1)
                dve.wait_ge(s_kl, u + 1)
                dve.scalar_tensor_tensor(out=kT[:, :], in0=k_exp[:, :], scalar=1.0, in1=k_lin[:, :],
                                         op0=ALU.min, op1=ALU.add).then_inc(s_k, 1)

            def bias_values(l, b):
                u = unit(l, b)
                dve.wait_ge(pe_v, u + 1)
                for r in range(4):
                    q = slice(32 * r, 32 * r + 32)
                    dve.tensor_tensor(v_blk[q, :, r, :], tiles(bank_tm)[q, :, :],
                                      row_v[q, :].unsqueeze(1).broadcast_to([32, NT, 128]), ALU.add)\
                        .then_inc(s_v, 1)

            def spread_keys(l, b):
                u = unit(l, b)
                dve.wait_ge(s_k, u + 1)
                for g in range(4):
                    dve.tensor_scalar(keys_g[:, :, g, :], kT[:, :].rearrange("p (n c) -> p n c", c=C),
                                      same_g[:, g:g + 1], None, ALU.mult).then_inc(s_kg, 1)
                dve.tensor_tensor_scan(k_sum[:, :], one_row, kT[:, :], 0.0, ALU.mult, ALU.add)\
                    .then_inc(s_ks, 1)

            def keys_to_tokens(l, b):
                u = unit(l, b)
                dve.wait_ge(pe_kT, u + 1)
                dve.tensor_copy(keys_tm[:, :, :], tiles(bank_tr)).then_inc(s_ktm, 1)

            def prefix_states(l, b):
                u = unit(l, b)
                dve.wait_ge(pe_kv, u + 1)
                dve.tensor_tensor(kv[:, :, :], bank_kv[:, :].rearrange("p (c n) -> p c n", n=NC),
                                  same_g_wide[:, :, :], ALU.mult).then_inc(s_kv, 1)
                dve.wait_ge(s_kv, u + 1)
                dve.tensor_tensor_scan(state[:, :, :].rearrange("p c n -> p (c n)"),
                                       scan_keep[:, :, :].rearrange("p c n -> p (c n)"),
                                       kv[:, :, :].rearrange("p c n -> p (c n)"),
                                       0.0, ALU.mult, ALU.add).then_inc(s_st, 1)

            def mask_scores(l, b):
                u = unit(l, b)
                for c4 in range(4):
                    dve.wait_ge(pe_s, 4 * u + c4 + 1)
                    dve.tensor_tensor(probs[:, 4 * c4:4 * c4 + 4, :], tiles(bank_s[c4 % 2]),
                                      causal[:, :, :], ALU.mult).then_inc(s_p, 1)
                    for i in range(2):
                        r, g = 2 + (2 * c4 + i) // 4, (2 * c4 + i) % 4
                        spread_values(dve, r, g).then_inc(s_vd, 1)

            def residual_sum2(l, b):
                m = unit(l, b)
                dve.wait_ge(pe_y2, m + 1)
                dve.wait_ge(s_r1, m + 1)
                if m:
                    dve.wait_ge(s_z2, NT * m)
                dve.tensor_tensor(y2[:, :, :], tiles(bank_kv), res1[:, :, :], ALU.add).then_inc(s_y2, 1)

            def norm2(l, b):
                m = unit(l, b)
                dve.wait_ge(s_y2, m + 1)
                stats(y2, bn2, mv2, s_bn2, s_mv2, m + 1)
                if m:
                    dve.wait_ge(s_res, B + m)
                normalise(z2, y2, mv2, rs2, s_rs2, s_z2, m + 1)

            def divide(l, b):
                u = unit(l, b)
                dve.wait_ge(pe_o, u + 1)
                dve.wait_ge(s_inv, u + 1)
                dve.tensor_tensor(attT[:, :], bank_o[:, :], inv_den[:, :], ALU.mult).then_inc(s_att, 1)

            for u in range(UNITS + 2):
                now, before, old = of_unit(u), of_unit(u - 1), of_unit(u - 2)
                if 1 <= u <= UNITS:
                    norm1(*before)
                if u < UNITS:
                    feature_map(*now)
                if u >= 2:
                    residual_sum2(*old)
                if u < UNITS:
                    bias_values(*now)
                    keys_to_tokens(*now)
                    spread_keys(*now)
                    prefix_states(*now)
                    mask_scores(*now)
                if u >= 2:
                    norm2(*old)
                if u < UNITS:
                    divide(*now)

            for b in range(B):
                dve.wait_ge(s_res, UNITS + b + 1)
                stats(res[:, b], bn0[:, b], mv0[:, b], f_bn, f_mv, b + 1)
            for b in range(B):
                normalise(res[:, b], res[:, b], mv0[:, b], rs0[:, b], f_rs, f_z, b + 1)
            for b in range(B):
                dve.wait_ge(f_z, NT * (b + 1))
                dve.tensor_tensor(res[:, b, :, :], res[:, b, :, :], over_tiles(rows0[:, 3, :]), ALU.mult)\
                    .then_inc(f_g, 1)
            for b in range(B):
                dve.wait_ge(f_b, b + 1)
                dve.tensor_tensor(res[:, b, :, :], res[:, b, :, :], x2[:, b, :, :], ALU.add).then_inc(f_y, 1)
                dve.wait_ge(f_y, b + 1)
                stats(res[:, b], bn0[:, b], mv0[:, b], f_bn, f_mv, B + b + 1)
            for b in range(B):
                normalise(x2[:, b], res[:, b], mv0[:, b], rs0[:, b], f_rs, f_z, B + b + 1)

            logits = banks[4][:, 0:B * NT * E].rearrange("p (n e) -> p n e", e=E)
            gate_n = gate_e[:, :, :, :].rearrange("p b t e -> p (b t) e")
            dve.wait_ge(pe_lg, 1)
            dve.tensor_reduce(logits_max[:, :], logits, AX.X, ALU.max).then_inc(m_gate, 1)
            dve.wait_ge(m_gate, 1)
            dve.tensor_tensor(gate_n, logits, logits_max[:, :].unsqueeze(2).broadcast_to([128, B * NT, E]),
                              ALU.subtract).then_inc(m_gate, 1)
            dve.wait_ge(a_gate, 1)
            dve.tensor_reduce(gate_sum[:, :], gate_n, AX.X, ALU.add).then_inc(m_gate, 1)
            dve.wait_ge(m_gate, 3)
            dve.reciprocal(gate_inv[:, :], gate_sum[:, :]).then_inc(m_gate, 1)
            dve.wait_ge(m_gate, 4)
            dve.tensor_tensor(gate_t[:, :, :].rearrange("p t (b e) -> p b t e", b=B), gate_e[:, :, :, :],
                              gate_inv[:, :].rearrange("p (b t) -> p b t", b=B).unsqueeze(3)
                              .broadcast_to([128, B, NT, E]), ALU.mult).then_inc(m_gate, 1)
            dve.wait_ge(pe_gt, 1)
            dve.tensor_copy(rank_a[:, :], banks[5][0:32, :]).then_inc(m_rank, 1)
            for i in range(CAP // 8):
                dve.wait_ge(m_rank, 2 * i + 1)
                dve.max(top8[:, :], rank_a[:, :]).then_inc(m_rank, 1)
                dve.wait_ge(m_rank, 2 * i + 2)
                dve.match_replace(rank_a[:, :], top8[:, :], rank_a[:, :], -1.0).then_inc(m_rank, 1)
            dve.wait_ge(m_rank, 33)
            dve.tensor_scalar(rank_a[:, :], rank_a[:, :], 0.0, None, ALU.is_lt).then_inc(m_rank, 1)
            dve.wait_ge(m_rank, 34)
            dve.tensor_tensor_scan(rank_b[:, :], one_row[0:32], rank_a[:, :], 0.0, ALU.mult, ALU.add)\
                .then_inc(m_rank, 1)
            dve.wait_ge(m_rank, 35)
            dve.tensor_tensor(rank_b[:, :], rank_b[:, :], rank_a[:, :], ALU.mult).then_inc(m_rank, 1)
            dve.wait_ge(pe_pt, 1)
            dve.tensor_scalar(pos_tm[:, :, :].rearrange("p t n -> p (t n)"), banks[6][:, 0:NT * 32], -1.0,
                              None, ALU.add).then_inc(m_pos, 1)
            dve.wait_ge(m_pos, 1)
            for n in range(B * NT):
                b, t = n // NT, n % NT
                if n >= 4:
                    dve.wait_ge(pe_g, n - 3)
                for e in range(E):
                    k = b * E + e
                    ins = dve.tensor_scalar(pick[n % 4][:, e // 4, (e % 4) * 128:(e % 4 + 1) * 128],
                                            slot_row[:, :], pos_tm[:, t, k:k + 1], None, ALU.is_equal)
                ins.then_inc(m_pick, 1)
                if t == NT - 1:
                    gathered(dve, b)
            for e in range(E):
                dve.wait_ge(pe_d, e + 1)
                dve.tensor_copy(ye(e), tiles(banks[6 + e % 2])).then_inc(m_d, 1)
                if e < 4:
                    weighted(dve, e)
            for n in range(B * NT + 1):
                if 4 <= n < B * NT:
                    weighted(dve, n)
                if n:
                    k = n - 1
                    b, t = k // NT, k % NT
                    dve.wait_ge(pe_sc, k + 1)
                    dve.tensor_tensor(res[:, b, t, :], banks[2 + k % 2][:, 0:128], x2[:, b, t, :], ALU.add)\
                        .then_inc(m_sc, 1)
                    if t == NT - 1:
                        dve.wait_ge(m_sc, k + 1)
                        stats(res[:, b], bn0[:, b], mv0[:, b], f_bn, f_mv, 2 * B + b + 1)
                        normalise(res[:, b], res[:, b], mv0[:, b], rs0[:, b], f_rs, f_z, 2 * B + b + 1)


        @block.gpsimd
        def _(pool):
            pool.memset(ln_eps[:, :], LN_EPS).then_inc(c_set, 1)
            pool.memset(att_eps[:, :], ATT_EPS).then_inc(c_set, 1)
            pool.memset(ones[:, :], 1.0).then_inc(c_set, 1)
            pool.wait_ge(c_set, 3)
            pool.affine_select(out=ident[:, :], in_=ones[:, :], compare_op=ALU.is_equal, fill=0.0, base=0,
                               pattern=[[-1, 128]], channel_multiplier=1).then_inc(c_done, 1)
            pool.affine_select(out=same_head[:, :], in_=ones[:, :], compare_op=ALU.is_ge, fill=0.0, base=0,
                               pattern=[[-HD, HEADS], [0, HD]], channel_multiplier=1).then_inc(c_sel, 1)
            pool.memset(causal[:, :, :], 1.0).then_inc(c_sel, 1)
            pool.memset(scan_keep[:, :, :], 1.0).then_inc(c_sel, 1)
            pool.iota(slot_int[:, :], pattern=[[1, 128]], base=0, channel_multiplier=0).then_inc(c_sel, 1)
            pool.wait_ge(c_sel, 4)
            pool.affine_select(out=same_head[:, :], in_=same_head[:, :], compare_op=ALU.is_ge, fill=0.0,
                               base=HD - 1, pattern=[[HD, HEADS], [0, HD]], channel_multiplier=-1)\
                .then_inc(c_sel, 1)
            pool.memset(scan_keep[:, :, 0:1], 0.0).then_inc(c_sel, 1)
            pool.tensor_copy(slot_row[:, :], slot_int[:, :]).then_inc(c_sel, 1)
            for j in range(Q4):
                q = slice(32 * j, 32 * j + 32)
                pool.wait_ge(c_sel, 7 + 3 * j)
                pool.affine_select(out=same_g[q, :], in_=ones[q, 0:4], compare_op=ALU.is_ge, fill=0.0, base=0,
                                   pattern=[[-HD, 4]], channel_multiplier=1).then_inc(c_sel, 1)
                pool.wait_ge(c_sel, 8 + 3 * j)
                pool.affine_select(out=same_g[q, :], in_=same_g[q, :], compare_op=ALU.is_ge, fill=0.0,
                                   base=HD - 1, pattern=[[HD, 4]], channel_multiplier=-1).then_inc(c_sel, 1)
                pool.wait_ge(c_sel, 9 + 3 * j)
                pool.affine_select(out=causal[q, :, :], in_=causal[q, :, :], compare_op=ALU.is_ge, fill=0.0,
                                   base=0, pattern=[[0, 4], [0, 4], [1, C]], channel_multiplier=-1)\
                    .then_inc(c_sel, 1)
            pool.wait_ge(c_sel, 19)
            pool.tensor_copy(same_g_wide[:, :, :].rearrange("p (g d) n -> p g (d n)", g=4),
                             same_g[:, :].unsqueeze(2).broadcast_to([128, 4, HD * NC])).then_inc(c_sel, 1)
            pool.memset(queries_j[:, :, :, :], 0.0).then_inc(c_wide, 1)
            pool.memset(values_g[:, :, :, :, :], 0.0).then_inc(c_wide, 1)
            pool.memset(v_blk[:, :, :, :], 0.0).then_inc(c_wide, 1)
            pool.wait_ge(p_a, B)
            pool.wait_ge(c_sel, 20)
            pool.memset(state_blk[:, :, :], 0.0).then_inc(c_wide, 1)

            for b in range(B):
                pool.wait_ge(a_kw, b + 1)
                pool.tensor_tensor(kw0[:, b], kw0[:, b], keys0[:, b, :], ALU.mult).then_inc(g_pk, 1)
            for b in range(B):
                pool.wait_ge(v_pool, b + 1)
                pool.wait_ge(v_val, b + 1)
                pool.tensor_tensor(ka0[:, b], cum0[:, b], vals0[:, b, :], ALU.mult).then_inc(g_prod, 1)
            pool.wait_ge(ld_r0, 32)
            for b in range(B):
                pool.wait_ge(v_sc, b + 1)
                pool.tensor_tensor(x_in[:, b], x_in[:, b], over_tiles(rows0[:, 1, :]), ALU.add).then_inc(g_bi, 1)
            for b in range(B):
                pool.wait_ge(d_z, NT * (2 * B + b + 1))
                pool.tensor_tensor(res[:, b], x2[:, b], over_tiles(rows0[:, 2, :]), ALU.add).then_inc(s_res, 1)

            def residual1(l, b):
                m = unit(l, b)
                if m + 1 < UNITS:
                    pool.wait_ge(s_vg, 8 * (m + 2))
                if b == 0:
                    pool.wait_ge(ld_1, 48 * (l + 1))
                    pool.tensor_tensor(shift_1[:, :], rows_1[:, 1, :], rows_1[:, 2, :], ALU.add).then_inc(s_sh1, 1)
                pool.wait_ge(s_z1, NT * (m + 1))
                if m:
                    pool.wait_ge(s_y2, m)
                pool.tensor_tensor(res1[:, :, :], z1[:, :, :], over_tiles(rows_1[:, 0, :]), ALU.mult)\
                    .then_inc(s_r1m, 1)
                pool.wait_ge(s_r1m, m + 1)
                pool.wait_ge(s_sh1, l + 1)
                pool.tensor_tensor(res1[:, :, :], res1[:, :, :], over_tiles(shift_1[:, :]), ALU.add)\
                    .then_inc(s_r1, 1)

            def weigh_key_sums(l, b):
                u = unit(l, b)
                pool.wait_ge(s_ks, u + 1)
                pool.wait_ge(s_q, u + 1)
                pool.wait_ge(s_vg, 8 * (u + 1))
                pool.tensor_tensor(qk_sum[:, :], qT[:, :], k_sum[:, :], ALU.mult).then_inc(s_qk, 1)

            def spread_first_values(l, b):
                u = unit(l, b)
                pool.wait_ge(s_v, 4 * (u + 1))
                for k in range(8):
                    if k:
                        pool.wait_ge(s_vg, 8 * u + k)
                    spread_values(pool, k // 4, k % 4).then_inc(s_vg, 1)

            def residual2(l, b):
                m = unit(l, b)
                if b == 0:
                    pool.wait_ge(ld_2v, 32 * (l + 1))
                    pool.tensor_tensor(shift_2[:, :], rows_2[:, 1, :], rows_2[:, 2, :], ALU.add).then_inc(s_sh2, 1)
                pool.wait_ge(s_z2, NT * (m + 1))
                pool.tensor_tensor(res[:, b], z2[:, :, :], over_tiles(rows_2[:, 0, :]), ALU.mult)\
                    .then_inc(s_r2m, 1)
                pool.wait_ge(s_r2m, m + 1)
                pool.wait_ge(s_sh2, l + 1)
                pool.tensor_tensor(res[:, b], res[:, b], over_tiles(shift_2[:, :]), ALU.add).then_inc(s_res, 1)

            for u in range(UNITS + 2):
                if u < UNITS:
                    spread_first_values(*of_unit(u))
                    weigh_key_sums(*of_unit(u))
                if 1 <= u <= UNITS:
                    residual1(*of_unit(u - 1))
                if u >= 2:
                    residual2(*of_unit(u - 2))
            for b in range(B):
                pool.wait_ge(f_g, b + 1)
                pool.tensor_tensor(res[:, b], res[:, b], over_tiles(rows0[:, 4, :]), ALU.add).then_inc(f_b, 1)


def kernel(**inputs):
    import numpy as np
    import concourse.bacc as bacc
    from concourse import mybir as mb
    from concourse.bass_utils import run_bass_kernel_spmd

    x = {k: np.asarray(v) for k, v in inputs.items()}
    at = {k[8:]: v for k, v in x.items() if k.startswith("L1_attn_")}
    l0 = {k[8:]: v for k, v in x.items() if k.startswith("L0_attn_")}
    b1 = at["b1"].reshape(L, NF, 128).transpose(0, 2, 1)
    no_bias = np.zeros_like(at["bo"][:1])
    packed = {
        "x": l0["hidden_states"],
        "cols0": np.stack([l0["gamma"], l0["beta"], l0["bk"], l0["bv"], l0["bka"]], axis=1),
        "w0": np.stack([l0["Wk"].T, l0["Wv"].T, l0["Wka"].T, x["L0_ffn_weights"].T]),
        "rows0": np.stack([x["L0_ffn_scale"], x["L0_ffn_bias"], at["bo"][0], at["gf"], at["bef"]]),
        "w_qkv": np.stack([at["Wq"], at["Wk"], at["Wv"]], axis=1),
        "cols_a": np.stack([at["bq"], at["bk"]], axis=2),
        "row_v": at["bv"],
        "w_o": at["Wo"],
        "w_1": at["W1"],
        "w_2": at["W2"],
        "cols_1": np.concatenate([at["g1"][:, :, None], at["be1"][:, :, None], b1], axis=2),
        "rows_1": np.stack([at["g1"], at["be1"], at["b2"]], axis=1),
        "cols_2": np.stack([at["g2"], at["be2"]], axis=2),
        "rows_2": np.stack([at["g2"], at["be2"], np.concatenate([at["bo"][1:], no_bias])], axis=1),
        "gate_w": x["L1_ffn_gate_w"],
        "we_1": x["L1_ffn_w1"],
        "we_2": x["L1_ffn_w2"],
    }
    nc = bacc.Bacc("TRN2", target_bir_lowering=False, num_devices=1)
    arrays, args = {}, {}
    for name, v in packed.items():
        v = np.ascontiguousarray(v)
        arrays[f"in_{name}"] = v
        args[name] = nc.dram_tensor(f"in_{name}", v.shape, mb.dt.from_np(v.dtype), kind="ExternalInput").ap()
    out = nc.dram_tensor("out", (B, S, D), mb.dt.float32, kind="ExternalOutput").ap()
    build(nc, args, out)
    r = run_bass_kernel_spmd(nc, [arrays], core_ids=[0])
    return r.results[0]["out"]
```

```python
import concourse.bass as bass
from concourse import mybir
from contextlib import ExitStack

D = 128
B = 4
S = 512
NT = S // 128
L = 4
FF = 512
NF = FF // 128
HEADS = 16
HD = D // HEADS
Q4 = 4
C = 32
NC = S // C
E = 8
CAP = 2 * S // E
LN_EPS = 1e-5
ATT_EPS = 1e-6
MAX_VAL = 100.0
UNITS = L * B
PARTS = 3
RING = 8
LN_EXP = "natural_log_exp_and_others"


def build(nc, a, out):
    f32 = mybir.dt.float32
    i32 = mybir.dt.int32
    bf16 = mybir.dt.bfloat16
    ALU = mybir.AluOpType
    ACT = mybir.ActivationFunctionType
    AX = mybir.AxisListType

    ctx = ExitStack()
    with ctx:
        def sb(name, shape, dt=f32):
            return ctx.enter_context(nc.sbuf_tensor(name, shape, dt))

        def pb(name):
            return ctx.enter_context(nc.psum_tensor(name, [128, 512], f32))

        def sem(name):
            return ctx.enter_context(nc.semaphore(name))

        ident = sb("ident", [128, 128])
        ident_bf = sb("ident_bf", [128, 128], bf16)
        ones = sb("ones", [128, 128])
        causal = sb("causal", [128, 4, 128])
        same_g = sb("same_g", [128, 4])
        same_g_wide = sb("same_g_wide", [128, C, NC])
        scan_keep = sb("scan_keep", [128, C, NC])
        of_head = sb("of_head", [128, HEADS])
        slot_row = sb("slot_row", [128, 128])
        slot_int = sb("slot_int", [128, 128], i32)
        ln_eps = sb("ln_eps", [128, 1])

        w0 = sb("w0", [128, 4, 128])
        w0_sign = sb("w0_sign", [128, 128])
        cols0 = sb("cols0", [128, 5])
        bka_s = sb("bka_s", [128, 1])
        rows0 = sb("rows0", [128, 5, 128])
        w_qkv = sb("w_qkv", [128, 3, 128])
        w_o = sb("w_o", [128, 128])
        w_1 = sb("w_1", [128, FF])
        w_2 = sb("w_2", [128, NF, 128])
        cols_a = sb("cols_a", [128, 2])
        row_v = sb("row_v", [128, 128])
        cols_1 = sb("cols_1", [128, 2 + NF])
        rows_1 = sb("rows_1", [128, 3, 128])
        cols_2 = sb("cols_2", [128, 2])
        rows_2 = sb("rows_2", [128, 3, 128])
        shift_1 = sb("shift_1", [128, 128])
        shift_2 = sb("shift_2", [128, 128])
        gate_w = sb("gate_w", [128, E])
        we_1 = sb("we_1", [128, E, FF])
        we_2 = sb("we_2", [128, E, NF, 128])

        xT = sb("xT", [128, B, S])
        res = sb("res", [128, B, NT, 128])
        x2 = sb("x2", [128, B, NT, 128])

        qT = sb("qT", [128, S])
        kT = sb("kT", [128, S])
        q_exp = sb("q_exp", [128, S])
        k_exp = sb("k_exp", [128, S])
        q_lin = sb("q_lin", [128, S])
        k_lin = sb("k_lin", [128, S])
        keys_g = sb("keys_g", [128, NC, 4, C])
        queries_j = sb("queries_j", [128, NC, 4, C])
        values_g = sb("values_g", [128, NC, 4, 4, HD])
        keys_tm = sb("keys_tm", [128, NT, 128])
        v_tm = sb("v_tm", [128, NT, 128])
        v_blk = sb("v_blk", [128, NT, 4, 128])
        probs = sb("probs", [128, NC, 128])
        kv = sb("kv", [128, C, NC])
        state = sb("state", [128, C, NC])
        state_blk = sb("state_blk", [128, NC, 128])
        k_sum = sb("k_sum", [128, S])
        qk_sum = sb("qk_sum", [128, S])
        den = sb("den", [128, NT * HEADS])
        inv_den = sb("inv_den", [128, NT * HEADS])
        att = sb("att", [128, NT, 128])
        attT = sb("attT", [128, S])
        y1 = sb("y1", [128, NT, 128])
        z1 = sb("z1", [128, NT, 128])
        x1T = sb("x1T", [128, S])
        res1 = sb("res1", [128, NT, 128])
        hidden = sb("hidden", [128, NF, S])
        y2 = sb("y2", [128, NT, 128])
        z2 = sb("z2", [128, NT, 128])
        bn1 = sb("bn1", [128, NT, 6])
        mv1 = sb("mv1", [128, NT, 2])
        lv1 = sb("lv1", [128, NT])
        rs1 = sb("rs1", [128, NT])
        bn2 = sb("bn2", [128, NT, 6])
        mv2 = sb("mv2", [128, NT, 2])
        lv2 = sb("lv2", [128, NT])
        rs2 = sb("rs2", [128, NT])
        bn0 = sb("bn0", [128, B, NT, 6])
        mv0 = sb("mv0", [128, B, NT, 2])
        lv0 = sb("lv0", [128, B, NT])
        rs0 = sb("rs0", [128, B, NT])
        logits_max = sb("logits_max", [128, B * NT])
        gate_e = sb("gate_e", [128, B, NT, E])
        gate_sum = sb("gate_sum", [128, B * NT])
        gate_inv = sb("gate_inv", [128, B * NT])
        gate_p = sb("gate_p", [128, B, NT, E])
        gate_t = sb("gate_t", [128, NT, B * E])
        pos_tm = sb("pos_tm", [128, NT, B * E])
        gate_parts = sb("gate_parts", [128, PARTS, NT * B * E], bf16)
        gate_rest = sb("gate_rest", [128, NT * B * E])
        slot_gate = sb("slot_gate", [128, B * E])
        top8 = sb("top8", [32, 8])
        rank_a = sb("rank_a", [32, S])
        rank_b = sb("rank_b", [32, S])

        x_in = probs[:, :, :].rearrange("p (b t) d -> p b t d", b=B)
        z0 = state_blk[:, :, :].rearrange("p (b t) d -> p b t d", b=B)
        hT = keys_g[:, :, :, :].rearrange("p (b n) g c -> p b (n g c)", b=B)
        keys0 = hidden
        vals0 = we_1[:, 0:4, :]
        ka0 = we_1[:, 4:8, :]
        cum0 = we_2[:, 0:4, :, :].rearrange("p a f d -> p a (f d)")
        kw0 = we_2[:, 4:8, :, :].rearrange("p a f d -> p a (f d)")
        def flat_bf(t, dims):
            return t.rearrange(dims).bitcast(bf16)

        pick = [flat_bf(t[:, :, :, :], "p n g c -> p (n g c)").rearrange("p (k x) -> p k x", k=RING // 2)[:, i, :]
                for t in (keys_g, queries_j) for i in range(RING // 2)]
        pick_t = [t[:, :].bitcast(bf16) for t in (qT, kT, q_exp, k_exp, q_lin, k_lin, k_sum, qk_sum, attT)] \
            + [flat_bf(t[:, :, :], "p t d -> p (t d)") for t in (keys_tm, v_tm, kv, state, att, y1, z1)]
        pick_t = [t.rearrange("p (e k) -> p e k", e=E) for t in pick_t]
        x_rest = res
        x_parts = [flat_bf(values_g[:, :, :, :, :], "p n j g e -> p (n j g e)")[:, i * B * S:(i + 1) * B * S]
                   for i in range(2)] + [flat_bf(xT[:, :, :], "p b s -> p (b s)")[:, 0:B * S]]
        x_parts = [t.rearrange("p (b t d) -> p b t d", b=B, t=NT) for t in x_parts]
        y_all = [x1T[:, :].rearrange("p (b d) -> p b d", b=B), res1[:, :, :]]
        y_rest = y2
        y_parts = flat_bf(queries_j[:, :, :, :], "p n g c -> p (n g c)")[:, 0:2 * PARTS * S]\
            .rearrange("p (r i b d) -> p r i b d", r=2, i=PARTS, b=B)
        xg_a = [t[:, :, :] for t in (probs, state_blk)]

        bank_q = pb("bank_q")
        bank_k = pb("bank_k")
        bank_tm = pb("bank_tm")
        bank_tr = pb("bank_tr")
        bank_kv = pb("bank_kv")
        bank_s = [pb("bank_s0"), pb("bank_s1")]
        bank_o = pb("bank_o")
        banks = [bank_q, bank_k, bank_tm, bank_tr, bank_kv, bank_s[0], bank_s[1], bank_o]

        def tiles(bank):
            return bank[:, :].rearrange("p (t d) -> p t d", d=128)

        def over_tiles(row):
            return row.unsqueeze(1).broadcast_to([128, NT, 128])

        ld_x = [sem(f"ld_x{b}") for b in range(B)]
        ld_w0 = sem("ld_w0")
        ld_c0 = sem("ld_c0")
        ld_r0 = sem("ld_r0")
        ld_a = sem("ld_a")
        ld_o = sem("ld_o")
        ld_1 = sem("ld_1")
        ld_2 = sem("ld_2")
        ld_2v = sem("ld_2v")
        ld_e = sem("ld_e")
        st_out = sem("st_out")
        c_set = sem("c_set")
        c_sel = sem("c_sel")
        c_done = sem("c_done")
        c_wide = sem("c_wide")
        d_bn = sem("d_bn")
        d_mv = sem("d_mv")
        d_lv = sem("d_lv")
        d_rs = sem("d_rs")
        d_z = sem("d_z")
        p_a = sem("p_a")
        a_hT = sem("a_hT")
        a_key = sem("a_key")
        v_val = sem("v_val")
        v_bka = sem("v_bka")
        v_sgn = sem("v_sgn")
        a_ka = sem("a_ka")
        a_ew = sem("a_ew")
        v_cum = sem("v_cum")
        a_lc = sem("a_lc")
        v_t = sem("v_t")
        a_kw = sem("a_kw")
        g_pk = sem("g_pk")
        v_pool = sem("v_pool")
        g_prod = sem("g_prod")
        v_y = sem("v_y")
        a_x1T = sem("a_x1T")
        v_sc = sem("v_sc")
        g_bi = sem("g_bi")
        v_cl = sem("v_cl")
        pe_q = sem("pe_q")
        pe_k = sem("pe_k")
        pe_v = sem("pe_v")
        pe_z1T = sem("pe_z1T")
        pe_h = sem("pe_h")
        pe_kT = sem("pe_kT")
        pe_kv = sem("pe_kv")
        pe_s = sem("pe_s")
        pe_den = sem("pe_den")
        pe_y2 = sem("pe_y2")
        pe_o = sem("pe_o")
        pe_z2T = sem("pe_z2T")
        pe_aT = sem("pe_aT")
        pe_wo = sem("pe_wo")
        s_qe = sem("s_qe")
        s_ke = sem("s_ke")
        s_lv1 = sem("s_lv1")
        s_rs1 = sem("s_rs1")
        s_lv2 = sem("s_lv2")
        s_rs2 = sem("s_rs2")
        s_x1T = sem("s_x1T")
        s_h = sem("s_h")
        s_qj = sem("s_qj")
        s_ktm = sem("s_ktm")
        s_sblk = sem("s_sblk")
        s_aT = sem("s_aT")
        s_xT = sem("s_xT")
        s_y1 = sem("s_y1")
        s_bn1 = sem("s_bn1")
        s_mv1 = sem("s_mv1")
        s_z1 = sem("s_z1")
        s_ql = sem("s_ql")
        s_kl = sem("s_kl")
        s_q = sem("s_q")
        s_k = sem("s_k")
        s_v = sem("s_v")
        s_kg = sem("s_kg")
        s_ks = sem("s_ks")
        s_kv = sem("s_kv")
        s_st = sem("s_st")
        s_p = sem("s_p")
        s_y2 = sem("s_y2")
        s_bn2 = sem("s_bn2")
        s_mv2 = sem("s_mv2")
        s_z2 = sem("s_z2")
        s_den = sem("s_den")
        s_inv = sem("s_inv")
        s_att = sem("s_att")
        s_sh1 = sem("s_sh1")
        s_sh2 = sem("s_sh2")
        s_r1m = sem("s_r1m")
        s_r1 = sem("s_r1")
        s_r2m = sem("s_r2m")
        s_res = sem("s_res")
        s_vg = sem("s_vg")
        s_vb = sem("s_vb")
        s_vd = sem("s_vd")
        s_qk = sem("s_qk")
        f_bn = sem("f_bn")
        f_mv = sem("f_mv")
        f_lv = sem("f_lv")
        f_rs = sem("f_rs")
        f_z = sem("f_z")
        f_g = sem("f_g")
        f_b = sem("f_b")
        f_y = sem("f_y")
        pe_x3 = sem("pe_x3")
        a_x3 = sem("a_x3")
        pe_lg = sem("pe_lg")
        m_gate = sem("m_gate")
        a_gate = sem("a_gate")
        pe_gt = sem("pe_gt")
        m_rank = sem("m_rank")
        pe_pt = sem("pe_pt")
        m_pos = sem("m_pos")
        m_pick = sem("m_pick")
        pe_g = sem("pe_g")
        m_xg = sem("m_xg")
        pe_u = sem("pe_u")
        a_u = sem("a_u")
        pe_d = sem("pe_d")
        a_xh = sem("a_xh")
        g_xr = sem("g_xr")
        a_xm = sem("a_xm")
        g_xl = sem("g_xl")
        pe_pick = sem("pe_pick")
        a_pt = sem("a_pt")
        m_gs = sem("m_gs")
        m_y = sem("m_y")
        m_yh = sem("m_yh")
        m_yr = sem("m_yr")
        m_ym = sem("m_ym")
        m_yl = sem("m_yl")
        pe_sc = sem("pe_sc")
        m_sc = sem("m_sc")

        block = ctx.enter_context(nc.Block())

        def unit(l, b):
            return l * B + b

        def of_unit(u):
            return u // B, u % B

        def rows_of(ap):
            return ap.unsqueeze(0).broadcast_to([128] + list(ap.shape))

        one_row = ones[:, 0:1].broadcast_to([128, S])

        def xg(e):
            return xg_a[e // 4][:, 4 * (e % 4):4 * (e % 4) + 4, :]

        def spread_values(eng, r, g):
            src = v_tm[32 * r:32 * r + 32, :, :].rearrange("p t (j g d) -> p t j g d", j=4, g=4)
            dst = values_g[32 * g:32 * g + 32, :, :, :, :].rearrange("p (t r) j g d -> p t r j g d", r=4)
            return eng.tensor_copy(dst[:, :, r, :, g, :], src[:, :, :, g, :])

        gate_flat = gate_t[:, :, :].rearrange("p t k -> p (t k)")

        def h_e(e):
            return hidden if e % 2 == 0 else he_b

        he_b = v_blk[:, :, :, :].rearrange("p t c d -> p t (c d)")

        @block.sync
        def _(sp):
            x_v = a["x"].rearrange("b (t p) d -> b p t d", p=128)
            for b in range(B):
                sp.dma_start(x_in[:, b, :, :], x_v[b]).then_inc(ld_x[b], 16)
                if b == 0:
                    sp.dma_start(cols0[:, :], a["cols0"]).then_inc(ld_c0, 16)
                    sp.dma_start(w0[:, :, :], a["w0"].rearrange("n i o -> i n o")).then_inc(ld_w0, 16)
            sp.dma_start(rows0[:, :, :], rows_of(a["rows0"])).then_inc(ld_r0, 16)
            sp.dma_start(gate_w[:, :], a["gate_w"]).then_inc(ld_r0, 16)
            for l in range(L):
                if l:
                    sp.wait_ge(s_v, unit(l, 0))
                    sp.wait_ge(s_ke, unit(l, 0))
                sp.dma_start(w_qkv[:, :, :], a["w_qkv"][l].rearrange("n i o -> i n o")).then_inc(ld_a, 16)
                sp.dma_start(cols_a[:, :], a["cols_a"][l]).then_inc(ld_a, 16)
                sp.dma_start(row_v[:, :], rows_of(a["row_v"][l])).then_inc(ld_a, 16)
                if l:
                    sp.wait_ge(pe_wo, unit(l, 0))
                sp.dma_start(w_o[:, :], a["w_o"][l]).then_inc(ld_o, 16)
                if l:
                    sp.wait_ge(s_h, NF * unit(l, 0))
                    sp.wait_ge(s_sh1, l)
                    sp.wait_ge(s_r1, unit(l, 0))
                sp.dma_start(w_1[:, :], a["w_1"][l]).then_inc(ld_1, 16)
                sp.dma_start(cols_1[:, :], a["cols_1"][l]).then_inc(ld_1, 16)
                sp.dma_start(rows_1[:, :, :], rows_of(a["rows_1"][l])).then_inc(ld_1, 16)
                if l:
                    sp.wait_ge(pe_y2, unit(l, 0))
                sp.dma_start(w_2[:, :, :], a["w_2"][l].rearrange("(f p) d -> p f d", p=128)).then_inc(ld_2, 16)
                if l:
                    sp.wait_ge(s_xT, unit(l + 1, 0))
                    sp.wait_ge(s_res, unit(l + 1, 0))
                sp.dma_start(cols_2[:, :], a["cols_2"][l]).then_inc(ld_2v, 16)
                sp.dma_start(rows_2[:, :, :], rows_of(a["rows_2"][l])).then_inc(ld_2v, 16)
                if l == 0:
                    sp.wait_ge(p_a, 5 * B)
                    sp.dma_start(we_1[:, :, :], a["we_1"].rearrange("e i f -> i e f")).then_inc(ld_e, 16)
                    sp.dma_start(we_2[:, :, :, :],
                                 a["we_2"].rearrange("e (f p) d -> p e f d", p=128)).then_inc(ld_e, 16)
            o_v = out.rearrange("b (t p) d -> b p t d", p=128)
            for n in range(B * NT):
                sp.wait_ge(f_z, NT * 2 * B + n + 1)
                sp.dma_start(o_v[n // NT, :, n % NT, :], res[:, n // NT, n % NT, :]).then_inc(st_out, 16)
            sp.wait_ge(st_out, 16 * B * NT)

        @block.tensor
        def _(pe):
            def transpose4(bank, src):
                for t in range(NT):
                    mm = pe.transpose(bank[:, t * 128:(t + 1) * 128], src[:, t, :], ident[:, :])
                return mm

            pe.wait_ge(c_done, 1)
            for b in range(B):
                pe.wait_ge(d_z, NT * (b + 1))
                transpose4(banks[b], z0[:, b]).then_inc(p_a, 1)
            pe.wait_ge(ld_w0, 16)
            for b in range(B):
                pe.wait_ge(a_hT, b + 1)
                pe.matmul(banks[4 + b][:, :], w0[:, 0, :], hT[:, b], start=True, stop=True).then_inc(p_a, 1)
                pe.matmul(banks[b][:, :], w0[:, 1, :], hT[:, b], start=True, stop=True).then_inc(p_a, 1)
            for b in range(B):
                pe.wait_ge(a_key, b + 1)
                pe.matmul(banks[4 + b][:, :], w0[:, 2, :], keys0[:, b, :], start=True, stop=True)\
                    .then_inc(p_a, 1)
            for b in range(B):
                pe.wait_ge(g_prod, b + 1)
                pe.wait_ge(v_val, b + 1)
                transpose4(banks[b], ka0[:, b].rearrange("p (t d) -> p t d", d=128)).then_inc(p_a, 1)
            for b in range(B):
                pe.wait_ge(d_z, NT * (B + b + 1))
                pe.wait_ge(a_ka, b + 1)
                transpose4(banks[4 + b], res[:, b]).then_inc(p_a, 1)
            pe.wait_ge(v_sgn, 2)
            for b in range(B):
                pe.wait_ge(a_x1T, b + 1)
                for t in range(NT):
                    mm = pe.matmul(banks[b][:, t * 128:(t + 1) * 128], xT[:, b, t * 128:(t + 1) * 128],
                                   w0_sign[:, :], start=True, stop=True)
                mm.then_inc(p_a, 1)
            for b in range(B):
                pe.wait_ge(d_z, NT * (2 * B + b + 1))
                transpose4(banks[4 + b], x2[:, b]).then_inc(p_a, 1)

            def project_queries_keys(l, b):
                u = unit(l, b)
                if b == 0:
                    pe.wait_ge(ld_a, 48 * (l + 1))
                pe.wait_ge(s_xT, u + 1)
                if u:
                    pe.wait_ge(s_aT, u)
                pe.matmul(bank_q[:, :], w_qkv[:, 0, :], xT[:, b, :], start=True, stop=True).then_inc(pe_q, 1)
                if u:
                    pe.wait_ge(s_kl, u)
                pe.matmul(bank_k[:, :], w_qkv[:, 1, :], xT[:, b, :], start=True, stop=True).then_inc(pe_k, 1)

            def project_values(l, b):
                u = unit(l, b)
                if u:
                    pe.wait_ge(s_den, u)
                for t in range(NT):
                    mm = pe.matmul(bank_kv[:, t * 128:(t + 1) * 128], xT[:, b, t * 128:(t + 1) * 128],
                                   w_qkv[:, 2, :], start=True, stop=True)
                mm.then_inc(pe_v, 1)

            def keys_to_tokens(l, b):
                u = unit(l, b)
                pe.wait_ge(s_k, u + 1)
                if u:
                    pe.wait_ge(s_x1T, u)
                transpose4(bank_tr, kT[:, :].rearrange("p (t d) -> p t d", d=128)).then_inc(pe_kT, 1)

            def norm1_to_features(l, b):
                m = unit(l, b)
                pe.wait_ge(s_z1, NT * (m + 1))
                if 2 <= m <= UNITS - B + 1:
                    pe.wait_ge(s_xT, B + m - 1)
                elif m > UNITS - B + 1:
                    pe.wait_ge(s_ktm, m + 1)
                transpose4(bank_tr, z1).then_inc(pe_z1T, 1)

            def mlp_up(l, b, other):
                m = unit(l, b)
                if b == 0:
                    pe.wait_ge(ld_1, 48 * (l + 1))
                pe.wait_ge(s_x1T, m + 1)
                for f in range(NF):
                    if f < 2:
                        pe.wait_ge(s_p, 4 * (m + 1))
                    else:
                        pe.wait_ge(s_h, NF * m + f - 1)
                    pe.matmul(bank_s[f % 2][:, :], w_1[:, f * 128:(f + 1) * 128], x1T[:, :],
                              start=True, stop=True).then_inc(pe_h, 1)
                    if f == 1 and other:
                        keys_to_tokens(*other)

            def states(l, b):
                u = unit(l, b)
                pe.wait_ge(s_v, u + 1)
                pe.wait_ge(s_ktm, u + 1)
                pe.wait_ge(s_vb, 4 * (u + 1))
                kv_out = bank_kv[:, :].rearrange("p (c t r) -> p t r c", t=NT, r=4)
                for t in range(NT):
                    for j in range(4):
                        q = slice(32 * j, 32 * j + 32)
                        mm = pe.matmul(kv_out[q, t, :, :], keys_tm[:, t, q], v_blk[:, t, :, q],
                                       start=True, stop=True, skip_group_check=True)
                mm.then_inc(pe_kv, 1)

            def scores(l, b):
                u = unit(l, b)
                pe.wait_ge(s_kg, 4 * (u + 1))
                pe.wait_ge(s_qj, 4 * (u + 1))
                for c4 in range(4):
                    if c4 < 2:
                        if u:
                            pe.wait_ge(s_h, NF * (u - 1) + 3 + c4)
                    else:
                        pe.wait_ge(s_p, 4 * u + c4 - 1)
                    for i in range(4):
                        n = 4 * c4 + i
                        mm = pe.matmul(bank_s[c4 % 2][:, i * 128:(i + 1) * 128], keys_g[:, n, :, :],
                                       queries_j[:, n, :, :], start=True, stop=True)
                    mm.then_inc(pe_s, 1)

            def denominators(l, b):
                u = unit(l, b)
                pe.wait_ge(s_qk, u + 1)
                pe.wait_ge(s_kv, u + 1)
                for t in range(NT):
                    mm = pe.matmul(bank_kv[:, t * HEADS:(t + 1) * HEADS], qk_sum[:, t * 128:(t + 1) * 128],
                                   of_head[:, :], start=True, stop=True)
                mm.then_inc(pe_den, 1)

            def mlp_down(l, b, first, last):
                m = unit(l, b)
                if first == 0:
                    if b == 0:
                        pe.wait_ge(ld_2, 16 * (l + 1))
                    pe.wait_ge(s_h, NF * (m + 1))
                    if m:
                        pe.wait_ge(s_y2, m)
                for t in range(first, last):
                    for f in range(NF):
                        mm = pe.matmul(bank_tm[:, t * 128:(t + 1) * 128], hidden[:, f, t * 128:(t + 1) * 128],
                                       w_2[:, f, :], start=(f == 0), stop=(f == NF - 1))
                if last == NT:
                    mm.then_inc(pe_y2, 1)

            def attend_before(l, b):
                u = unit(l, b)
                if u:
                    pe.wait_ge(s_y1, u)
                pe.wait_ge(s_sblk, 4 * (u + 1))
                for n in range(1, NC):
                    r = n % 4
                    mm = pe.matmul(tiles(bank_o)[32 * r:32 * r + 32, n // 4, :], qT[:, n * C:(n + 1) * C],
                                   state_blk[:, n - 1, :], start=(n <= 4), stop=False, skip_group_check=True)

            def attend_within(l, b):
                u = unit(l, b)
                pe.wait_ge(s_vg, 8 * (u + 1))
                pe.wait_ge(s_vd, 8 * (u + 1))
                for t in range(NT):
                    pe.wait_ge(s_p, 4 * u + t + 1)
                    for j in range(4):
                        q = slice(32 * j, 32 * j + 32)
                        for r in range(4):
                            n = 4 * t + r
                            mm = pe.matmul(tiles(bank_o)[32 * r:32 * r + 32, t, q], probs[:, n, q],
                                           values_g[:, n, j, :, :], start=False, stop=True,
                                           skip_group_check=True)
                mm.then_inc(pe_o, 1)

            def attention_to_features(l, b):
                u = unit(l, b)
                pe.wait_ge(s_att, u + 1)
                pe.wait_ge(s_ql, u + 1)
                transpose4(bank_q, att).then_inc(pe_aT, 1)

            def back_to_features(l, b):
                m = unit(l, b)
                pe.wait_ge(s_z2, NT * (m + 1))
                pe.wait_ge(s_ktm, m + 3)
                transpose4(bank_tr, z2).then_inc(pe_z2T, 1)

            def output(l, b):
                u = unit(l, b)
                if b == 0:
                    pe.wait_ge(ld_o, 16 * (l + 1))
                pe.wait_ge(s_aT, u + 1)
                pe.wait_ge(s_att, u + 1)
                for t in range(NT):
                    mm = pe.matmul(bank_o[:, t * 128:(t + 1) * 128], attT[:, t * 128:(t + 1) * 128],
                                   w_o[:, :], start=True, stop=True)
                mm.then_inc(pe_wo, 1)

            pe.wait_ge(g_bi, B)
            pe.wait_ge(s_xT, B)
            pe.wait_ge(c_wide, 5)
            for u in range(UNITS + 1):
                now, before, old = of_unit(u), of_unit(u - 1), of_unit(u - 2)
                if u < UNITS:
                    project_queries_keys(*now)
                if u:
                    norm1_to_features(*before)
                if u < UNITS:
                    project_values(*now)
                if u:
                    mlp_up(*before, now if u < UNITS else None)
                else:
                    keys_to_tokens(*now)
                if u < UNITS:
                    states(*now)
                    scores(*now)
                    attend_before(*now)
                    denominators(*now)
                    attend_within(*now)
                if u:
                    mlp_down(*before, 0, 1)
                if u < UNITS:
                    attention_to_features(*now)
                if u:
                    mlp_down(*before, 1, 2)
                if u < UNITS:
                    output(*now)
                if 2 <= u < UNITS - B + 2:
                    back_to_features(*old)
                if u:
                    mlp_down(*before, 2, NT)

            pe.wait_ge(s_y1, UNITS)
            pe.wait_ge(s_x1T, UNITS)
            for b in range(B):
                pe.wait_ge(f_z, NT * (B + b + 1))
                transpose4(banks[b], x2[:, b]).then_inc(pe_x3, 1)
            pe.wait_ge(ld_r0, 32)
            for b in range(B):
                pe.wait_ge(a_x3, b + 1)
                for t in range(NT):
                    n = b * NT + t
                    mm = pe.matmul(banks[4][:, n * E:(n + 1) * E], xT[:, b, t * 128:(t + 1) * 128],
                                   gate_w[:, :], start=True, stop=True)
            mm.then_inc(pe_lg, 1)
            pe.wait_ge(m_gate, 5)
            for t in range(NT):
                mm = pe.transpose(banks[5][0:32, t * 128:(t + 1) * 128], gate_t[:, t, :], ident[:, :])
            mm.then_inc(pe_gt, 1)
            pe.wait_ge(m_rank, 36)
            for t in range(NT):
                mm = pe.transpose(banks[6][:, t * 32:(t + 1) * 32], rank_b[:, t * 128:(t + 1) * 128],
                                  ident[0:32, 0:32])
            mm.then_inc(pe_pt, 1)
            pe.wait_ge(g_xl, B + 1)
            for b in range(B):
                for t in range(NT):
                    n = b * NT + t
                    pe.wait_ge(m_pick, n + 1)
                    if t == 0 and b >= 2:
                        pe.wait_ge(m_xg, 2 * (b - 1))
                    for h in range(2):
                        for i in range(PARTS):
                            mm = pe.matmul(banks[2 * (b % 2) + h][:, :], x_parts[i][:, b, t, :],
                                           pick[n % RING][:, h * 512:(h + 1) * 512],
                                           start=(t == 0 and i == 0), stop=(t == NT - 1 and i == PARTS - 1),
                                           skip_group_check=True)
                    mm.then_inc(pe_g, 1)
                    for e in range(E):
                        k = b * E + e
                        pe.matmul(banks[6][:, PARTS * k:PARTS * (k + 1)],
                                  pick[n % RING][:, e * 128:(e + 1) * 128],
                                  gate_parts[:, :, t * B * E + k], start=(n == 0 and e == 0),
                                  stop=(t == NT - 1), skip_group_check=True)
                    if n >= 2:
                        pe.wait_ge(a_pt, n - 1)
                    for e in range(E):
                        mm = pe.transpose(banks[4 + n % 2][:, :].bitcast(bf16)[:, e * 128:(e + 1) * 128],
                                          pick[n % RING][:, e * 128:(e + 1) * 128], ident_bf[:, :])
                    mm.then_inc(pe_pick, 1)

            def expert_up(e):
                for f in range(NF):
                    n = e * NF + f
                    if n == 0:
                        pe.wait_ge(m_xg, 2 * B)
                        pe.wait_ge(a_pt, B * NT)
                    if n >= 2:
                        pe.wait_ge(a_u, n - 1)
                    pe.matmul(banks[4 + n % 2][:, :], we_1[:, e, f * 128:(f + 1) * 128], xg(e),
                              start=True, stop=True).then_inc(pe_u, 1)

            def expert_down(e):
                pe.wait_ge(a_u, NF * (e + 1))
                if e == 0:
                    pe.wait_ge(m_gs, 1)
                if e >= 2:
                    pe.wait_ge(m_y, e - 1)
                for b in range(B):
                    for f in range(NF):
                        mm = pe.matmul(banks[6 + e % 2][:, b * 128:(b + 1) * 128],
                                       h_e(e)[:, f, b * 128:(b + 1) * 128], we_2[:, e, f, :],
                                       start=(f == 0), stop=(f == NF - 1))
                mm.then_inc(pe_d, 1)

            def scatter(e):
                pe.wait_ge(m_yl, e + 1)
                for b in range(B):
                    for t in range(NT):
                        for i in range(PARTS):
                            mm = pe.matmul(banks[b][:, t * 128:(t + 1) * 128], pick_t[b * NT + t][:, e, :],
                                           y_parts[:, e % 2, i, b, :],
                                           start=(e == 0 and t == 0 and i == 0),
                                           stop=(e == E - 1 and i == PARTS - 1), skip_group_check=True)
                    mm.then_inc(pe_sc, 1)

            pe.wait_ge(ld_e, 32)
            for e in range(E + 2):
                if e < E:
                    expert_up(e)
                if 1 <= e <= E:
                    expert_down(e - 1)
                if e >= 2:
                    scatter(e - 2)

        @block.scalar
        def _(act):
            def rstd(mv, lv, rs, ready, count, s_lv, s_rs, n):
                act.wait_ge(ready, count)
                act.activation(lv, mv, ACT.Ln, bias=ln_eps[:, 0:1]).then_inc(s_lv, 1)
                act.wait_ge(s_lv, n)
                act.activation(rs, lv, ACT.Exp, scale=-0.5).then_inc(s_rs, 1)

            act.preload_act_table_set(LN_EXP)
            act.wait_ge(c_set, 1)
            for b in range(B):
                rstd(mv0[:, b, :, 1], lv0[:, b, :], rs0[:, b, :], d_mv, NT * (b + 1), d_lv, d_rs, b + 1)
            act.wait_ge(ld_c0, 16)
            for b in range(B):
                act.wait_ge(p_a, b + 1)
                act.activation(hT[:, b], banks[b][:, :], ACT.Identity, bias=cols0[:, 1:2],
                               scale=cols0[:, 0:1]).then_inc(a_hT, 1)
            for b in range(B):
                act.wait_ge(p_a, B + 2 * b + 1)
                act.activation(keys0[:, b, :], banks[4 + b][:, :], ACT.Identity, bias=cols0[:, 2:3])\
                    .then_inc(a_key, 1)
            act.wait_ge(v_bka, 1)
            for b in range(B):
                act.wait_ge(p_a, 3 * B + b + 1)
                act.activation(ka0[:, b], banks[4 + b][:, :], ACT.Identity, bias=bka_s[:, 0:1],
                               scale=float(D) ** -0.5).then_inc(a_ka, 1)
                act.wait_ge(a_ka, b + 1)
                act.activation(kw0[:, b], ka0[:, b], ACT.Exp).then_inc(a_ew, 1)
            for b in range(B):
                act.wait_ge(v_cum, b + 1)
                act.activation(cum0[:, b], cum0[:, b], ACT.Ln).then_inc(a_lc, 1)
            for b in range(B):
                act.wait_ge(v_t, b + 1)
                act.activation(kw0[:, b], ka0[:, b], ACT.Exp).then_inc(a_kw, 1)
            for b in range(B):
                rstd(mv0[:, b, :, 1], lv0[:, b, :], rs0[:, b, :], d_mv, NT * (B + b + 1), d_lv, d_rs, B + b + 1)
            for b in range(B):
                act.wait_ge(p_a, 5 * B + b + 1)
                act.activation(xT[:, b, :], banks[4 + b][:, :], ACT.Copy).then_inc(a_x1T, 1)
            for b in range(B):
                rstd(mv0[:, b, :, 1], lv0[:, b, :], rs0[:, b, :], d_mv, NT * (2 * B + b + 1), d_lv, d_rs,
                     2 * B + b + 1)
            for b in range(B):
                act.wait_ge(p_a, 7 * B + b + 1)
                act.activation(xT[:, b, :], banks[4 + b][:, :], ACT.Copy).then_inc(s_xT, 1)

            def norm1(l, b):
                m = unit(l, b)
                rstd(mv1[:, :, 1], lv1[:, :], rs1[:, :], s_mv1, NT * (m + 1), s_lv1, s_rs1, m + 1)

            def feature_map_exp(l, b):
                u = unit(l, b)
                if b == 0:
                    act.wait_ge(ld_a, 48 * (l + 1))
                act.wait_ge(pe_q, u + 1)
                act.activation(q_exp[:, :], bank_q[:, :], ACT.Exp, bias=cols_a[:, 0:1]).then_inc(s_qe, 1)
                act.wait_ge(pe_k, u + 1)
                act.activation(k_exp[:, :], bank_k[:, :], ACT.Exp, bias=cols_a[:, 1:2]).then_inc(s_ke, 1)

            def norm1_to_features(l, b):
                m = unit(l, b)
                if b == 0:
                    act.wait_ge(ld_1, 48 * (l + 1))
                act.wait_ge(pe_z1T, m + 1)
                act.activation(x1T[:, :], bank_tr[:, :], ACT.Identity, bias=cols_1[:, 1:2],
                               scale=cols_1[:, 0:1]).then_inc(s_x1T, 1)

            def gelu(l, b, f):
                m = unit(l, b)
                act.wait_ge(pe_h, NF * m + f + 1)
                act.activation(hidden[:, f, :], bank_s[f % 2][:, :], ACT.Gelu, bias=cols_1[:, 2 + f:3 + f])\
                    .then_inc(s_h, 1)

            def spread_queries(l, b, j):
                act.wait_ge(s_q, unit(l, b) + 1)
                q = slice(32 * j, 32 * j + 32)
                act.activation(queries_j[q, :, j, :], qT[q, :].rearrange("p (n c) -> p n c", c=C),
                               ACT.Copy).then_inc(s_qj, 1)

            def spread_state(l, b):
                act.wait_ge(s_st, unit(l, b) + 1)
                for j in range(4):
                    q = slice(32 * j, 32 * j + 32)
                    act.activation(state_blk[q, :, q], state[q, :, :].rearrange("p c n -> p n c"),
                                   ACT.Copy).then_inc(s_sblk, 1)

            def attention_to_features(l, b):
                act.wait_ge(pe_aT, unit(l, b) + 1)
                act.activation(attT[:, :], bank_q[:, :], ACT.Copy).then_inc(s_aT, 1)

            def norm2(l, b):
                m = unit(l, b)
                rstd(mv2[:, :, 1], lv2[:, :], rs2[:, :], s_mv2, NT * (m + 1), s_lv2, s_rs2, m + 1)

            def norm2_to_features(l, b):
                m = unit(l, b)
                if b == 0:
                    act.wait_ge(ld_2v, 32 * (l + 1))
                act.wait_ge(pe_z2T, m + 1)
                act.activation(xT[:, b, :], bank_tr[:, :], ACT.Identity, bias=cols_2[:, 1:2],
                               scale=cols_2[:, 0:1]).then_inc(s_xT, 1)

            act.wait_ge(c_wide, 5)
            for u in range(UNITS + 2):
                now, before, old = of_unit(u), of_unit(u - 1), of_unit(u - 2)
                if 1 <= u <= UNITS:
                    norm1(*before)
                if u < UNITS:
                    feature_map_exp(*now)
                if 1 <= u <= UNITS:
                    norm1_to_features(*before)
                for step in ("gelu", 0), ("spread", 0), ("gelu", 1), ("spread", 1), ("spread", 2), ("gelu", 2), \
                        ("spread", 3), ("gelu", 3):
                    if step[0] == "gelu" and 1 <= u <= UNITS:
                        gelu(*before, step[1])
                    if step[0] == "spread" and u < UNITS:
                        spread_queries(*now, step[1])
                if 1 <= u <= UNITS:
                    act.preload_act_table_set(LN_EXP)
                if u < UNITS:
                    spread_state(*now)
                if u >= 2:
                    norm2(*old)
                if u < UNITS:
                    attention_to_features(*now)
                if 2 <= u < UNITS - B + 2:
                    norm2_to_features(*old)

            for n in range(2 * B):
                b = n % B
                rstd(mv0[:, b, :, 1], lv0[:, b, :], rs0[:, b, :], f_mv, NT * (n + 1), f_lv, f_rs, n + 1)
            for b in range(B):
                act.wait_ge(pe_x3, b + 1)
                act.activation(xT[:, b, :], banks[b][:, :], ACT.Copy).then_inc(a_x3, 1)
            act.wait_ge(m_gate, 2)
            act.activation(gate_e[:, :, :, :], gate_e[:, :, :, :], ACT.Exp).then_inc(a_gate, 1)
            for b in range(B + 1):
                if b == B:
                    act.wait_ge(m_gate, 5)
                    act.activation(gate_parts[:, 0, :], gate_flat, ACT.Copy).then_inc(a_xh, 1)
                else:
                    act.wait_ge(f_z, NT * (B + b + 1))
                    if b == 0:
                        act.wait_ge(pe_o, UNITS)
                    act.activation(x_parts[0][:, b], x2[:, b], ACT.Copy).then_inc(a_xh, 1)
            for b in range(B + 1):
                act.wait_ge(g_xr, b + 1)
                if b == B:
                    act.activation(gate_parts[:, 1, :], gate_rest[:, :], ACT.Copy).then_inc(a_xm, 1)
                else:
                    act.activation(x_parts[1][:, b], x_rest[:, b], ACT.Copy).then_inc(a_xm, 1)
            act.preload_act_table_set("gelu_and_others")
            for n in range(B * NT):
                act.wait_ge(pe_pick, n + 1)
                act.activation(pick_t[n], banks[4 + n % 2][:, :].bitcast(bf16).rearrange("p (e k) -> p e k", e=E),
                               ACT.Copy).then_inc(a_pt, 1)
            for e in range(E):
                for f in range(NF):
                    n = e * NF + f
                    act.wait_ge(pe_u, n + 1)
                    if e >= 2 and f == 0:
                        act.wait_ge(pe_d, e - 1)
                    act.activation(h_e(e)[:, f, :], banks[4 + n % 2][:, :], ACT.Gelu).then_inc(a_u, 1)
            act.preload_act_table_set(LN_EXP)
            for b in range(B):
                rstd(mv0[:, b, :, 1], lv0[:, b, :], rs0[:, b, :], f_mv, NT * (2 * B + b + 1), f_lv, f_rs,
                     2 * B + b + 1)

        @block.vector
        def _(dve):
            def stats(src, bn, mv, s_bn, s_mv, n):
                for t in range(NT):
                    dve.bn_stats(bn[:, t, :], src[:, t, :]).then_inc(s_bn, 1)
                for t in range(NT):
                    dve.wait_ge(s_bn, NT * (n - 1) + t + 1)
                    dve.bn_aggr(mv[:, t, :], bn[:, t, :]).then_inc(s_mv, 1)

            def normalise(dst, src, mv, rs, s_rs, s_z, n):
                dve.wait_ge(s_rs, n)
                for t in range(NT):
                    dve.tensor_scalar(dst[:, t, :], src[:, t, :], mv[:, t, 0:1], rs[:, t:t + 1],
                                      ALU.subtract, ALU.mult).then_inc(s_z, 1)

            for b in range(B):
                dve.wait_ge(ld_x[b], 16)
                stats(x_in[:, b], bn0[:, b], mv0[:, b], d_bn, d_mv, b + 1)
            for b in range(B):
                normalise(z0[:, b], x_in[:, b], mv0[:, b], rs0[:, b], d_rs, d_z, b + 1)
            dve.wait_ge(ld_c0, 16)
            dve.tensor_scalar(bka_s[:, :], cols0[:, 4:5], float(D) ** -0.5, None, ALU.mult).then_inc(v_bka, 1)
            dve.wait_ge(ld_w0, 16)
            dve.tensor_scalar(w0_sign[:, :], w0[:, 3, :], 0.0, 2.0, ALU.is_ge, ALU.mult).then_inc(v_sgn, 1)
            dve.wait_ge(v_sgn, 1)
            dve.tensor_scalar(w0_sign[:, :], w0_sign[:, :], -1.0, None, ALU.add).then_inc(v_sgn, 1)
            for b in range(B):
                dve.wait_ge(p_a, B + 2 * b + 2)
                dve.tensor_scalar(vals0[:, b, :], banks[b][:, :], cols0[:, 3:4], None, ALU.add)\
                    .then_inc(v_val, 1)
            dve.wait_ge(c_set, 2)
            for b in range(B):
                dve.wait_ge(a_ew, b + 1)
                dve.tensor_tensor_scan(cum0[:, b], one_row, kw0[:, b], 0.0, ALU.mult, ALU.add)\
                    .then_inc(v_cum, 1)
            for b in range(B):
                dve.wait_ge(a_lc, b + 1)
                dve.tensor_tensor(ka0[:, b], ka0[:, b], cum0[:, b], ALU.subtract).then_inc(v_t, 1)
            for b in range(B):
                dve.wait_ge(g_pk, b + 1)
                dve.tensor_tensor_scan(cum0[:, b], one_row, kw0[:, b], 0.0, ALU.mult, ALU.add)\
                    .then_inc(v_pool, 1)
            for b in range(B):
                dve.wait_ge(p_a, 4 * B + b + 1)
                dve.tensor_tensor(x_in[:, b, :, :], tiles(banks[b]), x_in[:, b, :, :], ALU.add).then_inc(v_y, 1)
                dve.wait_ge(v_y, b + 1)
                stats(x_in[:, b], bn0[:, b], mv0[:, b], d_bn, d_mv, B + b + 1)
            for b in range(B):
                normalise(res[:, b], x_in[:, b], mv0[:, b], rs0[:, b], d_rs, d_z, B + b + 1)
            dve.wait_ge(ld_r0, 32)
            for b in range(B):
                dve.wait_ge(p_a, 6 * B + b + 1)
                dve.tensor_tensor(x_in[:, b, :, :], tiles(banks[b]), over_tiles(rows0[:, 0, :]), ALU.mult)\
                    .then_inc(v_sc, 1)
            for b in range(B):
                dve.wait_ge(g_bi, b + 1)
                dve.tensor_scalar(x_in[:, b, :, :], x_in[:, b, :, :], -MAX_VAL, MAX_VAL, ALU.max, ALU.min)\
                    .then_inc(v_cl, 1)
                dve.wait_ge(v_cl, b + 1)
                dve.tensor_tensor(x_in[:, b, :, :], x_in[:, b, :, :], res[:, b, :, :], ALU.add)\
                    .then_inc(v_y, 1)
                dve.wait_ge(v_y, B + b + 1)
                stats(x_in[:, b], bn0[:, b], mv0[:, b], d_bn, d_mv, 2 * B + b + 1)
            for b in range(B):
                normalise(x2[:, b], x_in[:, b], mv0[:, b], rs0[:, b], d_rs, d_z, 2 * B + b + 1)

            def norm1(l, b):
                m = unit(l, b)
                dve.wait_ge(pe_wo, m + 1)
                dve.wait_ge(s_res, m + 1)
                dve.tensor_tensor(y1[:, :, :], tiles(bank_o), res[:, b, :, :], ALU.add).then_inc(s_y1, 1)
                dve.wait_ge(s_y1, m + 1)
                stats(y1, bn1, mv1, s_bn1, s_mv1, m + 1)
                if m:
                    dve.wait_ge(s_r1m, m)
                normalise(z1, y1, mv1, rs1, s_rs1, s_z1, m + 1)

            def feature_map(l, b):
                u = unit(l, b)
                if b == 0:
                    dve.wait_ge(ld_a, 48 * (l + 1))
                dve.wait_ge(s_qe, u + 1)
                dve.tensor_scalar(q_lin[:, :], bank_q[:, :], cols_a[:, 0:1], 0.0, ALU.add, ALU.max)\
                    .then_inc(s_ql, 1)
                dve.wait_ge(s_ke, u + 1)
                dve.tensor_scalar(k_lin[:, :], bank_k[:, :], cols_a[:, 1:2], 0.0, ALU.add, ALU.max)\
                    .then_inc(s_kl, 1)
                dve.wait_ge(s_ql, u + 1)
                dve.scalar_tensor_tensor(out=qT[:, :], in0=q_exp[:, :], scalar=1.0, in1=q_lin[:, :],
                                         op0=ALU.min, op1=ALU.add).then_inc(s_q, 1)
                dve.wait_ge(s_kl, u + 1)
                dve.scalar_tensor_tensor(out=kT[:, :], in0=k_exp[:, :], scalar=1.0, in1=k_lin[:, :],
                                         op0=ALU.min, op1=ALU.add).then_inc(s_k, 1)

            def bias_values(l, b):
                u = unit(l, b)
                dve.wait_ge(pe_v, u + 1)
                if u:
                    dve.wait_ge(s_vg, 8 * u)
                dve.tensor_tensor(v_tm[:, :, :], tiles(bank_kv), over_tiles(row_v[:, :]), ALU.add)\
                    .then_inc(s_v, 1)
                dve.wait_ge(s_v, u + 1)
                for r in range(4):
                    q = slice(32 * r, 32 * r + 32)
                    dve.tensor_copy(v_blk[q, :, r, :], v_tm[q, :, :]).then_inc(s_vb, 1)

            def spread_keys(l, b):
                u = unit(l, b)
                dve.wait_ge(s_k, u + 1)
                for g in range(4):
                    dve.tensor_scalar(keys_g[:, :, g, :], kT[:, :].rearrange("p (n c) -> p n c", c=C),
                                      same_g[:, g:g + 1], None, ALU.mult).then_inc(s_kg, 1)

            def sum_keys(l, b):
                u = unit(l, b)
                dve.tensor_tensor_scan(k_sum[:, :], one_row, kT[:, :], 0.0, ALU.mult, ALU.add)\
                    .then_inc(s_ks, 1)

            def keys_to_tokens(l, b):
                u = unit(l, b)
                dve.wait_ge(pe_kT, u + 1)
                dve.tensor_copy(keys_tm[:, :, :], tiles(bank_tr)).then_inc(s_ktm, 1)

            def prefix_states(l, b):
                u = unit(l, b)
                dve.wait_ge(pe_kv, u + 1)
                dve.tensor_tensor(kv[:, :, :], bank_kv[:, :].rearrange("p (c n) -> p c n", n=NC),
                                  same_g_wide[:, :, :], ALU.mult).then_inc(s_kv, 1)
                dve.wait_ge(s_kv, u + 1)
                dve.tensor_tensor_scan(state[:, :, :].rearrange("p c n -> p (c n)"),
                                       scan_keep[:, :, :].rearrange("p c n -> p (c n)"),
                                       kv[:, :, :].rearrange("p c n -> p (c n)"),
                                       0.0, ALU.mult, ALU.add).then_inc(s_st, 1)

            def mask_scores(l, b, first, last):
                u = unit(l, b)
                for c4 in range(first, last):
                    dve.wait_ge(pe_s, 4 * u + c4 + 1)
                    dve.tensor_tensor(probs[:, 4 * c4:4 * c4 + 4, :], tiles(bank_s[c4 % 2]),
                                      causal[:, :, :], ALU.mult).then_inc(s_p, 1)
                    for k in range(4 * (c4 - 2), 4 * (c4 - 1)) if c4 >= 2 else ():
                        spread_values(dve, 2 + k // 4, k % 4).then_inc(s_vd, 1)

            def residual_sum2(l, b):
                m = unit(l, b)
                dve.wait_ge(pe_y2, m + 1)
                dve.wait_ge(s_r1, m + 1)
                if m:
                    dve.wait_ge(s_z2, NT * m)
                dve.tensor_tensor(y2[:, :, :], tiles(bank_tm), res1[:, :, :], ALU.add).then_inc(s_y2, 1)
                dve.wait_ge(s_y2, m + 1)
                stats(y2, bn2, mv2, s_bn2, s_mv2, m + 1)

            def norm2(l, b):
                m = unit(l, b)
                if m:
                    dve.wait_ge(s_res, B + m)
                normalise(z2, y2, mv2, rs2, s_rs2, s_z2, m + 1)

            def invert_denominators(l, b):
                u = unit(l, b)
                dve.wait_ge(pe_den, u + 1)
                dve.tensor_scalar(den[:, :], bank_kv[:, 0:NT * HEADS], ATT_EPS, None, ALU.add).then_inc(s_den, 1)
                dve.wait_ge(s_den, u + 1)
                dve.reciprocal(inv_den[:, :], den[:, :]).then_inc(s_inv, 1)

            def divide(l, b):
                u = unit(l, b)
                dve.wait_ge(pe_o, u + 1)
                dve.wait_ge(s_inv, u + 1)
                dve.tensor_tensor(att[:, :, :].rearrange("p t (h e) -> p (t h) e", e=HD),
                                  bank_o[:, :].rearrange("p (n e) -> p n e", e=HD),
                                  inv_den[:, :].unsqueeze(2).broadcast_to([128, NT * HEADS, HD]), ALU.mult)\
                    .then_inc(s_att, 1)

            for u in range(UNITS + 2):
                now, before, old = of_unit(u), of_unit(u - 1), of_unit(u - 2)
                if 1 <= u <= UNITS:
                    norm1(*before)
                if u < UNITS:
                    feature_map(*now)
                    bias_values(*now)
                    keys_to_tokens(*now)
                    spread_keys(*now)
                    prefix_states(*now)
                    mask_scores(*now, 0, 2)
                    sum_keys(*now)
                    mask_scores(*now, 2, 4)
                    invert_denominators(*now)
                if u >= 2:
                    residual_sum2(*old)
                if u < UNITS:
                    divide(*now)
                if u >= 2:
                    norm2(*old)

            for b in range(B):
                dve.wait_ge(s_res, UNITS + b + 1)
                stats(res[:, b], bn0[:, b], mv0[:, b], f_bn, f_mv, b + 1)
            for b in range(B):
                normalise(res[:, b], res[:, b], mv0[:, b], rs0[:, b], f_rs, f_z, b + 1)
            for b in range(B):
                dve.wait_ge(f_z, NT * (b + 1))
                dve.tensor_tensor(res[:, b, :, :], res[:, b, :, :], over_tiles(rows0[:, 3, :]), ALU.mult)\
                    .then_inc(f_g, 1)
            for b in range(B):
                dve.wait_ge(f_b, b + 1)
                dve.tensor_tensor(res[:, b, :, :], res[:, b, :, :], x2[:, b, :, :], ALU.add).then_inc(f_y, 1)
                dve.wait_ge(f_y, b + 1)
                stats(res[:, b], bn0[:, b], mv0[:, b], f_bn, f_mv, B + b + 1)
            for b in range(B):
                normalise(x2[:, b], res[:, b], mv0[:, b], rs0[:, b], f_rs, f_z, B + b + 1)

            logits = banks[4][:, 0:B * NT * E].rearrange("p (n e) -> p n e", e=E)
            gate_n = gate_e[:, :, :, :].rearrange("p b t e -> p (b t) e")
            dve.wait_ge(pe_lg, 1)
            dve.tensor_reduce(logits_max[:, :], logits, AX.X, ALU.max).then_inc(m_gate, 1)
            dve.wait_ge(m_gate, 1)
            dve.tensor_tensor(gate_n, logits, logits_max[:, :].unsqueeze(2).broadcast_to([128, B * NT, E]),
                              ALU.subtract).then_inc(m_gate, 1)
            dve.wait_ge(a_gate, 1)
            dve.tensor_reduce(gate_sum[:, :], gate_n, AX.X, ALU.add).then_inc(m_gate, 1)
            dve.wait_ge(m_gate, 3)
            dve.reciprocal(gate_inv[:, :], gate_sum[:, :]).then_inc(m_gate, 1)
            dve.wait_ge(m_gate, 4)
            dve.tensor_tensor(gate_t[:, :, :].rearrange("p t (b e) -> p b t e", b=B), gate_e[:, :, :, :],
                              gate_inv[:, :].rearrange("p (b t) -> p b t", b=B).unsqueeze(3)
                              .broadcast_to([128, B, NT, E]), ALU.mult).then_inc(m_gate, 1)
            dve.wait_ge(pe_gt, 1)
            dve.tensor_copy(rank_a[:, :], banks[5][0:32, :]).then_inc(m_rank, 1)
            for i in range(CAP // 8):
                dve.wait_ge(m_rank, 2 * i + 1)
                dve.max(top8[:, :], rank_a[:, :]).then_inc(m_rank, 1)
                dve.wait_ge(m_rank, 2 * i + 2)
                dve.match_replace(rank_a[:, :], top8[:, :], rank_a[:, :], -1.0).then_inc(m_rank, 1)
            dve.wait_ge(m_rank, 33)
            dve.tensor_scalar(rank_a[:, :], rank_a[:, :], 0.0, None, ALU.is_lt).then_inc(m_rank, 1)
            dve.wait_ge(m_rank, 34)
            dve.tensor_tensor_scan(rank_b[:, :], one_row[0:32], rank_a[:, :], 0.0, ALU.mult, ALU.add)\
                .then_inc(m_rank, 1)
            dve.wait_ge(m_rank, 35)
            dve.tensor_tensor(rank_b[:, :], rank_b[:, :], rank_a[:, :], ALU.mult).then_inc(m_rank, 1)
            dve.wait_ge(pe_pt, 1)
            dve.tensor_scalar(pos_tm[:, :, :].rearrange("p t n -> p (t n)"), banks[6][:, 0:NT * 32], -1.0,
                              None, ALU.add).then_inc(m_pos, 1)
            dve.wait_ge(m_pos, 1)

            def one_hot(n):
                b, t = n // NT, n % NT
                if n >= RING:
                    dve.wait_ge(pe_pick, n - RING + 1)
                dve.tensor_tensor(pick[n % RING].rearrange("p (e k) -> p e k", e=E),
                                  slot_row[:, :].unsqueeze(1).broadcast_to([128, E, 128]),
                                  pos_tm[:, t, b * E:(b + 1) * E].unsqueeze(2).broadcast_to([128, E, 128]),
                                  ALU.is_equal).then_inc(m_pick, 1)

            def gathered(b):
                dve.wait_ge(pe_g, NT * (b + 1))
                for h in range(2):
                    dve.tensor_copy(xg_a[h].rearrange("p (e s) d -> p e s d", s=4)[:, :, b, :],
                                    tiles(banks[2 * (b % 2) + h])).then_inc(m_xg, 1)

            for n in range(B * NT):
                one_hot(n)
                if n >= RING - 1 and n % NT == NT - 1:
                    gathered(n // NT - 1)
            gathered(B - 1)
            dve.wait_ge(pe_pick, B * NT)
            dve.tensor_reduce(slot_gate[:, :], banks[6][:, 0:B * E * PARTS].rearrange("p (k i) -> p k i", i=PARTS),
                              AX.X, ALU.add).then_inc(m_gs, 1)
            dve.wait_ge(m_gs, 1)
            for e in range(E):
                y, parts = y_all[e % 2], y_parts[:, e % 2]
                dve.wait_ge(pe_d, e + 1)
                dve.tensor_tensor(y, tiles(banks[6 + e % 2]),
                                  slot_gate[:, :].rearrange("p (b e) -> p b e", b=B)[:, :, e].unsqueeze(2)
                                  .broadcast_to([128, B, 128]), ALU.mult).then_inc(m_y, 1)
                if e >= 2:
                    dve.wait_ge(pe_sc, B * (e - 1))
                dve.wait_ge(m_y, e + 1)
                dve.tensor_copy(parts[:, 0], y).then_inc(m_yh, 1)
                dve.wait_ge(m_yh, e + 1)
                dve.tensor_tensor(y_rest[:, :, :], y, parts[:, 0], ALU.subtract).then_inc(m_yr, 1)
                dve.wait_ge(m_yr, e + 1)
                dve.tensor_copy(parts[:, 1], y_rest[:, :, :]).then_inc(m_ym, 1)
                dve.wait_ge(m_ym, e + 1)
                dve.tensor_tensor(parts[:, 2], y_rest[:, :, :], parts[:, 1], ALU.subtract).then_inc(m_yl, 1)
                if e + 1 < E:
                    dve.wait_ge(m_yl, e + 1)
            for b in range(B + 1):
                if b < B:
                    dve.wait_ge(pe_sc, B * (E - 1) + b + 1)
                    dve.tensor_tensor(res[:, b, :, :], tiles(banks[b]), x2[:, b, :, :], ALU.add).then_inc(m_sc, 1)
                    dve.wait_ge(m_sc, b + 1)
                    stats(res[:, b], bn0[:, b], mv0[:, b], f_bn, f_mv, 2 * B + b + 1)
                if b:
                    c = b - 1
                    normalise(res[:, c], res[:, c], mv0[:, c], rs0[:, c], f_rs, f_z, 2 * B + c + 1)

        @block.gpsimd
        def _(pool):
            pool.memset(ln_eps[:, :], LN_EPS).then_inc(c_set, 1)
            pool.memset(ones[:, :], 1.0).then_inc(c_set, 1)
            pool.wait_ge(c_set, 2)
            pool.affine_select(out=ident[:, :], in_=ones[:, :], compare_op=ALU.is_equal, fill=0.0, base=0,
                               pattern=[[-1, 128]], channel_multiplier=1).then_inc(c_done, 1)
            pool.affine_select(out=of_head[:, :], in_=ones[:, 0:HEADS], compare_op=ALU.is_ge, fill=0.0, base=0,
                               pattern=[[-HD, HEADS]], channel_multiplier=1).then_inc(c_sel, 1)
            pool.memset(causal[:, :, :], 1.0).then_inc(c_sel, 1)
            pool.memset(scan_keep[:, :, :], 1.0).then_inc(c_sel, 1)
            pool.iota(slot_int[:, :], pattern=[[1, 128]], base=0, channel_multiplier=0).then_inc(c_sel, 1)
            pool.wait_ge(c_done, 1)
            pool.tensor_copy(ident_bf[:, :], ident[:, :]).then_inc(c_wide, 1)
            pool.wait_ge(c_sel, 4)
            pool.affine_select(out=of_head[:, :], in_=of_head[:, :], compare_op=ALU.is_ge, fill=0.0,
                               base=HD - 1, pattern=[[HD, HEADS]], channel_multiplier=-1)\
                .then_inc(c_sel, 1)
            pool.memset(scan_keep[:, :, 0:1], 0.0).then_inc(c_sel, 1)
            pool.tensor_copy(slot_row[:, :], slot_int[:, :]).then_inc(c_sel, 1)
            for j in range(Q4):
                q = slice(32 * j, 32 * j + 32)
                pool.wait_ge(c_sel, 7 + 3 * j)
                pool.affine_select(out=same_g[q, :], in_=ones[q, 0:4], compare_op=ALU.is_ge, fill=0.0, base=0,
                                   pattern=[[-HD, 4]], channel_multiplier=1).then_inc(c_sel, 1)
                pool.wait_ge(c_sel, 8 + 3 * j)
                pool.affine_select(out=same_g[q, :], in_=same_g[q, :], compare_op=ALU.is_ge, fill=0.0,
                                   base=HD - 1, pattern=[[HD, 4]], channel_multiplier=-1).then_inc(c_sel, 1)
                pool.wait_ge(c_sel, 9 + 3 * j)
                pool.affine_select(out=causal[q, :, :], in_=causal[q, :, :], compare_op=ALU.is_ge, fill=0.0,
                                   base=0, pattern=[[0, 4], [0, 4], [1, C]], channel_multiplier=-1)\
                    .then_inc(c_sel, 1)
            pool.wait_ge(c_sel, 19)
            pool.tensor_copy(same_g_wide[:, :, :].rearrange("p (g d) n -> p g (d n)", g=4),
                             same_g[:, :].unsqueeze(2).broadcast_to([128, 4, HD * NC])).then_inc(c_sel, 1)
            pool.memset(queries_j[:, :, :, :], 0.0).then_inc(c_wide, 1)
            pool.memset(values_g[:, :, :, :, :], 0.0).then_inc(c_wide, 1)
            pool.memset(v_blk[:, :, :, :], 0.0).then_inc(c_wide, 1)
            pool.wait_ge(p_a, B)
            pool.wait_ge(c_sel, 20)
            pool.memset(state_blk[:, :, :], 0.0).then_inc(c_wide, 1)

            for b in range(B):
                pool.wait_ge(a_kw, b + 1)
                pool.tensor_tensor(kw0[:, b], kw0[:, b], keys0[:, b, :], ALU.mult).then_inc(g_pk, 1)
            for b in range(B):
                pool.wait_ge(v_pool, b + 1)
                pool.wait_ge(v_val, b + 1)
                pool.tensor_tensor(ka0[:, b], cum0[:, b], vals0[:, b, :], ALU.mult).then_inc(g_prod, 1)
            pool.wait_ge(ld_r0, 32)
            for b in range(B):
                pool.wait_ge(v_sc, b + 1)
                pool.tensor_tensor(x_in[:, b], x_in[:, b], over_tiles(rows0[:, 1, :]), ALU.add).then_inc(g_bi, 1)
            for b in range(B):
                pool.wait_ge(d_z, NT * (2 * B + b + 1))
                pool.tensor_tensor(res[:, b], x2[:, b], over_tiles(rows0[:, 2, :]), ALU.add).then_inc(s_res, 1)

            def residual1(l, b):
                m = unit(l, b)
                if m + 1 < UNITS:
                    pool.wait_ge(s_vg, 8 * (m + 2))
                if b == 0:
                    pool.wait_ge(ld_1, 48 * (l + 1))
                    pool.tensor_tensor(shift_1[:, :], rows_1[:, 1, :], rows_1[:, 2, :], ALU.add).then_inc(s_sh1, 1)
                pool.wait_ge(s_z1, NT * (m + 1))
                if m:
                    pool.wait_ge(s_y2, m)
                pool.tensor_tensor(res1[:, :, :], z1[:, :, :], over_tiles(rows_1[:, 0, :]), ALU.mult)\
                    .then_inc(s_r1m, 1)
                pool.wait_ge(s_r1m, m + 1)
                pool.wait_ge(s_sh1, l + 1)
                pool.tensor_tensor(res1[:, :, :], res1[:, :, :], over_tiles(shift_1[:, :]), ALU.add)\
                    .then_inc(s_r1, 1)

            def weigh_key_sums(l, b):
                u = unit(l, b)
                pool.wait_ge(s_ks, u + 1)
                pool.wait_ge(s_q, u + 1)
                pool.wait_ge(s_vg, 8 * (u + 1))
                pool.tensor_tensor(qk_sum[:, :], qT[:, :], k_sum[:, :], ALU.mult).then_inc(s_qk, 1)

            def spread_first_values(l, b):
                u = unit(l, b)
                pool.wait_ge(s_v, u + 1)
                for k in range(8):
                    if k:
                        pool.wait_ge(s_vg, 8 * u + k)
                    spread_values(pool, k // 4, k % 4).then_inc(s_vg, 1)

            def residual2(l, b):
                m = unit(l, b)
                if b == 0:
                    pool.wait_ge(ld_2v, 32 * (l + 1))
                    pool.tensor_tensor(shift_2[:, :], rows_2[:, 1, :], rows_2[:, 2, :], ALU.add).then_inc(s_sh2, 1)
                pool.wait_ge(s_z2, NT * (m + 1))
                pool.tensor_tensor(res[:, b], z2[:, :, :], over_tiles(rows_2[:, 0, :]), ALU.mult)\
                    .then_inc(s_r2m, 1)
                pool.wait_ge(s_r2m, m + 1)
                pool.wait_ge(s_sh2, l + 1)
                pool.tensor_tensor(res[:, b], res[:, b], over_tiles(shift_2[:, :]), ALU.add).then_inc(s_res, 1)

            for u in range(UNITS + 2):
                if u < UNITS:
                    spread_first_values(*of_unit(u))
                    weigh_key_sums(*of_unit(u))
                if 1 <= u <= UNITS:
                    residual1(*of_unit(u - 1))
                if u >= 2:
                    residual2(*of_unit(u - 2))
            for b in range(B):
                pool.wait_ge(f_g, b + 1)
                pool.tensor_tensor(res[:, b], res[:, b], over_tiles(rows0[:, 4, :]), ALU.add).then_inc(f_b, 1)
            for b in range(B + 1):
                pool.wait_ge(a_xh, b + 1)
                if b == B:
                    pool.tensor_tensor(gate_rest[:, :], gate_flat, gate_parts[:, 0, :], ALU.subtract).then_inc(g_xr, 1)
                else:
                    pool.tensor_tensor(x_rest[:, b], x2[:, b], x_parts[0][:, b], ALU.subtract).then_inc(g_xr, 1)
            pool.wait_ge(pe_lg, 1)
            for b in range(B + 1):
                pool.wait_ge(a_xm, b + 1)
                if b == B:
                    pool.tensor_tensor(gate_parts[:, 2, :], gate_rest[:, :], gate_parts[:, 1, :], ALU.subtract)\
                        .then_inc(g_xl, 1)
                else:
                    pool.tensor_tensor(x_parts[2][:, b], x_rest[:, b], x_parts[1][:, b], ALU.subtract)\
                        .then_inc(g_xl, 1)


def kernel(**inputs):
    import numpy as np
    import concourse.bacc as bacc
    from concourse import mybir as mb
    from concourse.bass_utils import run_bass_kernel_spmd

    x = {k: np.asarray(v) for k, v in inputs.items()}
    at = {k[8:]: v for k, v in x.items() if k.startswith("L1_attn_")}
    l0 = {k[8:]: v for k, v in x.items() if k.startswith("L0_attn_")}
    b1 = at["b1"].reshape(L, NF, 128).transpose(0, 2, 1)
    no_bias = np.zeros_like(at["bo"][:1])
    packed = {
        "x": l0["hidden_states"],
        "cols0": np.stack([l0["gamma"], l0["beta"], l0["bk"], l0["bv"], l0["bka"]], axis=1),
        "w0": np.stack([l0["Wk"].T, l0["Wv"].T, l0["Wka"].T, x["L0_ffn_weights"].T]),
        "rows0": np.stack([x["L0_ffn_scale"], x["L0_ffn_bias"], at["bo"][0], at["gf"], at["bef"]]),
        "w_qkv": np.stack([at["Wq"], at["Wk"], at["Wv"]], axis=1),
        "cols_a": np.stack([at["bq"], at["bk"]], axis=2),
        "row_v": at["bv"],
        "w_o": at["Wo"],
        "w_1": at["W1"],
        "w_2": at["W2"],
        "cols_1": np.concatenate([at["g1"][:, :, None], at["be1"][:, :, None], b1], axis=2),
        "rows_1": np.stack([at["g1"], at["be1"], at["b2"]], axis=1),
        "cols_2": np.stack([at["g2"], at["be2"]], axis=2),
        "rows_2": np.stack([at["g2"], at["be2"], np.concatenate([at["bo"][1:], no_bias])], axis=1),
        "gate_w": x["L1_ffn_gate_w"],
        "we_1": x["L1_ffn_w1"],
        "we_2": x["L1_ffn_w2"],
    }
    nc = bacc.Bacc("TRN2", target_bir_lowering=False, num_devices=1)
    arrays, args = {}, {}
    for name, v in packed.items():
        v = np.ascontiguousarray(v)
        arrays[f"in_{name}"] = v
        args[name] = nc.dram_tensor(f"in_{name}", v.shape, mb.dt.from_np(v.dtype), kind="ExternalInput").ap()
    out = nc.dram_tensor("out", (B, S, D), mb.dt.float32, kind="ExternalOutput").ap()
    build(nc, args, out)
    r = run_bass_kernel_spmd(nc, [arrays], core_ids=[0])
    return r.results[0]["out"]
```

```python
import concourse.bass as bass
from concourse import mybir
from contextlib import ExitStack

D = 128
B = 4
S = 512
NT = S // 128
L = 4
FF = 512
NF = FF // 128
HEADS = 16
HD = D // HEADS
Q4 = 4
C = 32
NC = S // C
E = 8
CAP = 2 * S // E
LN_EPS = 1e-5
ATT_EPS = 1e-6
MAX_VAL = 100.0
UNITS = L * B
PARTS = 3
ROUNDS = CAP // 8
RING = 8
LN_EXP = "natural_log_exp_and_others"


def build(nc, a, out):
    f32 = mybir.dt.float32
    i32 = mybir.dt.int32
    bf16 = mybir.dt.bfloat16
    ALU = mybir.AluOpType
    ACT = mybir.ActivationFunctionType
    AX = mybir.AxisListType

    ctx = ExitStack()
    with ctx:
        def sb(name, shape, dt=f32):
            return ctx.enter_context(nc.sbuf_tensor(name, shape, dt))

        def pb(name):
            return ctx.enter_context(nc.psum_tensor(name, [128, 512], f32))

        def sem(name):
            return ctx.enter_context(nc.semaphore(name))

        ident = sb("ident", [128, 128])
        ident_bf = sb("ident_bf", [128, 128], bf16)
        ones = sb("ones", [128, 128])
        causal = sb("causal", [128, 4, 128])
        same_g = sb("same_g", [128, 4])
        same_g_wide = sb("same_g_wide", [128, C, NC])
        scan_keep = sb("scan_keep", [128, C, NC])
        of_head = sb("of_head", [128, HEADS])
        slot_row = sb("slot_row", [128, 128])
        slot_int = sb("slot_int", [128, 128], i32)
        ln_eps = sb("ln_eps", [128, NT])
        minus_half = sb("minus_half", [128, NT])

        w0 = sb("w0", [128, 4, 128])
        w0_sign = sb("w0_sign", [128, 128])
        cols0 = sb("cols0", [128, 7])
        bka_s = sb("bka_s", [128, 1])
        rows0 = sb("rows0", [128, 3, 128])
        w_qkv = sb("w_qkv", [128, 3, 128])
        w_o = sb("w_o", [128, 128])
        w_1 = sb("w_1", [128, FF])
        w_2 = sb("w_2", [128, NF, 128])
        cols_a = sb("cols_a", [128, 2])
        row_v = sb("row_v", [128, 128])
        cols_1 = sb("cols_1", [128, 2 + NF])
        rows_1 = sb("rows_1", [128, 3, 128])
        cols_2 = sb("cols_2", [128, 2])
        rows_2 = sb("rows_2", [128, 3, 128])
        shift_1 = sb("shift_1", [128, 128])
        shift_2 = sb("shift_2", [128, 128])
        gate_w = sb("gate_w", [128, E])
        we_1 = sb("we_1", [128, E, FF])
        we_2 = sb("we_2", [128, E, NF, 128])

        xT = sb("xT", [128, B, S])
        res = sb("res", [128, B, NT, 128])
        x2 = sb("x2", [128, B, NT, 128])

        qT = sb("qT", [128, S])
        kT = sb("kT", [128, S])
        q_exp = sb("q_exp", [128, S])
        k_exp = sb("k_exp", [128, S])
        q_lin = sb("q_lin", [128, S])
        k_lin = sb("k_lin", [128, S])
        keys_g = sb("keys_g", [128, NC, 4, C])
        queries_j = sb("queries_j", [128, NC, 4, C])
        values_g = sb("values_g", [128, NC, 4, 4, HD])
        keys_tm = sb("keys_tm", [128, NT, 128])
        v_tm = sb("v_tm", [128, NT, 128])
        v_blk = sb("v_blk", [128, NT, 4, 128])
        probs = sb("probs", [128, NC, 128])
        kv = sb("kv", [128, C, NC])
        state = sb("state", [128, C, NC])
        state_blk = sb("state_blk", [128, NC, 128])
        k_sum = sb("k_sum", [128, S])
        qk_sum = sb("qk_sum", [128, S])
        den = sb("den", [128, NT * HEADS])
        inv_den = sb("inv_den", [128, NT * HEADS])
        att = sb("att", [128, NT, 128])
        attT = sb("attT", [128, S])
        y1 = sb("y1", [128, NT, 128])
        z1 = sb("z1", [128, NT, 128])
        x1T = sb("x1T", [128, S])
        res1 = sb("res1", [128, NT, 128])
        hidden = sb("hidden", [128, NF, S])
        y2 = sb("y2", [128, NT, 128])
        z2 = sb("z2", [128, NT, 128])
        bn1 = sb("bn1", [128, NT, 6])
        mv1 = sb("mv1", [128, NT, 2])
        lv1 = sb("lv1", [128, NT])
        rs1 = sb("rs1", [128, NT])
        bn2 = sb("bn2", [128, NT, 6])
        mv2 = sb("mv2", [128, NT, 2])
        lv2 = sb("lv2", [128, NT])
        rs2 = sb("rs2", [128, NT])
        bn0 = sb("bn0", [128, B, NT, 6])
        mv0 = sb("mv0", [128, B, NT, 2])
        lv0 = sb("lv0", [128, B, NT])
        rs0 = sb("rs0", [128, B, NT])
        shift0 = sb("shift0", [128, B, NT])
        logits_max = sb("logits_max", [128, B * NT])
        gate_e = sb("gate_e", [128, B, NT, E])
        gate_sum = sb("gate_sum", [128, B * NT])
        gate_inv = sb("gate_inv", [128, B * NT])
        gate_t = sb("gate_t", [128, NT, B * E])
        pos_tm = sb("pos_tm", [128, NT, B * E])
        gate_parts = sb("gate_parts", [128, PARTS, NT * B * E], bf16)
        gate_rest = sb("gate_rest", [128, NT * B * E])
        slot_gate = sb("slot_gate", [128, B * E])
        half_p = sb("half_p", [64, S // 2])
        top_half = sb("top_half", [64, CAP])
        top_all = sb("top_all", [32, CAP])
        top_tie = sb("top_tie", [32, CAP])
        least = sb("least", [32, 1])
        ties = sb("ties", [32, 1])
        rank_a = sb("rank_a", [32, S])
        rank_b = sb("rank_b", [32, S])

        x_in = probs[:, :, :].rearrange("p (b t) d -> p b t d", b=B)
        z0 = state_blk[:, :, :].rearrange("p (b t) d -> p b t d", b=B)
        hT = keys_g[:, :, :, :].rearrange("p (b n) g c -> p b (n g c)", b=B)
        keys0 = hidden
        ffn0 = hidden
        vals0 = we_1[:, 0:4, :]
        ka0 = we_1[:, 4:8, :]
        cum0 = we_2[:, 0:4, :, :].rearrange("p a f d -> p a (f d)")
        kw0 = we_2[:, 4:8, :, :].rearrange("p a f d -> p a (f d)")
        def flat_bf(t, dims):
            return t.rearrange(dims).bitcast(bf16)

        pick = [flat_bf(t[:, :, :, :], "p n g c -> p (n g c)").rearrange("p (k x) -> p k x", k=RING // 2)[:, i, :]
                for t in (keys_g, queries_j) for i in range(RING // 2)]
        pick_t = [t[:, :].bitcast(bf16) for t in (qT, kT, q_exp, k_exp, q_lin, k_lin, k_sum, qk_sum, attT)] \
            + [flat_bf(t[:, :, :], "p t d -> p (t d)") for t in (keys_tm, v_tm, kv, state, att, y1, z1)]
        pick_t = [t.rearrange("p (e k) -> p e k", e=E) for t in pick_t]
        x_rest = res
        x_parts = [flat_bf(values_g[:, :, :, :, :], "p n j g e -> p (n j g e)")[:, i * B * S:(i + 1) * B * S]
                   for i in range(2)] + [flat_bf(xT[:, :, :], "p b s -> p (b s)")[:, 0:B * S]]
        x_parts = [t.rearrange("p (b t d) -> p b t d", b=B, t=NT) for t in x_parts]
        y_all = [x1T[:, :].rearrange("p (b d) -> p b d", b=B), res1[:, :, :]]
        y_rest = y2
        y_parts = flat_bf(queries_j[:, :, :, :], "p n g c -> p (n g c)")[:, 0:2 * PARTS * S]\
            .rearrange("p (r i b d) -> p r i b d", r=2, i=PARTS, b=B)
        xg_a = [t[:, :, :] for t in (probs, state_blk)]

        bank_q = pb("bank_q")
        bank_k = pb("bank_k")
        bank_tm = pb("bank_tm")
        bank_tr = pb("bank_tr")
        bank_kv = pb("bank_kv")
        bank_s = [pb("bank_s0"), pb("bank_s1")]
        bank_o = pb("bank_o")
        banks = [bank_q, bank_k, bank_tm, bank_tr, bank_kv, bank_s[0], bank_s[1], bank_o]

        def score_bank(c4):
            return (bank_s[0], bank_s[1], bank_k, bank_s[0])[c4]

        def tiles(bank):
            return bank[:, :].rearrange("p (t d) -> p t d", d=128)

        def over_tiles(row):
            return row.unsqueeze(1).broadcast_to([128, NT, 128])

        ld_x = [sem(f"ld_x{b}") for b in range(B)]
        ld_w0 = sem("ld_w0")
        ld_c0 = sem("ld_c0")
        ld_r0 = sem("ld_r0")
        ld_a = sem("ld_a")
        ld_o = sem("ld_o")
        ld_1 = sem("ld_1")
        ld_2 = sem("ld_2")
        ld_2v = sem("ld_2v")
        ld_e = sem("ld_e")
        st_out = sem("st_out")
        c_set = sem("c_set")
        c_sel = sem("c_sel")
        c_done = sem("c_done")
        c_wide = sem("c_wide")
        d_bn = sem("d_bn")
        d_mv = sem("d_mv")
        d_lv = sem("d_lv")
        d_rs = sem("d_rs")
        d_z = sem("d_z")
        d_za = sem("d_za")
        p_zT = sem("p_zT")
        p_k = sem("p_k")
        p_v = sem("p_v")
        p_ka = sem("p_ka")
        p_yT = sem("p_yT")
        d_nm = sem("d_nm")
        p_x1 = sem("p_x1")
        p_ff = sem("p_ff")
        p_fT = sem("p_fT")
        p_x2 = sem("p_x2")
        a_hT = sem("a_hT")
        a_ff = sem("a_ff")
        a_key = sem("a_key")
        v_val = sem("v_val")
        v_bka = sem("v_bka")
        v_sgn = sem("v_sgn")
        a_ka = sem("a_ka")
        a_ew = sem("a_ew")
        v_cum = sem("v_cum")
        a_lc = sem("a_lc")
        v_t = sem("v_t")
        a_kw = sem("a_kw")
        v_pk = sem("v_pk")
        v_pool = sem("v_pool")
        g_prod = sem("g_prod")
        v_y = sem("v_y")
        a_x1T = sem("a_x1T")
        v_cl = sem("v_cl")
        pe_q = sem("pe_q")
        pe_k = sem("pe_k")
        pe_v = sem("pe_v")
        pe_z1T = sem("pe_z1T")
        pe_h = sem("pe_h")
        pe_kT = sem("pe_kT")
        pe_kv = sem("pe_kv")
        pe_s = sem("pe_s")
        pe_den = sem("pe_den")
        pe_y2 = sem("pe_y2")
        pe_o = sem("pe_o")
        pe_z2T = sem("pe_z2T")
        pe_aT = sem("pe_aT")
        pe_wo = sem("pe_wo")
        s_qe = sem("s_qe")
        s_ke = sem("s_ke")
        s_lv1 = sem("s_lv1")
        s_rs1 = sem("s_rs1")
        s_lv2 = sem("s_lv2")
        s_rs2 = sem("s_rs2")
        s_x1T = sem("s_x1T")
        s_h = sem("s_h")
        s_qj = sem("s_qj")
        s_ktm = sem("s_ktm")
        s_sblk = sem("s_sblk")
        s_aT = sem("s_aT")
        s_xT = sem("s_xT")
        s_y1 = sem("s_y1")
        s_bn1 = sem("s_bn1")
        s_mv1 = sem("s_mv1")
        s_z1 = sem("s_z1")
        s_ql = sem("s_ql")
        s_kl = sem("s_kl")
        s_q = sem("s_q")
        s_k = sem("s_k")
        s_v = sem("s_v")
        s_kg = sem("s_kg")
        s_kp = sem("s_kp")
        s_ks = sem("s_ks")
        s_kv = sem("s_kv")
        s_st = sem("s_st")
        s_p = sem("s_p")
        s_y2 = sem("s_y2")
        s_bn2 = sem("s_bn2")
        s_mv2 = sem("s_mv2")
        s_z2 = sem("s_z2")
        s_den = sem("s_den")
        s_inv = sem("s_inv")
        s_att = sem("s_att")
        s_sh1 = sem("s_sh1")
        s_sh2 = sem("s_sh2")
        s_r1m = sem("s_r1m")
        s_r1 = sem("s_r1")
        s_r2m = sem("s_r2m")
        s_res = sem("s_res")
        s_vg = sem("s_vg")
        s_vb = sem("s_vb")
        s_vd = sem("s_vd")
        s_qk = sem("s_qk")
        f_bn = sem("f_bn")
        f_mv = sem("f_mv")
        f_lv = sem("f_lv")
        f_ve = sem("f_ve")
        f_ra = sem("f_ra")
        f_nm = sem("f_nm")
        f_za = sem("f_za")
        f_rs = sem("f_rs")
        f_z = sem("f_z")
        f_x3 = [sem(f"f_x3_{b}") for b in range(B)]
        f_g = sem("f_g")
        f_b = sem("f_b")
        f_y = sem("f_y")
        pe_x3 = sem("pe_x3")
        a_x3 = sem("a_x3")
        pe_lg = sem("pe_lg")
        m_gate = sem("m_gate")
        a_gate = sem("a_gate")
        pe_gt = sem("pe_gt")
        m_rank = sem("m_rank")
        pe_pt = sem("pe_pt")
        m_pos = sem("m_pos")
        m_pick = sem("m_pick")
        pe_g = sem("pe_g")
        m_xg = sem("m_xg")
        pe_u = sem("pe_u")
        a_u = sem("a_u")
        pe_d = sem("pe_d")
        a_xh = sem("a_xh")
        g_xr = sem("g_xr")
        a_xm = sem("a_xm")
        g_xl = sem("g_xl")
        pe_pick = sem("pe_pick")
        a_pt = sem("a_pt")
        m_gs = sem("m_gs")
        m_y = sem("m_y")
        m_yh = sem("m_yh")
        m_yr = sem("m_yr")
        m_ym = sem("m_ym")
        m_yl = sem("m_yl")
        pe_sc = sem("pe_sc")
        m_sc = sem("m_sc")

        block = ctx.enter_context(nc.Block())

        def unit(l, b):
            return l * B + b

        def of_unit(u):
            return u // B, u % B

        def rows_of(ap):
            return ap.unsqueeze(0).broadcast_to([128] + list(ap.shape))

        one_row = ones[:, 0:1].broadcast_to([128, S])

        def xg(e):
            return xg_a[e // 4][:, 4 * (e % 4):4 * (e % 4) + 4, :]

        def spread_values(eng, r, g):
            src = v_tm[32 * r:32 * r + 32, :, :].rearrange("p t (j g d) -> p t j g d", j=4, g=4)
            dst = values_g[32 * g:32 * g + 32, :, :, :, :].rearrange("p (t r) j g d -> p t r j g d", r=4)
            return eng.tensor_copy(dst[:, :, r, :, g, :], src[:, :, :, g, :])

        gate_flat = gate_t[:, :, :].rearrange("p t k -> p (t k)")

        final_order = [(0, 0), (0, 1), (1, 0), (2, 0), (1, 1), (2, 1), (3, 0), (3, 1)]
        by_pool = 5

        def final_no(b, k):
            return final_order.index((b, k))

        def h_e(e):
            return hidden if e % 2 == 0 else he_b

        he_b = v_blk[:, :, :, :].rearrange("p t c d -> p t (c d)")

        @block.sync
        def _(sp):
            x_v = a["x"].rearrange("b (t p) d -> b p t d", p=128)
            for b in range(B):
                sp.dma_start(x_in[:, b, :, :], x_v[b]).then_inc(ld_x[b], 16)
                if b == 0:
                    sp.dma_start(cols0[:, :], a["cols0"]).then_inc(ld_c0, 16)
                    sp.dma_start(w0[:, :, :], a["w0"].rearrange("n i o -> i n o")).then_inc(ld_w0, 16)
            sp.dma_start(rows0[:, :, :], rows_of(a["rows0"])).then_inc(ld_r0, 16)
            sp.dma_start(gate_w[:, :], a["gate_w"]).then_inc(ld_r0, 16)
            for l in range(L):
                if l:
                    sp.wait_ge(s_v, unit(l, 0))
                    sp.wait_ge(s_ke, unit(l, 0))
                sp.dma_start(w_qkv[:, :, :], a["w_qkv"][l].rearrange("n i o -> i n o")).then_inc(ld_a, 16)
                sp.dma_start(cols_a[:, :], a["cols_a"][l]).then_inc(ld_a, 16)
                sp.dma_start(row_v[:, :], rows_of(a["row_v"][l])).then_inc(ld_a, 16)
                if l:
                    sp.wait_ge(pe_wo, unit(l, 0))
                sp.dma_start(w_o[:, :], a["w_o"][l]).then_inc(ld_o, 16)
                if l:
                    sp.wait_ge(s_h, NF * unit(l, 0))
                    sp.wait_ge(s_sh1, l)
                    sp.wait_ge(s_r1, unit(l, 0))
                sp.dma_start(w_1[:, :], a["w_1"][l]).then_inc(ld_1, 16)
                sp.dma_start(cols_1[:, :], a["cols_1"][l]).then_inc(ld_1, 16)
                sp.dma_start(rows_1[:, :, :], rows_of(a["rows_1"][l])).then_inc(ld_1, 16)
                if l:
                    sp.wait_ge(pe_y2, unit(l, 0))
                sp.dma_start(w_2[:, :, :], a["w_2"][l].rearrange("(f p) d -> p f d", p=128)).then_inc(ld_2, 16)
                if l:
                    sp.wait_ge(s_xT, unit(l + 1, 0))
                    sp.wait_ge(s_res, unit(l + 1, 0))
                sp.dma_start(cols_2[:, :], a["cols_2"][l]).then_inc(ld_2v, 16)
                sp.dma_start(rows_2[:, :, :], rows_of(a["rows_2"][l])).then_inc(ld_2v, 16)
                if l == 0:
                    sp.wait_ge(p_yT, B)
                    sp.dma_start(we_1[:, :, :], a["we_1"].rearrange("e i f -> i e f")).then_inc(ld_e, 16)
                    sp.dma_start(we_2[:, :, :, :],
                                 a["we_2"].rearrange("e (f p) d -> p e f d", p=128)).then_inc(ld_e, 16)
            o_v = out.rearrange("b (t p) d -> b p t d", p=128)
            for n in range(B * NT):
                if n < (B - 1) * NT:
                    sp.wait_ge(f_za, n + 1)
                else:
                    sp.wait_ge(f_z, n - (B - 1) * NT + 1)
                sp.dma_start(o_v[n // NT, :, n % NT, :], res[:, n // NT, n % NT, :]).then_inc(st_out, 16)
            sp.wait_ge(st_out, 16 * B * NT)

        @block.tensor
        def _(pe):
            def transpose4(bank, src):
                for t in range(NT):
                    mm = pe.transpose(bank[:, t * 128:(t + 1) * 128], src[:, t, :], ident[:, :])
                return mm

            pe.wait_ge(c_done, 1)
            def normalised(n):
                pe.wait_ge(d_z, 2 * n)
                pe.wait_ge(d_za, 2 * n)

            for b in range(B):
                normalised(b + 1)
                transpose4(banks[b], z0[:, b]).then_inc(p_zT, 1)
            pe.wait_ge(ld_w0, 16)
            for b in range(B):
                pe.wait_ge(a_hT, b + 1)
                pe.matmul(banks[4 + b][:, :], w0[:, 0, :], hT[:, b], start=True, stop=True).then_inc(p_k, 1)
            for b in range(B):
                pe.wait_ge(a_key, b + 1)
                pe.matmul(banks[4 + b][:, :], w0[:, 2, :], keys0[:, b, :], start=True, stop=True)\
                    .then_inc(p_ka, 1)
                pe.matmul(banks[b][:, :], w0[:, 1, :], hT[:, b], start=True, stop=True).then_inc(p_v, 1)
            for b in range(B):
                pe.wait_ge(g_prod, b + 1)
                pe.wait_ge(v_val, b + 1)
                transpose4(banks[b], ka0[:, b].rearrange("p (t d) -> p t d", d=128)).then_inc(p_yT, 1)
            pe.wait_ge(v_sgn, 2)
            for i in range(B + 2):
                if i < B:
                    normalised(B + i + 1)
                    pe.wait_ge(a_ka, i + 1)
                    transpose4(banks[4 + i], res[:, i]).then_inc(p_x1, 1)
                if 1 <= i <= B:
                    pe.wait_ge(a_x1T, i)
                    pe.matmul(banks[i - 1][:, :], w0_sign[:, :], xT[:, i - 1, :], start=True, stop=True)\
                        .then_inc(p_ff, 1)
                if i >= 2:
                    b = i - 2
                    pe.wait_ge(v_cl, b + 1)
                    transpose4(banks[4 + b], ffn0[:, b].rearrange("p (t d) -> p t d", d=128)).then_inc(p_fT, 1)
            def project_queries_keys(l, b):
                u = unit(l, b)
                if b == 0:
                    pe.wait_ge(ld_a, 48 * (l + 1))
                pe.wait_ge(s_xT, u + 1)
                if u:
                    pe.wait_ge(s_aT, u)
                pe.matmul(bank_q[:, :], w_qkv[:, 0, :], xT[:, b, :], start=True, stop=True).then_inc(pe_q, 1)
                if u:
                    pe.wait_ge(s_p, 4 * u)
                pe.matmul(bank_k[:, :], w_qkv[:, 1, :], xT[:, b, :], start=True, stop=True).then_inc(pe_k, 1)

            def project_values(l, b):
                u = unit(l, b)
                if u:
                    pe.wait_ge(s_den, u)
                for t in range(NT):
                    mm = pe.matmul(bank_kv[:, t * 128:(t + 1) * 128], xT[:, b, t * 128:(t + 1) * 128],
                                   w_qkv[:, 2, :], start=True, stop=True)
                mm.then_inc(pe_v, 1)

            def keys_to_tokens(l, b):
                u = unit(l, b)
                pe.wait_ge(s_k, u + 1)
                if u:
                    pe.wait_ge(s_x1T, u)
                transpose4(bank_tr, kT[:, :].rearrange("p (t d) -> p t d", d=128)).then_inc(pe_kT, 1)

            def norm1_to_features(l, b):
                m = unit(l, b)
                pe.wait_ge(s_ktm, m + 1)
                for t in range(NT):
                    pe.wait_ge(s_z1, NT * m + t + 1)
                    mm = pe.transpose(bank_tr[:, t * 128:(t + 1) * 128], z1[:, t, :], ident[:, :])
                mm.then_inc(pe_z1T, 1)

            def mlp_up(l, b, other):
                m = unit(l, b)
                if b == 0:
                    pe.wait_ge(ld_1, 48 * (l + 1))
                pe.wait_ge(s_x1T, m + 1)
                for f in range(NF):
                    if f < 2:
                        pe.wait_ge(s_p, 4 * (m + 1))
                    else:
                        pe.wait_ge(s_h, NF * m + f - 1)
                    pe.matmul(bank_s[f % 2][:, :], w_1[:, f * 128:(f + 1) * 128], x1T[:, :],
                              start=True, stop=True).then_inc(pe_h, 1)
                    if f == 1:
                        keys_to_tokens(*other)

            def last_mlp(l, b):
                m = unit(l, b)
                pe.wait_ge(s_x1T, m + 1)
                pe.wait_ge(s_p, 4 * (m + 1))
                pe.wait_ge(s_y2, m)
                for f in range(NF + 1):
                    if f < NF:
                        if f >= 2:
                            pe.wait_ge(s_h, NF * m + f - 1)
                        pe.matmul(bank_s[f % 2][:, :], w_1[:, f * 128:(f + 1) * 128], x1T[:, :],
                                  start=True, stop=True).then_inc(pe_h, 1)
                    if f:
                        pe.wait_ge(s_h, NF * m + f)
                        for t in range(NT):
                            mm = pe.matmul(bank_tm[:, t * 128:(t + 1) * 128],
                                           hidden[:, f - 1, t * 128:(t + 1) * 128], w_2[:, f - 1, :],
                                           start=(f == 1 and t == 0), stop=(f == NF), skip_group_check=True)
                mm.then_inc(pe_y2, 1)

            def states(l, b):
                u = unit(l, b)
                pe.wait_ge(s_v, u + 1)
                pe.wait_ge(s_ktm, u + 1)
                pe.wait_ge(s_vb, 4 * (u + 1))
                kv_out = bank_kv[:, :].rearrange("p (c t r) -> p t r c", t=NT, r=4)
                for t in range(NT):
                    for j in range(4):
                        q = slice(32 * j, 32 * j + 32)
                        mm = pe.matmul(kv_out[q, t, :, :], keys_tm[:, t, q], v_blk[:, t, :, q],
                                       start=True, stop=True, skip_group_check=True)
                mm.then_inc(pe_kv, 1)

            def scores(l, b):
                u = unit(l, b)
                pe.wait_ge(s_kg, 3 * (u + 1))
                pe.wait_ge(s_kp, u + 1)
                pe.wait_ge(s_qj, 4 * (u + 1))
                for c4 in range(4):
                    if c4 < 2 and u:
                        pe.wait_ge(s_h, NF * (u - 1) + 3 + c4)
                    if c4 == 2:
                        pe.wait_ge(s_kl, u + 1)
                    if c4 == 3:
                        pe.wait_ge(s_p, 4 * u + 1)
                    for i in range(4):
                        n = 4 * c4 + i
                        mm = pe.matmul(score_bank(c4)[:, i * 128:(i + 1) * 128], keys_g[:, n, :, :],
                                       queries_j[:, n, :, :], start=True, stop=True)
                    mm.then_inc(pe_s, 1)

            def denominators(l, b):
                u = unit(l, b)
                pe.wait_ge(s_qk, u + 1)
                pe.wait_ge(s_kv, u + 1)
                for t in range(NT):
                    mm = pe.matmul(bank_kv[:, t * HEADS:(t + 1) * HEADS], qk_sum[:, t * 128:(t + 1) * 128],
                                   of_head[:, :], start=True, stop=True)
                mm.then_inc(pe_den, 1)

            def mlp_down(l, b, first, last):
                m = unit(l, b)
                if first == 0:
                    if b == 0:
                        pe.wait_ge(ld_2, 16 * (l + 1))
                    pe.wait_ge(s_h, NF * (m + 1))
                    if m:
                        pe.wait_ge(s_y2, m)
                for t in range(first, last):
                    for f in range(NF):
                        mm = pe.matmul(bank_tm[:, t * 128:(t + 1) * 128], hidden[:, f, t * 128:(t + 1) * 128],
                                       w_2[:, f, :], start=(f == 0), stop=(f == NF - 1))
                if last == NT:
                    mm.then_inc(pe_y2, 1)

            def attend_before(l, b):
                u = unit(l, b)
                if u:
                    pe.wait_ge(s_y1, u)
                if 3 <= u < UNITS - B + 3:
                    pe.wait_ge(s_xT, B + u - 2)
                pe.wait_ge(s_sblk, 4 * (u + 1))
                for n in range(1, NC):
                    r = n % 4
                    mm = pe.matmul(tiles(bank_o)[32 * r:32 * r + 32, n // 4, :], qT[:, n * C:(n + 1) * C],
                                   state_blk[:, n - 1, :], start=(n <= 4), stop=False, skip_group_check=True)

            def attend_within(l, b):
                u = unit(l, b)
                pe.wait_ge(s_vg, 8 * (u + 1))
                pe.wait_ge(s_vd, 8 * (u + 1))
                for t in range(NT):
                    pe.wait_ge(s_p, 4 * u + t + 1)
                    for j in range(4):
                        q = slice(32 * j, 32 * j + 32)
                        for r in range(4):
                            n = 4 * t + r
                            mm = pe.matmul(tiles(bank_o)[32 * r:32 * r + 32, t, q], probs[:, n, q],
                                           values_g[:, n, j, :, :], start=False, stop=True,
                                           skip_group_check=True)
                mm.then_inc(pe_o, 1)

            def attention_to_features(l, b):
                u = unit(l, b)
                pe.wait_ge(s_att, u + 1)
                pe.wait_ge(s_ql, u + 1)
                transpose4(bank_q, att).then_inc(pe_aT, 1)

            def back_to_features(l, b):
                m = unit(l, b)
                pe.wait_ge(s_z2, NT * (m + 1))
                pe.wait_ge(s_y1, m + 3)
                transpose4(bank_o, z2).then_inc(pe_z2T, 1)

            def output(l, b):
                u = unit(l, b)
                if b == 0:
                    pe.wait_ge(ld_o, 16 * (l + 1))
                pe.wait_ge(s_aT, u + 1)
                pe.wait_ge(s_att, u + 1)
                for t in range(NT):
                    mm = pe.matmul(bank_o[:, t * 128:(t + 1) * 128], attT[:, t * 128:(t + 1) * 128],
                                   w_o[:, :], start=True, stop=True)
                mm.then_inc(pe_wo, 1)

            for b in range(B):
                if b == B - 1:
                    pe.wait_ge(s_xT, 2)
                    pe.wait_ge(v_y, B + 1)
                    project_queries_keys(0, 0)
                    project_values(0, 0)
                normalised(2 * B + b + 1)
                transpose4(banks[b], x2[:, b]).then_inc(p_x2, 1)
            pe.wait_ge(v_y, 2 * B)
            pe.wait_ge(s_xT, B)
            pe.wait_ge(c_wide, 5)
            for u in range(UNITS):
                now, before = of_unit(u), of_unit(u - 1)
                if u:
                    project_queries_keys(*now)
                    norm1_to_features(*before)
                    project_values(*now)
                if 3 <= u < UNITS - B + 3:
                    back_to_features(*of_unit(u - 3))
                if u:
                    mlp_up(*before, now)
                else:
                    keys_to_tokens(*now)
                states(*now)
                scores(*now)
                attend_before(*now)
                denominators(*now)
                attend_within(*now)
                if u:
                    mlp_down(*before, 0, 1)
                attention_to_features(*now)
                if u:
                    mlp_down(*before, 1, 2)
                output(*now)
                if u:
                    mlp_down(*before, 2, NT)
            norm1_to_features(*of_unit(UNITS - 1))
            last_mlp(*of_unit(UNITS - 1))

            pe.wait_ge(s_y1, UNITS)
            pe.wait_ge(s_x1T, UNITS)
            pe.wait_ge(s_h, NF * UNITS)
            pe.wait_ge(ld_r0, 32)

            def x3_to_columns(b):
                if b >= 2:
                    pe.wait_ge(a_x3, b - 1)
                pe.wait_ge(f_x3[b], NT)
                transpose4(banks[b % 2], x2[:, b]).then_inc(pe_x3, 1)

            def expert_logits(b):
                pe.wait_ge(a_x3, b + 1)
                for t in range(NT):
                    n = b * NT + t
                    mm = pe.matmul(banks[4][:, n * E:(n + 1) * E], xT[:, b, t * 128:(t + 1) * 128],
                                   gate_w[:, :], start=True, stop=True)
                return mm

            x3_to_columns(0)
            x3_to_columns(1)
            expert_logits(0)
            x3_to_columns(2)
            expert_logits(1)
            x3_to_columns(3)
            expert_logits(2)
            expert_logits(3).then_inc(pe_lg, 1)
            pe.wait_ge(m_gate, 5)
            for i in range(NT // 2):
                mm = pe.transpose(banks[5][0:64, i * 128:(i + 1) * 128],
                                  gate_t[:, 2 * i:2 * i + 2, :].rearrange("p t k -> p (t k)"), ident[:, :])
            mm.then_inc(pe_gt, 1)
            for t in range(NT):
                mm = pe.transpose(banks[7][0:32, t * 128:(t + 1) * 128], gate_t[:, t, :], ident[:, :])
            mm.then_inc(pe_gt, 1)
            pe.wait_ge(m_rank, 2 * ROUNDS + 10)
            for t in range(NT):
                mm = pe.transpose(banks[6][:, t * 32:(t + 1) * 32], rank_b[:, t * 128:(t + 1) * 128],
                                  ident[0:32, 0:32])
            mm.then_inc(pe_pt, 1)
            pe.wait_ge(g_xl, B + 1)
            for b in range(B):
                for t in range(NT):
                    n = b * NT + t
                    pe.wait_ge(m_pick, n + 1)
                    if t == 0 and b >= 2:
                        pe.wait_ge(m_xg, 2 * (b - 1))
                    for h in range(2):
                        for i in range(PARTS):
                            mm = pe.matmul(banks[2 * (b % 2) + h][:, :], x_parts[i][:, b, t, :],
                                           pick[n % RING][:, h * 512:(h + 1) * 512],
                                           start=(t == 0 and i == 0), stop=(t == NT - 1 and i == PARTS - 1),
                                           skip_group_check=True)
                    mm.then_inc(pe_g, 1)
                    for e in range(E):
                        k = b * E + e
                        pe.matmul(banks[6][:, PARTS * k:PARTS * (k + 1)],
                                  pick[n % RING][:, e * 128:(e + 1) * 128],
                                  gate_parts[:, :, t * B * E + k], start=(n == 0 and e == 0),
                                  stop=(t == NT - 1), skip_group_check=True)
                    if n >= 2:
                        pe.wait_ge(a_pt, n - 1)
                    for e in range(E):
                        mm = pe.transpose(banks[4 + n % 2][:, :].bitcast(bf16)[:, e * 128:(e + 1) * 128],
                                          pick[n % RING][:, e * 128:(e + 1) * 128], ident_bf[:, :])
                    mm.then_inc(pe_pick, 1)

            def expert_up(e):
                for f in range(NF):
                    n = e * NF + f
                    if n == 0:
                        pe.wait_ge(m_xg, 2 * B - 1)
                    if n == E // 2 * NF:
                        pe.wait_ge(m_xg, 2 * B)
                    if n < 2:
                        pe.wait_ge(a_pt, B * NT - 1 + n)
                    else:
                        pe.wait_ge(a_u, n - 1)
                    pe.matmul(banks[4 + n % 2][:, :], we_1[:, e, f * 128:(f + 1) * 128], xg(e),
                              start=True, stop=True).then_inc(pe_u, 1)

            def expert_down(e):
                pe.wait_ge(a_u, NF * (e + 1))
                if e == 0:
                    pe.wait_ge(m_gs, 1)
                if e >= 2:
                    pe.wait_ge(m_y, e - 1)
                for b in range(B):
                    for f in range(NF):
                        mm = pe.matmul(banks[6 + e % 2][:, b * 128:(b + 1) * 128],
                                       h_e(e)[:, f, b * 128:(b + 1) * 128], we_2[:, e, f, :],
                                       start=(f == 0), stop=(f == NF - 1))
                mm.then_inc(pe_d, 1)

            def scatter(e):
                pe.wait_ge(m_yl, e + 1)
                for b in range(B):
                    if e == E - 1 and b == B // 2:
                        pe.wait_ge(m_yl, E + 1)
                    for t in range(NT):
                        for i in range(PARTS):
                            mm = pe.matmul(banks[b][:, t * 128:(t + 1) * 128], pick_t[b * NT + t][:, e, :],
                                           y_parts[:, e % 2, i, b, :],
                                           start=(e == 0 and t == 0 and i == 0),
                                           stop=(e == E - 1 and i == PARTS - 1), skip_group_check=True)
                    mm.then_inc(pe_sc, 1)

            pe.wait_ge(ld_e, 32)
            for e in range(E + 2):
                if e < E:
                    expert_up(e)
                if 1 <= e <= E:
                    expert_down(e - 1)
                if e >= 2:
                    scatter(e - 2)

        @block.scalar
        def _(act):
            def rstd(mv, lv, rs, ready, count, s_lv, s_rs, n):
                act.wait_ge(ready, count)
                act.activation(lv, mv, ACT.Ln, bias=ln_eps[:, 0:1]).then_inc(s_lv, 1)
                act.wait_ge(s_lv, n)
                act.activation(rs, lv, ACT.Exp, scale=-0.5).then_inc(s_rs, 1)

            act.preload_act_table_set(LN_EXP)
            act.wait_ge(c_set, 1)

            def norm0(k, dst, src, then, *more):
                for i in range(B + 1 + len((then,) + more)):
                    if i < B:
                        rstd(mv0[:, i, :, 1], lv0[:, i, :], rs0[:, i, :], d_mv, NT * (k * B + i + 1), d_lv, d_rs,
                             k * B + i + 1)
                    if 0 <= i - 1 < B:
                        b = i - 1
                        act.wait_ge(d_nm, k * B + b + 1)
                        for t in range(2, NT):
                            act.activation(dst[:, b, t, :], src[:, b, t, :], ACT.Identity,
                                           bias=shift0[:, b, t:t + 1], scale=rs0[:, b, t:t + 1]).then_inc(d_za, 1)
                    for j, step in enumerate((then,) + more):
                        if 0 <= i - 2 - j < B:
                            step(i - 2 - j)

            def hidden_to_features(b):
                if b == 0:
                    act.wait_ge(ld_c0, 16)
                act.wait_ge(p_zT, b + 1)
                act.activation(hT[:, b], banks[b][:, :], ACT.Identity, bias=cols0[:, 1:2],
                               scale=cols0[:, 0:1]).then_inc(a_hT, 1)

            def x1_to_features(b):
                act.wait_ge(p_x1, b + 1)
                act.activation(xT[:, b, :], banks[4 + b][:, :], ACT.Copy).then_inc(a_x1T, 1)

            def ffn_scale(b):
                act.wait_ge(p_ff, b + 1)
                act.activation(ffn0[:, b, :], banks[b][:, :], ACT.Identity, bias=cols0[:, 6:7],
                               scale=cols0[:, 5:6]).then_inc(a_ff, 1)

            def x2_to_features(b):
                act.wait_ge(p_x2, b + 1)
                act.activation(xT[:, b, :], banks[b][:, :], ACT.Copy).then_inc(s_xT, 1)

            norm0(0, z0, x_in, hidden_to_features)
            for b in range(B):
                act.wait_ge(p_k, b + 1)
                act.activation(keys0[:, b, :], banks[4 + b][:, :], ACT.Identity, bias=cols0[:, 2:3])\
                    .then_inc(a_key, 1)
            act.wait_ge(v_bka, 1)
            for i in range(B + 2):
                if i < B:
                    act.wait_ge(p_ka, i + 1)
                    act.activation(ka0[:, i], banks[4 + i][:, :], ACT.Identity, bias=bka_s[:, 0:1],
                                   scale=float(D) ** -0.5).then_inc(a_ka, 1)
                    act.wait_ge(a_ka, i + 1)
                    act.activation(kw0[:, i], ka0[:, i], ACT.Exp).then_inc(a_ew, 1)
                if 1 <= i <= B:
                    act.wait_ge(v_cum, i)
                    act.activation(cum0[:, i - 1], cum0[:, i - 1], ACT.Ln).then_inc(a_lc, 1)
                if i >= 2:
                    act.wait_ge(v_t, i - 1)
                    act.activation(kw0[:, i - 2], ka0[:, i - 2], ACT.Exp).then_inc(a_kw, 1)
            norm0(1, res, x_in, x1_to_features, ffn_scale)
            def norm1(l, b):
                m = unit(l, b)
                rstd(mv1[:, :, 1], lv1[:, :], rs1[:, :], s_mv1, NT * (m + 1), s_lv1, s_rs1, m + 1)

            def feature_map_exp(l, b):
                u = unit(l, b)
                if b == 0:
                    act.wait_ge(ld_a, 48 * (l + 1))
                act.wait_ge(pe_q, u + 1)
                act.activation(q_exp[:, :], bank_q[:, :], ACT.Exp, bias=cols_a[:, 0:1]).then_inc(s_qe, 1)
                act.wait_ge(pe_k, u + 1)
                act.activation(k_exp[:, :], bank_k[:, :], ACT.Exp, bias=cols_a[:, 1:2]).then_inc(s_ke, 1)

            def x2_then_features(b):
                if b == B - 1:
                    feature_map_exp(0, 0)
                x2_to_features(b)

            norm0(2, x2, x_in, x2_then_features)

            def norm1_to_features(l, b):
                m = unit(l, b)
                if b == 0:
                    act.wait_ge(ld_1, 48 * (l + 1))
                act.wait_ge(pe_z1T, m + 1)
                act.activation(x1T[:, :], bank_tr[:, :], ACT.Identity, bias=cols_1[:, 1:2],
                               scale=cols_1[:, 0:1]).then_inc(s_x1T, 1)

            def gelu(l, b, f):
                m = unit(l, b)
                act.wait_ge(pe_h, NF * m + f + 1)
                act.activation(hidden[:, f, :], bank_s[f % 2][:, :], ACT.Gelu, bias=cols_1[:, 2 + f:3 + f])\
                    .then_inc(s_h, 1)

            def spread_queries(l, b, j):
                act.wait_ge(s_q, unit(l, b) + 1)
                q = slice(32 * j, 32 * j + 32)
                act.activation(queries_j[q, :, j, :], qT[q, :].rearrange("p (n c) -> p n c", c=C),
                               ACT.Copy).then_inc(s_qj, 1)

            def spread_state(l, b):
                act.wait_ge(s_st, unit(l, b) + 1)
                for j in range(4):
                    q = slice(32 * j, 32 * j + 32)
                    act.activation(state_blk[q, :, q], state[q, :, :].rearrange("p c n -> p n c"),
                                   ACT.Copy).then_inc(s_sblk, 1)

            def attention_to_features(l, b):
                act.wait_ge(pe_aT, unit(l, b) + 1)
                act.activation(attT[:, :], bank_q[:, :], ACT.Copy).then_inc(s_aT, 1)

            def norm2(l, b):
                m = unit(l, b)
                rstd(mv2[:, :, 1], lv2[:, :], rs2[:, :], s_mv2, NT * (m + 1), s_lv2, s_rs2, m + 1)

            def norm2_to_features(l, b):
                m = unit(l, b)
                if b == 0:
                    act.wait_ge(ld_2v, 32 * (l + 1))
                act.wait_ge(pe_z2T, m + 1)
                act.activation(xT[:, b, :], bank_o[:, :], ACT.Identity, bias=cols_2[:, 1:2],
                               scale=cols_2[:, 0:1]).then_inc(s_xT, 1)

            def final_rstd(n):
                b = final_order[n][0] if n < 2 * B else n - 2 * B
                act.wait_ge(f_mv, NT * (n + 1))
                act.activation(lv0[:, b, :], mv0[:, b, :, 1], ACT.Ln, bias=ln_eps[:, 0:1]).then_inc(f_lv, 1)
                act.wait_ge(f_lv, n - by_pool + 1)
                act.activation(rs0[:, b, :], lv0[:, b, :], ACT.Exp, scale=-0.5).then_inc(f_ra, 1)

            def x3_to_features(b):
                act.wait_ge(pe_x3, b + 1)
                act.activation(xT[:, b, :], banks[b % 2][:, :], ACT.Copy).then_inc(a_x3, 1)

            def final_norm(b):
                act.wait_ge(f_nm, b + 1)
                for t in range(NT):
                    act.activation(x2[:, b, t, :], res[:, b, t, :], ACT.Identity, bias=shift0[:, b, t:t + 1],
                                   scale=rs0[:, b, t:t + 1]).then_inc(f_x3[b], 1)

            act.wait_ge(c_wide, 5)
            for u in range(UNITS + 2):
                now, before, old = of_unit(u), of_unit(u - 1), of_unit(u - 2)
                if 1 <= u <= UNITS:
                    norm1(*before)
                if 1 <= u < UNITS:
                    feature_map_exp(*now)
                if 1 <= u <= UNITS:
                    norm1_to_features(*before)
                if u == UNITS:
                    norm2(*old)
                for f in range(NF):
                    if f == 2 and u < UNITS:
                        spread_queries(*now, 2)
                    if f == 3 and u < UNITS:
                        spread_queries(*now, 3)
                    if 1 <= u <= UNITS:
                        gelu(*before, f)
                    if f < 2 and u < UNITS:
                        spread_queries(*now, f)
                if 3 <= u < UNITS - B + 3:
                    norm2_to_features(*of_unit(u - 3))
                if u < UNITS:
                    spread_state(*now)
                if 1 <= u <= UNITS:
                    act.preload_act_table_set(LN_EXP)
                if u == UNITS + 1:
                    final_norm(0)
                if u >= 2 and u != UNITS:
                    norm2(*old)
                if u < UNITS:
                    attention_to_features(*now)

            final_norm(1)
            final_rstd(5)
            x3_to_features(0)
            x3_to_features(1)
            final_rstd(6)
            final_norm(2)
            final_rstd(7)
            x3_to_features(2)
            x3_to_features(3)
            act.wait_ge(m_gate, 2)
            act.activation(gate_e[:, :, :, :], gate_e[:, :, :, :], ACT.Exp).then_inc(a_gate, 1)
            for b in range(B + 1):
                if b == B:
                    act.wait_ge(m_gate, 5)
                    act.activation(gate_parts[:, 0, :], gate_flat, ACT.Copy).then_inc(a_xh, 1)
                else:
                    act.wait_ge(f_x3[b], NT)
                    if b == 0:
                        act.wait_ge(pe_o, UNITS)
                    act.activation(x_parts[0][:, b], x2[:, b], ACT.Copy).then_inc(a_xh, 1)
            for b in range(B + 1):
                act.wait_ge(g_xr, b + 1)
                if b == B:
                    act.activation(gate_parts[:, 1, :], gate_rest[:, :], ACT.Copy).then_inc(a_xm, 1)
                else:
                    act.activation(x_parts[1][:, b], x_rest[:, b], ACT.Copy).then_inc(a_xm, 1)
            act.preload_act_table_set("gelu_and_others")
            for n in range(B * NT):
                act.wait_ge(pe_pick, n + 1)
                act.activation(pick_t[n], banks[4 + n % 2][:, :].bitcast(bf16).rearrange("p (e k) -> p e k", e=E),
                               ACT.Copy).then_inc(a_pt, 1)
            for e in range(E):
                for f in range(NF):
                    n = e * NF + f
                    act.wait_ge(pe_u, n + 1)
                    if e >= 2 and f == 0:
                        act.wait_ge(pe_d, e - 1)
                    act.activation(h_e(e)[:, f, :], banks[4 + n % 2][:, :], ACT.Gelu).then_inc(a_u, 1)
            act.preload_act_table_set(LN_EXP)
            for b in range(B):
                final_rstd(2 * B + b)
                if b < B - 1:
                    act.wait_ge(f_nm, B + b)
                    for t in range(NT):
                        act.activation(res[:, b, t, :], res[:, b, t, :], ACT.Identity,
                                       bias=shift0[:, b, t:t + 1], scale=rs0[:, b, t:t + 1]).then_inc(f_za, 1)

        @block.vector
        def _(dve):
            def stats(src, bn, mv, s_bn, s_mv, n):
                for t in range(NT):
                    dve.bn_stats(bn[:, t, :], src[:, t, :]).then_inc(s_bn, 1)
                for t in range(NT):
                    dve.wait_ge(s_bn, NT * (n - 1) + t + 1)
                    dve.bn_aggr(mv[:, t, :], bn[:, t, :]).then_inc(s_mv, 1)

            def normalise(dst, src, mv, rs, s_rs, s_z, n):
                dve.wait_ge(s_rs, n)
                for t in range(NT):
                    dve.tensor_scalar(dst[:, t, :], src[:, t, :], mv[:, t, 0:1], rs[:, t:t + 1],
                                      ALU.subtract, ALU.mult).then_inc(s_z, 1)

            def norm0(dst, src, b, n):
                dve.wait_ge(d_rs, n)
                if n > B:
                    dve.wait_ge(d_za, 2 * (n - B))
                dve.scalar_tensor_tensor(out=shift0[:, b, :], in0=mv0[:, b, :, 0], scalar=-1.0,
                                         in1=rs0[:, b, :], op0=ALU.mult, op1=ALU.mult).then_inc(d_nm, 1)
                for t in range(2):
                    dve.tensor_scalar(dst[:, b, t, :], src[:, b, t, :], mv0[:, b, t, 0:1], rs0[:, b, t:t + 1],
                                      ALU.subtract, ALU.mult).then_inc(d_z, 1)

            for b in range(B + 1):
                if b < B:
                    dve.wait_ge(ld_x[b], 16)
                    stats(x_in[:, b], bn0[:, b], mv0[:, b], d_bn, d_mv, b + 1)
                if b:
                    norm0(z0, x_in, b - 1, b)
            dve.wait_ge(ld_c0, 16)
            dve.tensor_scalar(bka_s[:, :], cols0[:, 4:5], float(D) ** -0.5, None, ALU.mult).then_inc(v_bka, 1)
            dve.wait_ge(ld_w0, 16)
            dve.tensor_scalar(w0_sign[:, :], w0[:, 3, :], 0.0, 2.0, ALU.is_ge, ALU.mult).then_inc(v_sgn, 1)
            dve.wait_ge(v_sgn, 1)
            dve.tensor_scalar(w0_sign[:, :], w0_sign[:, :], -1.0, None, ALU.add).then_inc(v_sgn, 1)
            dve.wait_ge(c_set, 3)
            for i in range(B + 2):
                if i < B:
                    dve.wait_ge(a_ew, i + 1)
                    dve.tensor_tensor_scan(cum0[:, i], one_row, kw0[:, i], 0.0, ALU.mult, ALU.add)\
                        .then_inc(v_cum, 1)
                    dve.wait_ge(p_v, i + 1)
                    dve.tensor_scalar(vals0[:, i, :], banks[i][:, :], cols0[:, 3:4], None, ALU.add)\
                        .then_inc(v_val, 1)
                if 1 <= i <= B:
                    dve.wait_ge(a_lc, i)
                    dve.tensor_tensor(ka0[:, i - 1], ka0[:, i - 1], cum0[:, i - 1], ALU.subtract).then_inc(v_t, 1)
                if i >= 2:
                    b = i - 2
                    dve.wait_ge(a_kw, b + 1)
                    dve.tensor_tensor(kw0[:, b], kw0[:, b], keys0[:, b, :], ALU.mult).then_inc(v_pk, 1)
                    dve.wait_ge(v_pk, b + 1)
                    dve.tensor_tensor_scan(cum0[:, b], one_row, kw0[:, b], 0.0, ALU.mult, ALU.add)\
                        .then_inc(v_pool, 1)
            for b in range(B + 1):
                if b < B:
                    dve.wait_ge(p_yT, b + 1)
                    dve.tensor_tensor(x_in[:, b, :, :], tiles(banks[b]), x_in[:, b, :, :], ALU.add)\
                        .then_inc(v_y, 1)
                    dve.wait_ge(v_y, b + 1)
                    stats(x_in[:, b], bn0[:, b], mv0[:, b], d_bn, d_mv, B + b + 1)
                if b:
                    norm0(res, x_in, b - 1, B + b)
            for i in range(B + 2):
                if i < B:
                    dve.wait_ge(a_ff, i + 1)
                    dve.tensor_scalar(ffn0[:, i, :], ffn0[:, i, :], -MAX_VAL, MAX_VAL, ALU.max, ALU.min)\
                        .then_inc(v_cl, 1)
                if 1 <= i <= B:
                    b = i - 1
                    dve.wait_ge(p_fT, b + 1)
                    dve.tensor_tensor(x_in[:, b, :, :], tiles(banks[4 + b]), res[:, b, :, :], ALU.add)\
                        .then_inc(v_y, 1)
                    dve.wait_ge(v_y, B + b + 1)
                    stats(x_in[:, b], bn0[:, b], mv0[:, b], d_bn, d_mv, 2 * B + b + 1)
                if i >= 2:
                    norm0(x2, x_in, i - 2, 2 * B + i - 1)

            def norm1(l, b):
                m = unit(l, b)
                dve.wait_ge(pe_wo, m + 1)
                dve.wait_ge(s_res, m + 1)
                dve.tensor_tensor(y1[:, :, :], tiles(bank_o), res[:, b, :, :], ALU.add).then_inc(s_y1, 1)
                dve.wait_ge(s_y1, m + 1)
                stats(y1, bn1, mv1, s_bn1, s_mv1, m + 1)
                if m:
                    dve.wait_ge(s_r1m, m)
                normalise(z1, y1, mv1, rs1, s_rs1, s_z1, m + 1)

            def feature_map(l, b):
                u = unit(l, b)
                if b == 0:
                    dve.wait_ge(ld_a, 48 * (l + 1))
                dve.wait_ge(s_qe, u + 1)
                dve.tensor_scalar(q_lin[:, :], bank_q[:, :], cols_a[:, 0:1], 0.0, ALU.add, ALU.max)\
                    .then_inc(s_ql, 1)
                dve.wait_ge(s_ke, u + 1)
                dve.tensor_scalar(k_lin[:, :], bank_k[:, :], cols_a[:, 1:2], 0.0, ALU.add, ALU.max)\
                    .then_inc(s_kl, 1)
                dve.wait_ge(s_ql, u + 1)
                dve.scalar_tensor_tensor(out=qT[:, :], in0=q_exp[:, :], scalar=1.0, in1=q_lin[:, :],
                                         op0=ALU.min, op1=ALU.add).then_inc(s_q, 1)
                dve.wait_ge(s_kl, u + 1)
                dve.scalar_tensor_tensor(out=kT[:, :], in0=k_exp[:, :], scalar=1.0, in1=k_lin[:, :],
                                         op0=ALU.min, op1=ALU.add).then_inc(s_k, 1)

            def bias_values(l, b):
                u = unit(l, b)
                dve.wait_ge(pe_v, u + 1)
                if u:
                    dve.wait_ge(s_vg, 8 * u)
                dve.tensor_tensor(v_tm[:, :, :], tiles(bank_kv), over_tiles(row_v[:, :]), ALU.add)\
                    .then_inc(s_v, 1)
                dve.wait_ge(s_v, u + 1)
                for r in range(4):
                    q = slice(32 * r, 32 * r + 32)
                    dve.tensor_copy(v_blk[q, :, r, :], v_tm[q, :, :]).then_inc(s_vb, 1)

            def spread_keys(l, b):
                u = unit(l, b)
                dve.wait_ge(s_k, u + 1)
                for g in range(3):
                    dve.tensor_scalar(keys_g[:, :, g, :], kT[:, :].rearrange("p (n c) -> p n c", c=C),
                                      same_g[:, g:g + 1], None, ALU.mult).then_inc(s_kg, 1)

            def sum_keys(l, b):
                u = unit(l, b)
                dve.tensor_tensor_scan(k_sum[:, :], one_row, kT[:, :], 0.0, ALU.mult, ALU.add)\
                    .then_inc(s_ks, 1)

            def keys_to_tokens(l, b):
                u = unit(l, b)
                dve.wait_ge(pe_kT, u + 1)
                dve.tensor_copy(keys_tm[:, :, :], tiles(bank_tr)).then_inc(s_ktm, 1)

            def prefix_states(l, b):
                u = unit(l, b)
                dve.wait_ge(pe_kv, u + 1)
                dve.tensor_tensor(kv[:, :, :], bank_kv[:, :].rearrange("p (c n) -> p c n", n=NC),
                                  same_g_wide[:, :, :], ALU.mult).then_inc(s_kv, 1)
                dve.wait_ge(s_kv, u + 1)
                dve.tensor_tensor_scan(state[:, :, :].rearrange("p c n -> p (c n)"),
                                       scan_keep[:, :, :].rearrange("p c n -> p (c n)"),
                                       kv[:, :, :].rearrange("p c n -> p (c n)"),
                                       0.0, ALU.mult, ALU.add).then_inc(s_st, 1)

            def mask_scores(l, b, first, last):
                u = unit(l, b)
                for c4 in range(first, last):
                    dve.wait_ge(pe_s, 4 * u + c4 + 1)
                    dve.tensor_tensor(probs[:, 4 * c4:4 * c4 + 4, :], tiles(score_bank(c4)),
                                      causal[:, :, :], ALU.mult).then_inc(s_p, 1)
                    for k in range(4 * (c4 - 2), 4 * (c4 - 1)) if c4 >= 2 else ():
                        spread_values(dve, 2 + k // 4, k % 4).then_inc(s_vd, 1)

            def residual_sum2(l, b):
                m = unit(l, b)
                dve.wait_ge(pe_y2, m + 1)
                dve.wait_ge(s_r1, m + 1)
                if m:
                    dve.wait_ge(s_z2, NT * m)
                dve.tensor_tensor(y2[:, :, :], tiles(bank_tm), res1[:, :, :], ALU.add).then_inc(s_y2, 1)
                dve.wait_ge(s_y2, m + 1)
                stats(y2, bn2, mv2, s_bn2, s_mv2, m + 1)

            def norm2(l, b):
                m = unit(l, b)
                if m:
                    dve.wait_ge(s_res, B + m)
                normalise(z2, y2, mv2, rs2, s_rs2, s_z2, m + 1)

            def invert_denominators(l, b):
                u = unit(l, b)
                dve.wait_ge(pe_den, u + 1)
                dve.tensor_scalar(den[:, :], bank_kv[:, 0:NT * HEADS], ATT_EPS, None, ALU.add).then_inc(s_den, 1)
                dve.wait_ge(s_den, u + 1)
                dve.reciprocal(inv_den[:, :], den[:, :]).then_inc(s_inv, 1)

            def divide(l, b):
                u = unit(l, b)
                dve.wait_ge(pe_o, u + 1)
                dve.wait_ge(s_inv, u + 1)
                dve.tensor_tensor(att[:, :, :].rearrange("p t (h e) -> p (t h) e", e=HD),
                                  bank_o[:, :].rearrange("p (n e) -> p n e", e=HD),
                                  inv_den[:, :].unsqueeze(2).broadcast_to([128, NT * HEADS, HD]), ALU.mult)\
                    .then_inc(s_att, 1)

            def wait_final_rstd(n):
                if n < by_pool:
                    dve.wait_ge(f_rs, n + 1)
                else:
                    dve.wait_ge(f_ra, n - by_pool + 1)

            def final_stats(b):
                dve.wait_ge(s_res, UNITS + b + 1)
                stats(res[:, b], bn0[:, b], mv0[:, b], f_bn, f_mv, final_no(b, 0) + 1)

            def final_centre(b):
                for t in range(NT):
                    dve.wait_ge(f_mv, NT * final_no(b, 0) + t + 1)
                    dve.scalar_tensor_tensor(out=res[:, b, t, :], in0=res[:, b, t, :], scalar=mv0[:, b, t, 0:1],
                                             in1=rows0[:, 1, :], op0=ALU.subtract, op1=ALU.mult).then_inc(f_g, 1)

            def final_sum(b):
                wait_final_rstd(final_no(b, 0))
                dve.wait_ge(f_b, b + 1)
                for t in range(NT):
                    dve.wait_ge(f_g, NT * b + t + 1)
                    dve.scalar_tensor_tensor(out=res[:, b, t, :], in0=res[:, b, t, :], scalar=rs0[:, b, t:t + 1],
                                             in1=x2[:, b, t, :], op0=ALU.mult, op1=ALU.add).then_inc(f_y, 1)
                dve.wait_ge(f_y, NT * (b + 1))
                stats(res[:, b], bn0[:, b], mv0[:, b], f_bn, f_mv, final_no(b, 1) + 1)

            def final_norm(b):
                wait_final_rstd(final_no(b, 1))
                if b < B - 1:
                    dve.scalar_tensor_tensor(out=shift0[:, b, :], in0=mv0[:, b, :, 0], scalar=-1.0,
                                             in1=rs0[:, b, :], op0=ALU.mult, op1=ALU.mult).then_inc(f_nm, 1)
                    return
                for t in range(NT):
                    dve.tensor_scalar(x2[:, b, t, :], res[:, b, t, :], mv0[:, b, t, 0:1], rs0[:, b, t:t + 1],
                                      ALU.subtract, ALU.mult).then_inc(f_x3[b], 1)

            for u in range(UNITS + 2):
                now, before, old = of_unit(u), of_unit(u - 1), of_unit(u - 2)
                if 1 <= u <= UNITS:
                    norm1(*before)
                if u < UNITS:
                    feature_map(*now)
                    bias_values(*now)
                    keys_to_tokens(*now)
                    spread_keys(*now)
                    prefix_states(*now)
                    mask_scores(*now, 0, 2)
                    sum_keys(*now)
                    mask_scores(*now, 2, 4)
                if u >= 2:
                    residual_sum2(*old)
                if u == UNITS + 1:
                    final_sum(1)
                if u < UNITS:
                    invert_denominators(*now)
                    divide(*now)
                if u == UNITS:
                    final_sum(0)
                if u >= 2:
                    norm2(*old)
                if u == UNITS - 1:
                    final_stats(0)
                    final_centre(0)
                if u == UNITS:
                    final_stats(1)
                    final_centre(1)
                    final_norm(0)
                    final_stats(2)
                    final_centre(2)
            final_norm(1)
            final_sum(2)
            final_norm(2)
            final_stats(3)
            final_centre(3)
            final_sum(3)
            final_norm(3)

            logits = banks[4][:, 0:B * NT * E].rearrange("p (n e) -> p n e", e=E)
            gate_n = gate_e[:, :, :, :].rearrange("p b t e -> p (b t) e")
            dve.wait_ge(pe_lg, 1)
            dve.tensor_reduce(logits_max[:, :], logits, AX.X, ALU.max).then_inc(m_gate, 1)
            dve.wait_ge(m_gate, 1)
            dve.tensor_tensor(gate_n, logits, logits_max[:, :].unsqueeze(2).broadcast_to([128, B * NT, E]),
                              ALU.subtract).then_inc(m_gate, 1)
            dve.wait_ge(a_gate, 1)
            dve.tensor_reduce(gate_sum[:, :], gate_n, AX.X, ALU.add).then_inc(m_gate, 1)
            dve.wait_ge(m_gate, 3)
            dve.reciprocal(gate_inv[:, :], gate_sum[:, :]).then_inc(m_gate, 1)
            dve.wait_ge(m_gate, 4)
            dve.tensor_tensor(gate_t[:, :, :].rearrange("p t (b e) -> p b t e", b=B), gate_e[:, :, :, :],
                              gate_inv[:, :].rearrange("p (b t) -> p b t", b=B).unsqueeze(3)
                              .broadcast_to([128, B, NT, E]), ALU.mult).then_inc(m_gate, 1)
            dve.wait_ge(pe_gt, 1)
            for i in range(ROUNDS):
                left = half_p[:, :] if i else banks[5][0:64, 0:S // 2]
                if i:
                    dve.wait_ge(m_rank, 2 * i)
                dve.max(top_half[:, 8 * i:8 * i + 8], left).then_inc(m_rank, 1)
                if i < ROUNDS - 1:
                    dve.wait_ge(m_rank, 2 * i + 1)
                    dve.match_replace(half_p[:, :], top_half[:, 8 * i:8 * i + 8], left, -1.0).then_inc(m_rank, 1)
            n = 2 * ROUNDS - 1
            dve.wait_ge(m_rank, n)
            dve.tensor_copy(top_all[:, :], top_half[32:64, ::-1]).then_inc(m_rank, 1)
            dve.wait_ge(m_rank, n + 1)
            dve.tensor_tensor(top_all[:, :], top_all[:, :], top_half[0:32, :], ALU.max).then_inc(m_rank, 1)
            dve.wait_ge(m_rank, n + 2)
            dve.tensor_reduce(least[:, :], top_all[:, :], AX.X, ALU.min).then_inc(m_rank, 1)
            gates = banks[7][0:32, :]
            dve.wait_ge(pe_gt, 2)
            dve.wait_ge(m_rank, n + 3)
            dve.tensor_scalar(top_tie[:, :], top_all[:, :], least[:, 0:1], None, ALU.is_equal).then_inc(m_rank, 1)
            dve.tensor_scalar(rank_a[:, :], gates, least[:, 0:1], None, ALU.is_equal).then_inc(m_rank, 1)
            dve.wait_ge(m_rank, n + 4)
            dve.tensor_reduce(ties[:, :], top_tie[:, :], AX.X, ALU.add).then_inc(m_rank, 1)
            dve.wait_ge(m_rank, n + 5)
            dve.tensor_tensor_scan(rank_b[:, :], one_row[0:32], rank_a[:, :], 0.0, ALU.mult, ALU.add)\
                .then_inc(m_rank, 1)
            dve.wait_ge(m_rank, n + 7)
            dve.scalar_tensor_tensor(out=rank_b[:, :], in0=rank_b[:, :], scalar=ties[:, 0:1], in1=rank_a[:, :],
                                     op0=ALU.is_gt, op1=ALU.mult).then_inc(m_rank, 1)
            dve.wait_ge(m_rank, n + 8)
            dve.scalar_tensor_tensor(out=rank_a[:, :], in0=gates, scalar=least[:, 0:1], in1=rank_b[:, :],
                                     op0=ALU.is_ge, op1=ALU.subtract).then_inc(m_rank, 1)
            dve.wait_ge(m_rank, n + 9)
            dve.tensor_tensor_scan(rank_b[:, :], one_row[0:32], rank_a[:, :], 0.0, ALU.mult, ALU.add)\
                .then_inc(m_rank, 1)
            dve.wait_ge(m_rank, n + 10)
            dve.tensor_tensor(rank_b[:, :], rank_b[:, :], rank_a[:, :], ALU.mult).then_inc(m_rank, 1)
            dve.wait_ge(pe_pt, 1)
            dve.tensor_scalar(pos_tm[:, :, :].rearrange("p t n -> p (t n)"), banks[6][:, 0:NT * 32], -1.0,
                              None, ALU.add).then_inc(m_pos, 1)
            dve.wait_ge(m_pos, 1)

            def one_hot(n):
                b, t = n // NT, n % NT
                if n >= RING:
                    dve.wait_ge(pe_pick, n - RING + 1)
                dve.tensor_tensor(pick[n % RING].rearrange("p (e k) -> p e k", e=E),
                                  slot_row[:, :].unsqueeze(1).broadcast_to([128, E, 128]),
                                  pos_tm[:, t, b * E:(b + 1) * E].unsqueeze(2).broadcast_to([128, E, 128]),
                                  ALU.is_equal).then_inc(m_pick, 1)

            def gathered(b):
                dve.wait_ge(pe_g, NT * (b + 1))
                for h in range(2):
                    dve.tensor_copy(xg_a[h].rearrange("p (e s) d -> p e s d", s=4)[:, :, b, :],
                                    tiles(banks[2 * (b % 2) + h])).then_inc(m_xg, 1)

            for n in range(B * NT):
                one_hot(n)
                if n >= RING - 1 and n % NT == NT - 1:
                    gathered(n // NT - 1)
            gathered(B - 1)
            dve.wait_ge(pe_pick, B * NT)
            dve.tensor_reduce(slot_gate[:, :], banks[6][:, 0:B * E * PARTS].rearrange("p (k i) -> p k i", i=PARTS),
                              AX.X, ALU.add).then_inc(m_gs, 1)
            dve.wait_ge(m_gs, 1)
            def weigh_results(e, rows):
                y, parts, rest = y_all[e % 2][:, rows], y_parts[:, e % 2, :, rows], y_rest[:, rows]
                n = e + 1 if rows.start == 0 else E + 1
                dve.wait_ge(pe_d, e + 1)
                if n > 1:
                    dve.wait_ge(m_yl, n - 1)
                dve.tensor_tensor(y, tiles(banks[6 + e % 2])[:, rows],
                                  slot_gate[:, :].rearrange("p (b e) -> p b e", b=B)[:, rows, e].unsqueeze(2)
                                  .broadcast_to([128, rows.stop - rows.start, 128]), ALU.mult).then_inc(m_y, 1)
                if e >= 2:
                    dve.wait_ge(pe_sc, B * (e - 1))
                dve.wait_ge(m_y, n)
                dve.tensor_copy(parts[:, 0], y).then_inc(m_yh, 1)
                dve.wait_ge(m_yh, n)
                dve.tensor_tensor(rest, y, parts[:, 0], ALU.subtract).then_inc(m_yr, 1)
                dve.wait_ge(m_yr, n)
                dve.tensor_copy(parts[:, 1], rest).then_inc(m_ym, 1)
                dve.wait_ge(m_ym, n)
                dve.tensor_tensor(parts[:, 2], rest, parts[:, 1], ALU.subtract).then_inc(m_yl, 1)

            def final_shift(b):
                wait_final_rstd(2 * B + b)
                dve.scalar_tensor_tensor(out=shift0[:, b, :], in0=mv0[:, b, :, 0], scalar=-1.0,
                                         in1=rs0[:, b, :], op0=ALU.mult, op1=ALU.mult).then_inc(f_nm, 1)

            for e in range(E - 1):
                weigh_results(e, slice(0, B))
            weigh_results(E - 1, slice(0, B // 2))
            weigh_results(E - 1, slice(B // 2, B))
            for b in range(B):
                dve.wait_ge(pe_sc, B * (E - 1) + b + 1)
                dve.tensor_tensor(res[:, b, :, :], tiles(banks[b]), x2[:, b, :, :], ALU.add).then_inc(m_sc, 1)
                if b:
                    final_shift(b - 1)
                dve.wait_ge(m_sc, b + 1)
                stats(res[:, b], bn0[:, b], mv0[:, b], f_bn, f_mv, 2 * B + b + 1)
            b = B - 1
            wait_final_rstd(2 * B + b)
            for t in range(NT):
                dve.tensor_scalar(res[:, b, t, :], res[:, b, t, :], mv0[:, b, t, 0:1], rs0[:, b, t:t + 1],
                                  ALU.subtract, ALU.mult).then_inc(f_z, 1)

        @block.gpsimd
        def _(pool):
            pool.memset(ln_eps[:, :], LN_EPS).then_inc(c_set, 1)
            pool.memset(ones[:, :], 1.0).then_inc(c_set, 1)
            pool.memset(minus_half[:, :], -0.5).then_inc(c_set, 1)
            pool.wait_ge(c_set, 3)
            pool.affine_select(out=ident[:, :], in_=ones[:, :], compare_op=ALU.is_equal, fill=0.0, base=0,
                               pattern=[[-1, 128]], channel_multiplier=1).then_inc(c_done, 1)
            pool.affine_select(out=of_head[:, :], in_=ones[:, 0:HEADS], compare_op=ALU.is_ge, fill=0.0, base=0,
                               pattern=[[-HD, HEADS]], channel_multiplier=1).then_inc(c_sel, 1)
            pool.memset(causal[:, :, :], 1.0).then_inc(c_sel, 1)
            pool.memset(scan_keep[:, :, :], 1.0).then_inc(c_sel, 1)
            pool.iota(slot_int[:, :], pattern=[[1, 128]], base=0, channel_multiplier=0).then_inc(c_sel, 1)
            pool.wait_ge(c_done, 1)
            pool.tensor_copy(ident_bf[:, :], ident[:, :]).then_inc(c_wide, 1)
            pool.wait_ge(c_sel, 4)
            pool.affine_select(out=of_head[:, :], in_=of_head[:, :], compare_op=ALU.is_ge, fill=0.0,
                               base=HD - 1, pattern=[[HD, HEADS]], channel_multiplier=-1)\
                .then_inc(c_sel, 1)
            pool.memset(scan_keep[:, :, 0:1], 0.0).then_inc(c_sel, 1)
            pool.tensor_copy(slot_row[:, :], slot_int[:, :]).then_inc(c_sel, 1)
            for j in range(Q4):
                q = slice(32 * j, 32 * j + 32)
                pool.wait_ge(c_sel, 7 + 3 * j)
                pool.affine_select(out=same_g[q, :], in_=ones[q, 0:4], compare_op=ALU.is_ge, fill=0.0, base=0,
                                   pattern=[[-HD, 4]], channel_multiplier=1).then_inc(c_sel, 1)
                pool.wait_ge(c_sel, 8 + 3 * j)
                pool.affine_select(out=same_g[q, :], in_=same_g[q, :], compare_op=ALU.is_ge, fill=0.0,
                                   base=HD - 1, pattern=[[HD, 4]], channel_multiplier=-1).then_inc(c_sel, 1)
                pool.wait_ge(c_sel, 9 + 3 * j)
                pool.affine_select(out=causal[q, :, :], in_=causal[q, :, :], compare_op=ALU.is_ge, fill=0.0,
                                   base=0, pattern=[[0, 4], [0, 4], [1, C]], channel_multiplier=-1)\
                    .then_inc(c_sel, 1)
            pool.wait_ge(c_sel, 19)
            pool.tensor_copy(same_g_wide[:, :, :].rearrange("p (g d) n -> p g (d n)", g=4),
                             same_g[:, :].unsqueeze(2).broadcast_to([128, 4, HD * NC])).then_inc(c_sel, 1)
            pool.memset(queries_j[:, :, :, :], 0.0).then_inc(c_wide, 1)
            pool.memset(values_g[:, :, :, :, :], 0.0).then_inc(c_wide, 1)
            pool.memset(v_blk[:, :, :, :], 0.0).then_inc(c_wide, 1)
            pool.wait_ge(p_zT, B)
            pool.wait_ge(c_sel, 20)
            pool.memset(state_blk[:, :, :], 0.0).then_inc(c_wide, 1)

            for b in range(B):
                pool.wait_ge(v_pool, b + 1)
                pool.wait_ge(v_val, b + 1)
                pool.tensor_tensor(ka0[:, b], cum0[:, b], vals0[:, b, :], ALU.mult).then_inc(g_prod, 1)
            pool.wait_ge(ld_r0, 32)
            for b in range(B):
                pool.wait_ge(d_z, 2 * (2 * B + b + 1))
                pool.wait_ge(d_za, 2 * (2 * B + b + 1))
                pool.tensor_tensor(res[:, b], x2[:, b], over_tiles(rows0[:, 0, :]), ALU.add).then_inc(s_res, 1)

            def residual1(l, b):
                m = unit(l, b)
                if m + 1 < UNITS:
                    pool.wait_ge(s_vg, 8 * (m + 2))
                if b == 0:
                    pool.wait_ge(ld_1, 48 * (l + 1))
                    pool.tensor_tensor(shift_1[:, :], rows_1[:, 1, :], rows_1[:, 2, :], ALU.add).then_inc(s_sh1, 1)
                pool.wait_ge(s_z1, NT * (m + 1))
                if m:
                    pool.wait_ge(s_y2, m)
                pool.tensor_tensor(res1[:, :, :], z1[:, :, :], over_tiles(rows_1[:, 0, :]), ALU.mult)\
                    .then_inc(s_r1m, 1)
                pool.wait_ge(s_r1m, m + 1)
                pool.wait_ge(s_sh1, l + 1)
                pool.tensor_tensor(res1[:, :, :], res1[:, :, :], over_tiles(shift_1[:, :]), ALU.add)\
                    .then_inc(s_r1, 1)

            def weigh_key_sums(l, b):
                u = unit(l, b)
                pool.wait_ge(s_ks, u + 1)
                pool.wait_ge(s_q, u + 1)
                pool.wait_ge(s_vg, 8 * (u + 1))
                pool.tensor_tensor(qk_sum[:, :], qT[:, :], k_sum[:, :], ALU.mult).then_inc(s_qk, 1)

            def spread_last_keys(l, b):
                u = unit(l, b)
                pool.wait_ge(s_k, u + 1)
                pool.tensor_scalar(keys_g[:, :, 3, :], kT[:, :].rearrange("p (n c) -> p n c", c=C),
                                   same_g[:, 3:4], 1.0, ALU.mult, ALU.mult).then_inc(s_kp, 1)

            def spread_first_values(l, b):
                u = unit(l, b)
                pool.wait_ge(s_v, u + 1)
                for k in range(8):
                    if k:
                        pool.wait_ge(s_vg, 8 * u + k)
                    spread_values(pool, k // 4, k % 4).then_inc(s_vg, 1)

            def residual2(l, b):
                m = unit(l, b)
                if b == 0:
                    pool.wait_ge(ld_2v, 32 * (l + 1))
                    pool.tensor_tensor(shift_2[:, :], rows_2[:, 1, :], rows_2[:, 2, :], ALU.add).then_inc(s_sh2, 1)
                pool.wait_ge(s_z2, NT * (m + 1))
                pool.tensor_tensor(res[:, b], z2[:, :, :], over_tiles(rows_2[:, 0, :]), ALU.mult)\
                    .then_inc(s_r2m, 1)
                pool.wait_ge(s_r2m, m + 1)
                pool.wait_ge(s_sh2, l + 1)
                pool.tensor_tensor(res[:, b], res[:, b], over_tiles(shift_2[:, :]), ALU.add).then_inc(s_res, 1)

            def final_rstd(n):
                b = final_order[n][0]
                pool.wait_ge(f_mv, NT * (n + 1))
                pool.tensor_tensor(lv0[:, b, :], mv0[:, b, :, 1], ln_eps[:, :], ALU.add).then_inc(f_ve, 1)
                pool.wait_ge(f_ve, n + 1)
                pool.tensor_tensor(rs0[:, b, :], lv0[:, b, :], minus_half[:, :], ALU.pow).then_inc(f_rs, 1)

            for u in range(UNITS + 2):
                if u < UNITS:
                    spread_last_keys(*of_unit(u))
                    spread_first_values(*of_unit(u))
                    weigh_key_sums(*of_unit(u))
                if u < B:
                    pool.wait_ge(s_xT, u + 1)
                    pool.tensor_tensor(x2[:, u], x2[:, u], over_tiles(rows0[:, 2, :]), ALU.add).then_inc(f_b, 1)
                if 1 <= u <= UNITS:
                    residual1(*of_unit(u - 1))
                if u == UNITS:
                    final_rstd(1)
                if u >= 2:
                    residual2(*of_unit(u - 2))
                if u == UNITS:
                    for n in range(2, by_pool):
                        final_rstd(n)
                if u == UNITS - 1:
                    final_rstd(0)
            for b in range(B + 1):
                pool.wait_ge(a_xh, b + 1)
                if b == B:
                    pool.tensor_tensor(gate_rest[:, :], gate_flat, gate_parts[:, 0, :], ALU.subtract).then_inc(g_xr, 1)
                else:
                    pool.tensor_tensor(x_rest[:, b], x2[:, b], x_parts[0][:, b], ALU.subtract).then_inc(g_xr, 1)
            pool.wait_ge(pe_lg, 1)
            for b in range(B + 1):
                pool.wait_ge(a_xm, b + 1)
                if b == B:
                    pool.tensor_tensor(gate_parts[:, 2, :], gate_rest[:, :], gate_parts[:, 1, :], ALU.subtract)\
                        .then_inc(g_xl, 1)
                else:
                    pool.tensor_tensor(x_parts[2][:, b], x_rest[:, b], x_parts[1][:, b], ALU.subtract)\
                        .then_inc(g_xl, 1)


def kernel(**inputs):
    import numpy as np
    import concourse.bacc as bacc
    from concourse import mybir as mb
    from concourse.bass_utils import run_bass_kernel_spmd

    x = {k: np.asarray(v) for k, v in inputs.items()}
    at = {k[8:]: v for k, v in x.items() if k.startswith("L1_attn_")}
    l0 = {k[8:]: v for k, v in x.items() if k.startswith("L0_attn_")}
    b1 = at["b1"].reshape(L, NF, 128).transpose(0, 2, 1)
    no_bias = np.zeros_like(at["bo"][:1])
    packed = {
        "x": l0["hidden_states"],
        "cols0": np.stack([l0["gamma"], l0["beta"], l0["bk"], l0["bv"], l0["bka"],
                           x["L0_ffn_scale"], x["L0_ffn_bias"]], axis=1),
        "w0": np.stack([l0["Wk"].T, l0["Wv"].T, l0["Wka"].T, x["L0_ffn_weights"].T]),
        "rows0": np.stack([at["bo"][0], at["gf"], at["bef"]]),
        "w_qkv": np.stack([at["Wq"], at["Wk"], at["Wv"]], axis=1),
        "cols_a": np.stack([at["bq"], at["bk"]], axis=2),
        "row_v": at["bv"],
        "w_o": at["Wo"],
        "w_1": at["W1"],
        "w_2": at["W2"],
        "cols_1": np.concatenate([at["g1"][:, :, None], at["be1"][:, :, None], b1], axis=2),
        "rows_1": np.stack([at["g1"], at["be1"], at["b2"]], axis=1),
        "cols_2": np.stack([at["g2"], at["be2"]], axis=2),
        "rows_2": np.stack([at["g2"], at["be2"], np.concatenate([at["bo"][1:], no_bias])], axis=1),
        "gate_w": x["L1_ffn_gate_w"],
        "we_1": x["L1_ffn_w1"],
        "we_2": x["L1_ffn_w2"],
    }
    nc = bacc.Bacc("TRN2", target_bir_lowering=False, num_devices=1)
    arrays, args = {}, {}
    for name, v in packed.items():
        v = np.ascontiguousarray(v)
        arrays[f"in_{name}"] = v
        args[name] = nc.dram_tensor(f"in_{name}", v.shape, mb.dt.from_np(v.dtype), kind="ExternalInput").ap()
    out = nc.dram_tensor("out", (B, S, D), mb.dt.float32, kind="ExternalOutput").ap()
    build(nc, args, out)
    r = run_bass_kernel_spmd(nc, [arrays], core_ids=[0])
    return r.results[0]["out"]
```
